# Optimizing a Trainium2 kernel written in Bass

```python
import numpy as np
import jax
import jax.numpy as jnp

def _softmax(x, axis=-1):
    return jax.nn.softmax(x, axis=axis)

def _gelu(x):
    return jax.nn.gelu(x, approximate=True)

def _silu(x):
    return jax.nn.silu(x)

def _sigmoid(x):
    return jax.nn.sigmoid(x)

def _layernorm(x, axis=-1, eps=1e-05):
    m = jnp.mean(x, axis=axis, keepdims=True)
    v = jnp.var(x, axis=axis, keepdims=True)
    return (x - m) / jnp.sqrt(v + eps)

def _scatter_add(tgt, idx, src, axis=0):
    return tgt.at[idx].add(src)

def _segment_sum(src, seg, n):
    return jax.ops.segment_sum(src, seg, n)
kernel_name = 'mk_decoder_postln_d2_seqx_r4_aec3b8'

def setup_inputs(seed: int=0):
    np.random.seed(seed)
    _w = jnp.asarray

    def _rec_inputs():
        import jax
        import jax.numpy as jnp
        _rk = jax.random.key(seed)
        x = 7.22e-05 + 1 * jax.random.normal(jax.random.fold_in(_rk, 1), (32, 128, 256), jnp.float32)
        _lenS = 128 - jax.random.randint(jax.random.fold_in(_rk, 7), (32,), 0, max(1, 128 // 4) + 1, jnp.int32)
        _lenS2 = 128 - jax.random.randint(jax.random.fold_in(_rk, 8), (32,), 0, max(1, 128 // 4) + 1, jnp.int32)
        _ctx_1024P = jax.random.normal(jax.random.fold_in(_rk, 11), (32, 16, 256), jnp.float32)
        _ctx_1024c = jax.random.dirichlet(jax.random.fold_in(_rk, 511), 0.3 * jnp.ones((16,), jnp.float32), (32, 128))
        _ctx_1024t = jnp.einsum('bsk,bkd->bsd', _ctx_1024c, _ctx_1024P)
        _ctx_1024t = _ctx_1024t * jax.lax.rsqrt(jnp.mean(jnp.square(_ctx_1024t)) + 1e-12) * 0.953939
        ctx_1024 = 4.13588e-05 + 0.999923 * (_ctx_1024t + 0.3 * jax.random.normal(jax.random.fold_in(_rk, 611), (32, 128, 256), jnp.float32))
        _validS = jnp.arange(128)[None, :] < _lenS[:, None]
        _validS2 = jnp.arange(128)[None, :] < _lenS2[:, None]
        _causal = jnp.tril(jnp.ones((128, 128), dtype=bool))
        mask_BxS2_bk0 = jnp.logical_not(jnp.broadcast_to(_validS2[:, :], (32, 128)))
        return (x, ctx_1024, mask_BxS2_bk0)
    x, ctx_1024, mask_BxS2_bk0 = _rec_inputs()

    def _L0_attn_setup():
        import jax, jax.numpy as jnp
        import numpy as np
        B, T, D, H = (8, 1024, 256, 8)
        BW = D // H
        MIN_DECAY = 0.001
        EPS = 1e-05
        SCAN_EPS = 1e-07

        def block_diag_linear(x, w, b):
            xb = x.reshape(x.shape[:-1] + (H, BW))
            y = jnp.einsum('bthi,hij->bthj', xb, w) + b
            return y.reshape(x.shape)

        def closed_form_rnn_scan(x, a):
            a_cumprod = jnp.cumprod(a, axis=1)
            ones = jnp.ones((x.shape[0], 1, x.shape[2]), dtype=x.dtype)
            p_prefix = jnp.concatenate([ones, a_cumprod[:, :-1, :]], axis=1)
            p_prefix = jnp.maximum(p_prefix, SCAN_EPS)
            w = (x + SCAN_EPS) / p_prefix
            S = jnp.cumsum(w, axis=1)
            h = p_prefix * S
            return (h, h[:, -1, :])
        key = jax.random.key(seed)
        k0, k1, k2 = jax.random.split(key, 3)
        x = jax.random.normal(k0, (B, T, D), dtype=jnp.float32)
        a_param = jnp.full((D,), -3.0, dtype=jnp.float32)
        w_in = jax.random.normal(k1, (H, BW, BW), dtype=jnp.float32) * (1.0 / np.sqrt(BW))
        b_in = jnp.ones((H, BW), dtype=jnp.float32)
        w_a = jax.random.normal(k2, (H, BW, BW), dtype=jnp.float32) * (1.0 / np.sqrt(BW))
        b_a = jnp.ones((H, BW), dtype=jnp.float32)
        return {'x': x, 'a_param': a_param, 'w_in': w_in, 'b_in': b_in, 'w_a': w_a, 'b_a': b_a}
    _L0_attn_all = _L0_attn_setup()
    _L0_attn_in = {k: v for k, v in _L0_attn_all.items() if k in ('a_param', 'w_in', 'b_in', 'w_a', 'b_a')}
    del _L0_attn_all

    def _L0_xattn_setup():
        import jax, jax.numpy as jnp
        import numpy as np
        EMBED_DIM = 256
        HEAD_DIM = 256
        GAMMA = 0.96875
        THETA = 10000.0
        SCALE_BASE = 512.0

        def _dup_interleave(x):
            return jnp.repeat(x, 2, axis=-1)

        def _rotate_half(x):
            x_even = x[..., ::2]
            x_odd = x[..., 1::2]
            return jnp.stack((-x_odd, x_even), axis=-1).reshape(x.shape)

        def _xpos(x, offset=0, inverse_scale=False):
            l = x.shape[-2]
            half = HEAD_DIM // 2
            scale_vec = (jnp.arange(0, HEAD_DIM, 2, dtype=jnp.float32) + 0.4 * HEAD_DIM) / (1.4 * HEAD_DIM)
            pos = jnp.arange(offset, offset + l, dtype=jnp.float32)
            scale = scale_vec[None, :] ** (pos / SCALE_BASE)[:, None]
            freqs = 1.0 / THETA ** (jnp.arange(half, dtype=jnp.float32) / half)
            sin_in = pos[:, None] * freqs[None, :]
            sin, cos = (jnp.sin(sin_in), jnp.cos(sin_in))
            if inverse_scale:
                scale = 1.0 / scale
            return x * _dup_interleave(cos * scale) + _rotate_half(x) * _dup_interleave(sin * scale)

        def _decay_mask(l, gamma):
            idx = jnp.arange(l, dtype=jnp.float32)
            diff = idx[:, None] - idx[None, :]
            return jnp.where(diff >= 0, gamma ** diff, 0.0)
        key = jax.random.key(seed)
        k1, k2, k3, k4, k5, k6 = jax.random.split(key, 6)
        B, L = (4, 512)
        s = 1.0 / np.sqrt(EMBED_DIM)
        return {'q': jax.random.normal(k1, (B, L, EMBED_DIM), dtype=jnp.float32), 'k': jax.random.normal(k2, (B, L, EMBED_DIM), dtype=jnp.float32), 'v': jax.random.normal(k3, (B, L, EMBED_DIM), dtype=jnp.float32), 'Wq': jax.random.normal(k4, (EMBED_DIM, HEAD_DIM), dtype=jnp.float32) * s, 'Wk': jax.random.normal(k5, (EMBED_DIM, HEAD_DIM), dtype=jnp.float32) * s, 'Wv': jax.random.normal(k6, (EMBED_DIM, HEAD_DIM), dtype=jnp.float32) * s}
    _L0_xattn_all = _L0_xattn_setup()
    _L0_xattn_in = {k: v for k, v in _L0_xattn_all.items() if k in ('Wq', 'Wk', 'Wv')}
    del _L0_xattn_all

    def _L0_ffn_setup():
        import jax, jax.numpy as jnp
        import numpy as np
        E = 8
        K = 2
        CAP_FACTOR = 1.0
        key = jax.random.key(seed)
        k0, k1, k2, k3 = jax.random.split(key, 4)
        B, S, M, H = (4, 512, 256, 1024)
        x = jax.random.normal(k0, (B, S, M), jnp.float32)
        wg = jax.random.normal(k1, (M, E), jnp.float32) * 0.02
        w1 = jax.random.normal(k2, (E, M, H), jnp.float32) * 0.02
        b1 = jnp.zeros((E, H), jnp.float32)
        w2 = jax.random.normal(k3, (E, H, M), jnp.float32) * 0.02
        b2 = jnp.zeros((E, M), jnp.float32)
        return {'x': x, 'wg': wg, 'w1': w1, 'b1': b1, 'w2': w2, 'b2': b2}
    _L0_ffn_all = _L0_ffn_setup()
    _L0_ffn_in = {k: v for k, v in _L0_ffn_all.items() if k in ('wg', 'w1', 'b1', 'w2', 'b2')}
    del _L0_ffn_all

    def _L1_attn_setup():
        import jax, jax.numpy as jnp
        import numpy as np
        D_HEAD = 128
        ROTARY_BASE = 10000.0
        NEG = 1e+30

        def frac_rope(x, base=ROTARY_BASE):
            rot, skip = jnp.split(x, 2, axis=-1)
            T, W = (rot.shape[-2], rot.shape[-1])
            pos = jnp.arange(T)[:, None]
            dims = jnp.arange(W // 2)
            ang = jnp.power(base, -dims / (W // 2))[None, :]
            rad = pos * ang
            cos = jnp.cos(rad).astype(x.dtype)
            sin = jnp.sin(rad).astype(x.dtype)
            even, odd = jnp.split(rot, 2, axis=-1)
            r_even = even * cos - odd * sin
            r_odd = even * sin + odd * cos
            return jnp.concatenate([r_even, r_odd, skip], axis=-1)
        key = jax.random.key(seed)
        B, T, M, D = (4, 512, 256, D_HEAD)
        H = M // D
        ks = jax.random.split(key, 5)
        scale = M ** (-0.5)
        x = jax.random.normal(ks[0], (B, T, M), dtype=jnp.float32)
        wq = jax.random.normal(ks[1], (M, H, D), dtype=jnp.float32) * scale
        wk = jax.random.normal(ks[2], (M, H, D), dtype=jnp.float32) * scale
        wv = jax.random.normal(ks[3], (M, H, D), dtype=jnp.float32) * scale
        wo = jax.random.normal(ks[4], (H, D, M), dtype=jnp.float32) * scale
        return {'x': x, 'wq': wq, 'wk': wk, 'wv': wv, 'wo': wo}
    _L1_attn_all = _L1_attn_setup()
    _L1_attn_in = {k: v for k, v in _L1_attn_all.items() if k in ('wq', 'wk', 'wv', 'wo')}
    del _L1_attn_all

    def _L1_xattn_setup():
        import jax, jax.numpy as jnp
        import numpy as np
        import math
        B, SQ, SKV = (2, 512, 512)
        DQ, DKV, H, NH = (256, 256, 256, 16)
        HD = H // NH
        key = jax.random.key(seed)
        ks = jax.random.split(key, 12)
        s = 0.02
        return {'query_input': jax.random.normal(ks[0], (B, SQ, DQ), jnp.float32), 'key_value_input': jax.random.normal(ks[1], (B, SKV, DKV), jnp.float32), 'key_padding_mask': jax.random.randint(ks[2], (B, SKV), 0, 2) > 0, 'Wq': jax.random.normal(ks[3], (DQ, H), jnp.float32) * s, 'bq': jnp.zeros((H,), jnp.float32), 'Wk': jax.random.normal(ks[4], (DKV, H), jnp.float32) * s, 'bk': jnp.zeros((H,), jnp.float32), 'Wv': jax.random.normal(ks[5], (DKV, H), jnp.float32) * s, 'bv': jnp.zeros((H,), jnp.float32), 'Wo': jax.random.normal(ks[6], (H, DQ), jnp.float32) * s, 'bo': jnp.zeros((DQ,), jnp.float32)}
    _L1_xattn_all = _L1_xattn_setup()
    _L1_xattn_in = {k: v for k, v in _L1_xattn_all.items() if k in ('Wq', 'bq', 'Wk', 'bk', 'Wv', 'bv', 'Wo', 'bo')}
    del _L1_xattn_all

    def _L1_ffn_setup():
        import jax, jax.numpy as jnp
        import numpy as np
        TOP_K = 4
        key = jax.random.key(seed)
        ks = jax.random.split(key, 5)
        B, T, D = (2, 256, 256)
        P, PD = (64, 32)
        return {'x': jax.random.normal(ks[0], (B, T, D), dtype=jnp.float32), 'hasher_w': jax.random.normal(ks[1], (PD, D), dtype=jnp.float32) * 0.03, 'keys': jax.random.normal(ks[2], (P, PD), dtype=jnp.float32) * 0.1, 'values_down': jax.random.normal(ks[3], (P, D, PD), dtype=jnp.float32) * 0.01, 'values_up': jax.random.normal(ks[4], (P, PD, D), dtype=jnp.float32) * 0.01, 'scale': jnp.full((1,), 0.1, dtype=jnp.float32)}
    _L1_ffn_all = _L1_ffn_setup()
    _L1_ffn_in = {k: v for k, v in _L1_ffn_all.items() if k in ('hasher_w', 'keys', 'values_down', 'values_up', 'scale')}
    del _L1_ffn_all
    return {'x': x, 'ctx_1024': ctx_1024, 'mask_BxS2_bk0': mask_BxS2_bk0, 'L0_attn_a_param': _L0_attn_in['a_param'], 'L0_attn_w_in': _L0_attn_in['w_in'], 'L0_attn_b_in': _L0_attn_in['b_in'], 'L0_attn_w_a': _L0_attn_in['w_a'], 'L0_attn_b_a': _L0_attn_in['b_a'], 'L0_xattn_Wq': _L0_xattn_in['Wq'], 'L0_xattn_Wk': _L0_xattn_in['Wk'], 'L0_xattn_Wv': _L0_xattn_in['Wv'], 'L0_ffn_wg': _L0_ffn_in['wg'], 'L0_ffn_w1': _L0_ffn_in['w1'], 'L0_ffn_b1': _L0_ffn_in['b1'], 'L0_ffn_w2': _L0_ffn_in['w2'], 'L0_ffn_b2': _L0_ffn_in['b2'], 'L1_attn_wq': _L1_attn_in['wq'], 'L1_attn_wk': _L1_attn_in['wk'], 'L1_attn_wv': _L1_attn_in['wv'], 'L1_attn_wo': _L1_attn_in['wo'], 'L1_xattn_Wq': _L1_xattn_in['Wq'], 'L1_xattn_bq': _L1_xattn_in['bq'], 'L1_xattn_Wk': _L1_xattn_in['Wk'], 'L1_xattn_bk': _L1_xattn_in['bk'], 'L1_xattn_Wv': _L1_xattn_in['Wv'], 'L1_xattn_bv': _L1_xattn_in['bv'], 'L1_xattn_Wo': _L1_xattn_in['Wo'], 'L1_xattn_bo': _L1_xattn_in['bo'], 'L1_ffn_hasher_w': _L1_ffn_in['hasher_w'], 'L1_ffn_keys': _L1_ffn_in['keys'], 'L1_ffn_values_down': _L1_ffn_in['values_down'], 'L1_ffn_values_up': _L1_ffn_in['values_up'], 'L1_ffn_scale': _L1_ffn_in['scale']}

def reference(x, ctx_1024, mask_BxS2_bk0, L0_attn_a_param, L0_attn_w_in, L0_attn_b_in, L0_attn_w_a, L0_attn_b_a, L0_xattn_Wq, L0_xattn_Wk, L0_xattn_Wv, L0_ffn_wg, L0_ffn_w1, L0_ffn_b1, L0_ffn_w2, L0_ffn_b2, L1_attn_wq, L1_attn_wk, L1_attn_wv, L1_attn_wo, L1_xattn_Wq, L1_xattn_bq, L1_xattn_Wk, L1_xattn_bk, L1_xattn_Wv, L1_xattn_bv, L1_xattn_Wo, L1_xattn_bo, L1_ffn_hasher_w, L1_ffn_keys, L1_ffn_values_down, L1_ffn_values_up, L1_ffn_scale):
    import jax
    import jax.numpy as jnp

    def _L0_attn_ref(x, a_param, w_in, b_in, w_a, b_a):
        import jax, jax.numpy as jnp
        import numpy as np
        B, T, D, H = (8, 1024, 256, 8)
        BW = D // H
        MIN_DECAY = 0.001
        EPS = 1e-05
        SCAN_EPS = 1e-07

        def block_diag_linear(x, w, b):
            xb = x.reshape(x.shape[:-1] + (H, BW))
            y = jnp.einsum('bthi,hij->bthj', xb, w) + b
            return y.reshape(x.shape)

        def closed_form_rnn_scan(x, a):
            a_cumprod = jnp.cumprod(a, axis=1)
            ones = jnp.ones((x.shape[0], 1, x.shape[2]), dtype=x.dtype)
            p_prefix = jnp.concatenate([ones, a_cumprod[:, :-1, :]], axis=1)
            p_prefix = jnp.maximum(p_prefix, SCAN_EPS)
            w = (x + SCAN_EPS) / p_prefix
            S = jnp.cumsum(w, axis=1)
            h = p_prefix * S
            return (h, h[:, -1, :])
        gate_x = jax.nn.sigmoid(block_diag_linear(x, w_in, b_in))
        gate_a = jax.nn.sigmoid(block_diag_linear(x, w_a, b_a))
        log_a = -gate_a * (jax.nn.softplus(a_param) + MIN_DECAY)
        a = jnp.minimum(jnp.exp(log_a), 1.0 - EPS)
        gated_x = x * gate_x
        multiplier = jnp.sqrt(jnp.maximum(1.0 - a * a, EPS))
        normed_x = gated_x * multiplier
        h, _ = closed_form_rnn_scan(normed_x, a)
        return h

    def _L0_xattn_ref(q, k, v, Wq, Wk, Wv):
        import jax, jax.numpy as jnp
        import numpy as np
        EMBED_DIM = 256
        HEAD_DIM = 256
        GAMMA = 0.96875
        THETA = 10000.0
        SCALE_BASE = 512.0

        def _dup_interleave(x):
            return jnp.repeat(x, 2, axis=-1)

        def _rotate_half(x):
            x_even = x[..., ::2]
            x_odd = x[..., 1::2]
            return jnp.stack((-x_odd, x_even), axis=-1).reshape(x.shape)

        def _xpos(x, offset=0, inverse_scale=False):
            l = x.shape[-2]
            half = HEAD_DIM // 2
            scale_vec = (jnp.arange(0, HEAD_DIM, 2, dtype=jnp.float32) + 0.4 * HEAD_DIM) / (1.4 * HEAD_DIM)
            pos = jnp.arange(offset, offset + l, dtype=jnp.float32)
            scale = scale_vec[None, :] ** (pos / SCALE_BASE)[:, None]
            freqs = 1.0 / THETA ** (jnp.arange(half, dtype=jnp.float32) / half)
            sin_in = pos[:, None] * freqs[None, :]
            sin, cos = (jnp.sin(sin_in), jnp.cos(sin_in))
            if inverse_scale:
                scale = 1.0 / scale
            return x * _dup_interleave(cos * scale) + _rotate_half(x) * _dup_interleave(sin * scale)

        def _decay_mask(l, gamma):
            idx = jnp.arange(l, dtype=jnp.float32)
            diff = idx[:, None] - idx[None, :]
            return jnp.where(diff >= 0, gamma ** diff, 0.0)
        qh = _xpos(q @ Wq, offset=0, inverse_scale=False)
        kh = _xpos(k @ Wk, offset=0, inverse_scale=True)
        vh = v @ Wv
        L = qh.shape[-2]
        mask = _decay_mask(L, GAMMA)
        scores = jnp.einsum('bld,bmd->blm', qh, kh) * mask[None, :, :]
        return scores @ vh

    def _L0_ffn_ref(x, wg, w1, b1, w2, b2):
        import jax, jax.numpy as jnp
        import numpy as np
        E = 8
        K = 2
        CAP_FACTOR = 1.0
        B, S, M = x.shape
        N = B * S
        capacity = int(CAP_FACTOR * K * N // E)
        xt = x.reshape(N, M)
        logits = xt @ wg
        scores = jax.nn.softmax(logits, axis=-1)
        topv, topi = jax.lax.top_k(scores, K)
        topv = topv / jnp.sum(topv, axis=-1, keepdims=True)
        masks = jax.nn.one_hot(topi.T, E, dtype=jnp.int32)
        flat = masks.reshape(K * N, E)
        locs = jnp.cumsum(flat, axis=0) - 1
        pos = jnp.sum(locs * flat, axis=-1).reshape(K, N).T
        valid = pos < capacity
        gate = topv * valid.astype(topv.dtype)
        pos_c = jnp.where(valid, pos, 0)
        xk = xt[:, None, :] * valid[..., None].astype(xt.dtype)
        disp = jnp.zeros((E, capacity, M), xt.dtype)
        disp = disp.at[topi, pos_c].add(xk)
        h = jax.nn.relu(jnp.einsum('ecm,emh->ech', disp, w1) + b1[:, None, :])
        y = jnp.einsum('ech,ehm->ecm', h, w2) + b2[:, None, :]
        out = jnp.sum(gate[..., None] * y[topi, pos_c], axis=1)
        return out.reshape(B, S, M)

    def _L1_attn_ref(x, wq, wk, wv, wo):
        import jax, jax.numpy as jnp
        import numpy as np
        D_HEAD = 128
        ROTARY_BASE = 10000.0
        NEG = 1e+30

        def frac_rope(x, base=ROTARY_BASE):
            rot, skip = jnp.split(x, 2, axis=-1)
            T, W = (rot.shape[-2], rot.shape[-1])
            pos = jnp.arange(T)[:, None]
            dims = jnp.arange(W // 2)
            ang = jnp.power(base, -dims / (W // 2))[None, :]
            rad = pos * ang
            cos = jnp.cos(rad).astype(x.dtype)
            sin = jnp.sin(rad).astype(x.dtype)
            even, odd = jnp.split(rot, 2, axis=-1)
            r_even = even * cos - odd * sin
            r_odd = even * sin + odd * cos
            return jnp.concatenate([r_even, r_odd, skip], axis=-1)
        T = x.shape[1]
        q = jnp.einsum('btm,mhd->bhtd', x, wq)
        k = jnp.einsum('btm,mhd->bhtd', x, wk)
        v = jnp.einsum('btm,mhd->bhtd', x, wv)
        q = frac_rope(q) * D_HEAD ** (-0.5)
        k = frac_rope(k) * D_HEAD ** (-0.5)
        s = jnp.einsum('bhid,bhjd->bhij', q, k)
        i = jnp.arange(T)[:, None]
        j = jnp.arange(T)[None, :]
        s = s - NEG * jnp.less(i, j).astype(s.dtype)
        p = jax.nn.softmax(s, axis=-1)
        o = jnp.einsum('bhij,bhjd->bhid', p, v)
        return jnp.einsum('bhid,hdm->bim', o, wo)

    def _L1_xattn_ref(query_input, key_value_input, key_padding_mask, Wq, bq, Wk, bk, Wv, bv, Wo, bo):
        import jax, jax.numpy as jnp
        import numpy as np
        import math
        B, SQ, SKV = (2, 512, 512)
        DQ, DKV, H, NH = (256, 256, 256, 16)
        HD = H // NH
        b, sq, _ = query_input.shape
        skv = key_value_input.shape[1]
        Q = query_input @ Wq + bq
        K = key_value_input @ Wk + bk
        V = key_value_input @ Wv + bv
        Q = Q.reshape(b, sq, NH, HD).transpose(0, 2, 1, 3)
        K = K.reshape(b, skv, NH, HD).transpose(0, 2, 1, 3)
        V = V.reshape(b, skv, NH, HD).transpose(0, 2, 1, 3)
        scores = jnp.einsum('bhqd,bhkd->bhqk', Q, K) / math.sqrt(HD)
        mask = key_padding_mask[:, None, None, :]
        scores = jnp.where(mask, -jnp.inf, scores)
        attn = jax.nn.softmax(scores, axis=-1)
        out = jnp.einsum('bhqk,bhkd->bhqd', attn, V)
        out = out.transpose(0, 2, 1, 3).reshape(b, sq, H)
        return out @ Wo + bo

    def _L1_ffn_ref(x, hasher_w, keys, values_down, values_up, scale):
        import jax, jax.numpy as jnp
        import numpy as np
        TOP_K = 4
        h = jnp.einsum('btd,pd->btp', x, hasher_w)
        sim = jnp.einsum('btp,np->btn', h, keys)
        vals, idx = jax.lax.top_k(sim, TOP_K)
        w = jax.nn.softmax(vals, axis=-1)
        out = jnp.zeros_like(x)
        for k in range(TOP_K):
            ik = idx[..., k]
            vd = values_down[ik]
            vu = values_up[ik]
            proj = jax.nn.silu(jnp.einsum('btd,btdp->btp', x, vd))
            o = jnp.einsum('btp,btpd->btd', proj, vu)
            out = out + o * w[..., k:k + 1]
        return x + out * scale
    x = _layernorm(x + _L0_attn_ref(x, L0_attn_a_param, L0_attn_w_in, L0_attn_b_in, L0_attn_w_a, L0_attn_b_a), axis=-1)
    x = _layernorm(x + _L0_xattn_ref(x, ctx_1024, ctx_1024, L0_xattn_Wq, L0_xattn_Wk, L0_xattn_Wv), axis=-1)
    x = _layernorm(x + _L0_ffn_ref(x, L0_ffn_wg, L0_ffn_w1, L0_ffn_b1, L0_ffn_w2, L0_ffn_b2), axis=-1)
    x = _layernorm(x + _L1_attn_ref(x, L1_attn_wq, L1_attn_wk, L1_attn_wv, L1_attn_wo), axis=-1)
    x = _layernorm(x + _L1_xattn_ref(x, ctx_1024, mask_BxS2_bk0, L1_xattn_Wq, L1_xattn_bq, L1_xattn_Wk, L1_xattn_bk, L1_xattn_Wv, L1_xattn_bv, L1_xattn_Wo, L1_xattn_bo), axis=-1)
    x = _layernorm(x + _L1_ffn_ref(x, L1_ffn_hasher_w, L1_ffn_keys, L1_ffn_values_down, L1_ffn_values_up, L1_ffn_scale), axis=-1)
    return x

_drawn_inputs = setup_inputs


def setup_inputs(seed=0):
    import zlib

    import numpy as np

    out = dict(_drawn_inputs(seed))
    spreads = {'L0_attn_a_param': (-3.0, 0.2),
     'L0_attn_b_in': (1.0, 0.2),
     'L0_attn_b_a': (1.0, 0.6),
     'L0_ffn_b1': (0.0, 0.1),
     'L0_ffn_b2': (0.0, 0.1),
     'L1_xattn_bq': (0.0, 0.8),
     'L1_xattn_bk': (0.0, 2.0),
     'L1_xattn_bv': (0.0, 0.1),
     'L1_xattn_bo': (0.0, 0.1)}
    factors = {'L1_xattn_Wq': 8.0,
     'L1_xattn_Wk': 8.0,
     'L1_ffn_hasher_w': 27.529,
     'L1_ffn_keys': 27.462,
     'L1_ffn_values_down': 29.522,
     'L1_ffn_values_up': 27.247}
    for name, (base, spread) in spreads.items():
        noise = np.random.default_rng([zlib.crc32(name.encode()), seed]).standard_normal(out[name].shape)
        drawn = base * np.exp(spread * noise) if base else spread * noise
        out[name] = jnp.asarray(drawn.astype(out[name].dtype))
    for name, factor in factors.items():
        out[name] = (out[name] * factor).astype(out[name].dtype)
    return out
```

```python
from contextlib import ExitStack

import numpy as np
import concourse.bass as bass
from concourse import mybir

F32 = mybir.dt.float32
BF16 = mybir.dt.bfloat16
I32 = mybir.dt.int32
U8 = mybir.dt.uint8
ALU = mybir.AluOpType
ACT = mybir.ActivationFunctionType
AX = mybir.AxisListType.X

P = 128
B, S, D = 32, 128, 256
NC_ = D // P
UB = 2
T = UB * S
UNITS = B // UB
LN_EPS = 1e-5
BIG = 1e30

E0, HID0, TOP0 = 8, 1024, 2
CAP = TOP0 * B * S // E0
SLOTS = E0 * CAP
BW = 32
MIN_DECAY, A_EPS, SCAN_EPS = 0.001, 1e-5, 1e-7
GAMMA, THETA, SCALE_BASE = 0.96875, 10000.0, 512.0
H1 = 2
NH, HD = 16, 16
NE1, PD, TOP1 = 64, 32, 4


def constants():
    f = np.float32
    pos = np.arange(S, dtype=f)
    half = D // 2
    scale_vec = (np.arange(0, D, 2, dtype=f) + f(0.4 * D)) / f(1.4 * D)
    scale = (scale_vec[None, :] ** (pos / f(SCALE_BASE))[:, None]).astype(f)
    freqs = (f(1.0) / f(THETA) ** (np.arange(half, dtype=f) / f(half))).astype(f)
    ang = pos[:, None] * freqs[None, :]
    sin, cos = np.sin(ang).astype(f), np.cos(ang).astype(f)
    inv = (f(1.0) / scale).astype(f)
    diff = pos[:, None] - pos[None, :]
    decay = np.where(diff >= 0, f(GAMMA) ** diff, 0).astype(f)
    rot = 32
    rang = pos[:, None] * np.power(f(10000.0), -np.arange(rot, dtype=f) / f(rot)).astype(f)[None, :]
    rsin, rcos = np.sin(rang).astype(f), np.cos(rang).astype(f)
    rope_c = np.zeros((P, S), f)
    rope_c[0:32], rope_c[32:64] = rcos.T, rcos.T
    rope_s = np.zeros((P, S), f)
    rope_s[0:32], rope_s[32:64] = rsin.T, -rsin.T
    first = (np.arange(NC_ * T) % S) == 0
    odd = ((np.arange(P) // HD) % 2).astype(f)
    seg = np.arange(E0 * TOP0 * B) % (TOP0 * B) != 0

    def row(a):
        return np.broadcast_to(np.asarray(a, f), (P, len(a)))

    tables = {
        "ident": np.eye(P, dtype=f),
        "xpos_q_cos": (cos * scale).T, "xpos_q_sin": (sin * scale).T,
        "xpos_k_cos": (cos * inv).T, "xpos_k_sin": (sin * inv).T,
        "decay_t": decay.T,
        "rope_cos": rope_c, "rope_sin": rope_s,
        "causal": np.where(diff >= 0, 0, -BIG).astype(f),
        "before": (diff.T > 0).astype(f),
        "ones": np.ones((P, P), f),
        "floor": row(np.where(first, 1.0, SCAN_EPS)),
        "keep": row(np.where(first, 0.0, 1.0)),
        "keep_seg": row(seg.astype(f)),
        "rank": row(E0 - np.arange(E0)),
        "base": row(np.arange(E0) * CAP),
        "even_heads": (1 - odd)[:, None], "odd_heads": odd[:, None],
    }
    at, parts, where = 0, [], {}
    for name, a in tables.items():
        where[name] = (at, a.shape[1])
        at += a.shape[1]
        parts.append(np.asarray(a, f))
    return np.ascontiguousarray(np.concatenate(parts, axis=1)), where


class Arena:

    def __init__(self, tile, size):
        self.tile, self.size, self.at = tile, size, 0

    def reset(self, at=0):
        self.at = at

    def take(self, shape):
        n = int(np.prod(shape[1:]))
        assert self.at + n <= self.size, (self.at + n, self.size)
        ap = self.tile[:, self.at:self.at + n]
        self.at += n
        if len(shape) > 2:
            names = "abcdef"[:len(shape) - 1]
            ap = ap.rearrange("p (" + " ".join(names) + ") -> p " + " ".join(names),
                              **dict(zip(names, shape[1:])))
        return ap


class Unit:

    def __init__(self, i, c, m=2):
        self.i, self.c, self.m = i, c, m
        self.fixed = isinstance(i, int)

    @property
    def n(self):
        return self.c if self.fixed else self.i * self.m + self.c

    def div(self, k):
        return self.c // k if self.fixed else self.i * (self.m // k) + self.c // k

    @property
    def p(self):
        return self.c % 2

    def back(self, k):
        return Unit(self.i, self.c - k, self.m)

    def at(self, k, count):
        u = self.back(k)
        return u if not u.fixed or 0 <= u.n < count else None


def pipelined(eng, count, lag, step, unroll=2):
    head = lag + 2
    head += (count - head) % unroll
    for t in range(head):
        step(Unit(0, t, unroll))
    with eng.Fori(0, (count - head) // unroll) as i:
        for j in range(unroll):
            step(Unit(i, head + j, unroll))
    for t in range(count, count + lag):
        step(Unit(0, t, unroll))


def done(eng, sem, u, per=1):
    if u.fixed and u.n < 0:
        return
    eng.wait_ge(sem, (u.n + 1) * per)


def landed(eng, sems, u, per=1):
    if u.fixed and u.n < 0:
        return
    eng.wait_ge(sems[u.p], (u.div(2) + 1) * (16 * per))


def decoder(nc, a, where, out):
    ctx = ExitStack()
    with ctx:
        def sb(name, shape, dt=F32):
            return ctx.enter_context(nc.sbuf_tensor(name, shape, dt))

        in_use = []

        def sem(name):
            in_use.append(nc.alloc_semaphore(name))
            return in_use[-1]

        def sem2(name):
            return [sem(name + "_0"), sem(name + "_1")]

        psum = ctx.enter_context(nc.psum_tensor("psum", [P, 8, 512], F32))

        def bank(k):
            return psum[:, k, :]

        def units(ap):
            return ap.rearrange("(u b) s d -> u s b d", b=UB)

        ZW = 512
        x2_d = nc.dram_tensor("x2_d", [B, S, D], F32, kind="Internal").ap()
        x4_d = nc.dram_tensor("x4_d", [B, S, D], F32, kind="Internal").ap()
        x5_d = nc.dram_tensor("x5_d", [B, S, D], F32, kind="Internal").ap()
        disp_d = nc.dram_tensor("disp_d", [SLOTS, D], F32, kind="Internal").ap()
        y_d = nc.dram_tensor("y_d", [SLOTS, D], F32, kind="Internal").ap()
        x_u, ctx_u, out_u = units(a["x"]), units(a["ctx_1024"]), units(out)
        x2_u, x4_u, x5_u = units(x2_d), units(x4_d), units(x5_d)

        n_const = a["constants"].shape[1]
        const = sb("const", [P, n_const])

        def table(name):
            at, n = where[name]
            return const[:, at:at + n]

        ident = table("ident")
        gate_w = sb("gate_w", [P, 2, NC_, P])
        w = {n: sb(n, [P, NC_, D]) for n in
             ("L0_xattn_Wq", "L0_xattn_Wk", "L0_xattn_Wv", "L1_attn_wq", "L1_attn_wk", "L1_attn_wv",
              "L1_attn_wo", "L1_xattn_Wq", "L1_xattn_Wk", "L1_xattn_Wv", "L1_xattn_Wo")}
        w_route = sb("w_route", [P, NC_, E0])
        w_hash = sb("w_hash", [P, NC_, PD])
        w_keys = sb("w_keys", [PD, NE1])
        VEC_ROWS = 10 + E0 * HID0 // P
        vec_rows = sb("vec_rows", [VEC_ROWS, P])
        vec = sb("vec", [P, VEC_ROWS])
        V_A, V_BIN, V_BA, V_BQ, V_BK, V_B1 = 0, 2, 4, 6, 8, 10
        hgate_b = sb("hgate_b", [P, 4])
        sp_tmp = sb("sp_tmp", [P, 3, NC_])
        ndecay = sb("ndecay", [P, NC_])
        kb_par = sb("kb_par", [P, 2, NC_])
        bv2_b = sb("bv2_b", [P, UB * D])
        bo_b = sb("bo_b", [P, D])
        b2_b = sb("b2_b", [P, E0, D])
        scale_b = sb("scale_b", [P, 1])
        ARENA_X, ARENA_Y = 23040, 14464
        arena_x, arena_y = Arena(sb("arena_x", [P, ARENA_X]), ARENA_X), Arena(sb("arena_y", [P, ARENA_Y]), ARENA_Y)
        mask_u8 = arena_y.take([P, B * S // 4])[0:1, :].bitcast(U8)
        mask_row = sb("mask_row", [1, B * S], BF16)
        ones_row = sb("ones_row", [1, P], BF16)
        ident_bf = sb("ident_bf", [P, P], BF16)
        causal_bf = sb("causal_bf", [P, P], BF16)
        zeros = sb("zeros", [P, ZW])
        wait_cell = sb("wait_cell", [1, 1])
        minus_half = sb("minus_half", [P, UB, 1])
        logits = sb("logits", [P, B, E0])
        gates = sb("gates", [P, TOP0, B])
        slot_g = sb("slot_g", [P, TOP0, B], I32)
        slot_s = sb("slot_s", [P, TOP0, B], I32)

        s_const, s_zero, s_prefill = sem("s_const"), sem("s_zero"), sem("s_prefill")
        s_vecT, s_vec, s_setup = sem("s_vecT"), sem("s_vec"), sem("s_setup")
        s_act_setup = sem("s_act_setup")

        s_pow = sem("s_pow")
        loads = [(const[:, :], a["constants"])]
        vec_src = [("L0_attn_a_param", 2), ("L0_attn_b_in", 2), ("L0_attn_b_a", 2),
                   ("L1_xattn_bq", 2), ("L1_xattn_bk", 2), ("L0_ffn_b1", E0 * HID0 // P)]
        at = 0
        for name, n in vec_src:
            v = a[name]
            if len(v.shape) == 2:
                v = v.rearrange("a b -> (a b)")
            loads.append((vec_rows[at:at + n, :], v.rearrange("(r p) -> r p", p=P)))
            at += n
        diag = []
        for g, name in enumerate(("L0_attn_w_in", "L0_attn_w_a")):
            for h in range(D // BW):
                c, r = divmod(h, P // BW)
                diag.append((gate_w[r * BW:(r + 1) * BW, g, c, r * BW:(r + 1) * BW], a[name][h]))
        for name in ("L0_xattn_Wq", "L0_xattn_Wk", "L0_xattn_Wv"):
            loads.append((w[name][:, :, :], a[name].rearrange("(c p) n -> p c n", p=P)))
        loads.append((w_route[:, :, :], a["L0_ffn_wg"].rearrange("(c p) n -> p c n", p=P)))
        N_EARLY = len(loads) + len(diag)
        late = []
        for name in ("L1_attn_wq", "L1_attn_wk", "L1_attn_wv"):
            late.append((w[name][:, :, :], a[name].rearrange("(c p) h n -> p c (h n)", p=P)))
        late.append((w["L1_attn_wo"][:, :, :], a["L1_attn_wo"].rearrange("h p n -> p h n")))
        for name in ("L1_xattn_Wq", "L1_xattn_Wk", "L1_xattn_Wv", "L1_xattn_Wo"):
            late.append((w[name][:, :, :], a[name].rearrange("(c p) n -> p c n", p=P)))
        late.append((w_hash[:, :, :], a["hash_t"].rearrange("(c p) n -> p c n", p=P)))
        late.append((w_keys[:, :], a["keys_t"]))
        for b in range(UB):
            late.append((bv2_b[:, b * D:(b + 1) * D],
                         a["L1_xattn_bv"].rearrange("(a n) -> a n", a=1).broadcast_to([P, D])))
        late.append((bo_b[:, :], a["L1_xattn_bo"].rearrange("(a n) -> a n", a=1).broadcast_to([P, D])))
        late.append((b2_b[:, :, :], a["L0_ffn_b2"].rearrange("(a e) n -> a e n", a=1).broadcast_to([P, E0, D])))
        late.append((scale_b[:, :], a["L1_ffn_scale"].rearrange("(a n) -> a n", a=1).broadcast_to([P, 1])))
        late.append((mask_u8[:, :], a["mask"].rearrange("(a b) s -> a (b s)", a=1)))
        s_late = sem("s_late")
        N_LATE = len(late)

        phases = {"sync": [], "tensor": [], "scalar": [], "vector": [], "gpsimd": []}

        def run_layer():
            with nc.Block() as block:
                @block.sync
                def _(eng):
                    for part in phases["sync"]:
                        part(eng)

                @block.tensor
                def _(eng):
                    for part in phases["tensor"]:
                        part(eng)

                @block.scalar
                def _(eng):
                    for part in phases["scalar"]:
                        part(eng)

                @block.vector
                def _(eng):
                    for part in phases["vector"]:
                        part(eng)

                @block.gpsimd
                def _(eng):
                    for part in phases["gpsimd"]:
                        part(eng)
            nc.clear_and_free_semaphores(list(in_use))
            nc.all_engine_barrier()
            in_use.clear()
            for parts in phases.values():
                parts.clear()

        def setup_sync(sp):
            for dst, src in loads:
                sp.dma_start(dst, src).then_inc(s_const, 16)
            sp.wait_ge(s_zero, 1)
            for dst, src in diag:
                sp.dma_start(dst, src).then_inc(s_const, 16)
            for dst, src in late:
                sp.dma_start(dst, src).then_inc(s_late, 16)

        def setup_pool(pool):
            nc.gpsimd.memset(gate_w[:, :, :, :], 0.0).then_inc(s_zero, 1)
            nc.gpsimd.memset(zeros[:, :], 0.0).then_inc(s_zero, 1)
            nc.gpsimd.memset(pool_cell[:, :], 0.0).then_inc(s_pow, 1)
            nc.gpsimd.memset(minus_half[:, :, :], -0.5).then_inc(s_pow, 1)
            pool.wait_ge(s_pow, 2)

        def setup_scalar(act):
            act.wait_ge(s_zero, 2)
            for k in range(SLOTS * D // (P * ZW)):
                n = P * ZW // D
                act.dma_start(disp_d[k * n:(k + 1) * n, :].rearrange("(p r) d -> p (r d)", p=P),
                              zeros[:, :]).then_inc(s_prefill, 16)
            act.wait_ge(s_vec, 1)
            nc.scalar.activation(sp_tmp[:, 0, :], vec[:, V_A:V_A + 2], ACT.Abs).then_inc(s_act_setup, 1)
            act.wait_ge(s_act_setup, 1)
            nc.scalar.activation(sp_tmp[:, 1, :], sp_tmp[:, 0, :], ACT.Exp, scale=-1.0).then_inc(s_act_setup, 1)
            act.wait_ge(s_act_setup, 2)
            nc.scalar.activation(sp_tmp[:, 2, :], sp_tmp[:, 1, :], ACT.Ln, bias=1.0).then_inc(s_act_setup, 1)

        def setup_tensor(pe):
            pe.wait_ge(s_const, 16 * N_EARLY)
            nc.tensor.transpose(bank(7)[:, 0:VEC_ROWS], vec_rows[:, :], ident[0:VEC_ROWS, 0:VEC_ROWS]).then_inc(s_vecT, 1)

        def setup_vector(dve):
            dve.wait_ge(s_vecT, 1)
            nc.vector.tensor_copy(vec[:, :], bank(7)[:, 0:VEC_ROWS]).then_inc(s_vec, 1)
            dve.wait_ge(s_vec, 1)
            nc.vector.tensor_scalar(hgate_b[:, :], vec[:, V_BIN:V_BIN + 4], 0.5, None, ALU.mult).then_inc(s_setup, 1)
            nc.vector.tensor_scalar(kb_par[:, 0, :], vec[:, V_BK:V_BK + 2], table("even_heads"), None,
                                    ALU.mult).then_inc(s_setup, 1)
            nc.vector.tensor_scalar(kb_par[:, 1, :], vec[:, V_BK:V_BK + 2], table("odd_heads"), None,
                                    ALU.mult).then_inc(s_setup, 1)
            nc.vector.tensor_scalar(ndecay[:, :], vec[:, V_A:V_A + 2], 0.0, MIN_DECAY, ALU.max,
                                    ALU.add).then_inc(s_setup, 1)
            nc.vector.tensor_copy(ident_bf[:, :], ident).then_inc(s_setup, 1)
            nc.vector.tensor_copy(causal_bf[:, :], table("causal")).then_inc(s_setup, 1)
            nc.vector.memset(ones_row[:, :], 1.0).then_inc(s_setup, 1)
            dve.wait_ge(s_act_setup, 3)
            dve.wait_ge(s_setup, 4)
            nc.vector.tensor_tensor(ndecay[:, :], ndecay[:, :], sp_tmp[:, 2, :], ALU.add).then_inc(s_setup, 1)
            dve.wait_ge(s_setup, 8)
            nc.vector.tensor_scalar(ndecay[:, :], ndecay[:, :], -0.5, None, ALU.mult).then_inc(s_setup, 1)
            dve.wait_ge(s_late, 16 * N_LATE)
            nc.vector.tensor_scalar(mask_row[:, :], mask_u8[:, :], -BIG, None, ALU.mult).then_inc(s_setup, 1)
        N_SETUP = 10

        phases["sync"].append(setup_sync)
        phases["gpsimd"].append(setup_pool)
        phases["scalar"].append(setup_scalar)
        phases["tensor"].append(setup_tensor)
        phases["vector"].append(setup_vector)

        def ln_stats(dve, u, src, stats, sems):
            s_st, s_ag, s_rs, s_out = sems
            for b in range(UB):
                ins = nc.vector.bn_stats(stats[:, b, 0:6], src[:, b, :])
            ins.then_inc(s_st, 1)
            dve.wait_ge(s_st, u.n * 2 + 1)
            nc.vector.memset(wait_cell[:, :], 0.0)
            for b in range(UB):
                ins = nc.vector.bn_aggr(stats[:, b, 6:8], stats[:, b, 0:6])
            ins.then_inc(s_st, 1)
            done(dve, s_st, u, 2)
            nc.vector.tensor_scalar(stats[:, :, 9:10], stats[:, :, 7:8], LN_EPS, None, ALU.add).then_inc(s_ag, 1)

        def ln_apply(dve, u, src, dst, stats, sems):
            s_st, s_ag, s_rs, s_out = sems
            done(dve, s_rs, u)
            for b in range(UB):
                ins = nc.vector.tensor_scalar(dst[:, b, :], src[:, b, :], stats[:, b, 6:7], stats[:, b, 8:9],
                                              ALU.subtract, ALU.mult)
            ins.then_inc(s_out, 1)

        def layer_norm(dve, u, src, dst, stats, sems):
            ln_stats(dve, u, src, stats, sems)
            ln_apply(dve, u, src, dst, stats, sems)

        def rstd(pool, u, stats, sems):
            s_st, s_ag, s_rs, s_out = sems
            done(pool, s_ag, u)
            nc.gpsimd.tensor_tensor(stats[:, :, 8:9], stats[:, :, 9:10], minus_half[:, :, :], ALU.pow).then_inc(s_rs, 1)

        def to_feature(dst, src):
            for c in range(NC_):
                for b in range(UB):
                    ins = nc.tensor.transpose(dst[:, c * T + b * S:c * T + (b + 1) * S],
                                              src[:, b, c * P:(c + 1) * P], ident)
            return ins

        def chunks(ap):
            return ap.rearrange("p (c t) -> p c t", c=NC_)

        def seqs(ap):
            return ap.rearrange("p (b d) -> p b d", b=UB)


        def add(engine, part):
            phases[engine].append(part)

        pool_cell = sb("pool_cell", [1, 8])

        def carry(pool, k):
            nc.gpsimd.tensor_tensor(pool_cell[:, k:k + 1], pool_cell[:, 7:8], pool_cell[:, 7:8], ALU.add)

        A = {}
        for n in ("x", "cx"):
            A[n] = arena_x.take([P, 2, UB, D])
        for n in ("xF", "cF", "thx", "tha", "a", "ash", "m", "g", "pp", "w", "r1", "x1F", "qr", "kr", "x2F"):
            A[n] = arena_x.take([P, 2, NC_, T])
        A["rp"] = arena_x.take([P, NC_, T])
        A["t1"] = arena_x.take([P, NC_, T])
        A["t2"] = arena_x.take([P, NC_, T])
        for n in ("x1", "x2", "v"):
            A[n] = arena_x.take([P, 2, UB, D])
        A["r2"] = arena_x.take([P, UB, D])
        A["sc"] = arena_x.take([P, 2, UB, S])
        A_st1 = sb("A_st1", [P, UB, 10])
        A_st2 = sb("A_st2", [P, UB, 10])

        a_in = sem2("a_in")
        aT_x, aT_c, aT_r1, aT_x1, aT_x2 = (sem("aT_" + n) for n in ("x", "c", "r1", "x1", "x2"))
        a_gate, a_k, a_v, a_q, a_score, a_ret, a_logit = (
            sem("a_" + n) for n in ("gate", "k", "v", "q", "score", "ret", "logit"))
        a_xF, a_cF, a_thx, a_tha, a_dec, a_vs, a_x1F, a_x2F, a_lg = (
            sem("a_" + n) for n in ("xF", "cF", "thx", "tha", "dec", "vs", "x1F", "x2F", "lg"))
        a_sh, a_min, a_m1, a_m2, a_g1, a_g2, a_p, a_rp, a_w, a_s, a_h, a_r1 = (
            sem("a_" + n) for n in ("sh", "min", "m1", "m2", "g1", "g2", "p", "rp", "w", "s", "h", "r1"))
        a_qt, a_qr, a_kt, a_kr, a_sc, a_r2 = (sem("a_" + n) for n in ("qt", "qr", "kt", "kr", "sc", "r2"))
        ln1 = [sem("ln1_" + n) for n in ("st", "ag", "rs", "out")]
        ln2 = [sem("ln2_" + n) for n in ("st", "ag", "rs", "out")]
        a_x1, a_x2 = ln1[3], ln2[3]
        a_st = sem2("a_st")
        A_LAG = 2

        def a_sync(sp):
            def step(t):
                u = t.at(0, UNITS)
                if u:
                    done(sp, aT_x, u.back(2))
                    done(sp, aT_c, u.back(2))
                    sp.dma_start(A["x"][:, u.p, :, :], x_u[u.n]).then_inc(a_in[u.p], 16)
                    sp.dma_start(A["cx"][:, u.p, :, :], ctx_u[u.n]).then_inc(a_in[u.p], 16)
                u = t.at(2, UNITS)
                if u:
                    done(sp, a_x2, u)
                    sp.dma_start(x2_u[u.n], A["x2"][:, u.p, :, :]).then_inc(a_st[u.p], 16)
            pipelined(sp, UNITS, A_LAG, step)

        def a_tensor(pe):
            pe.wait_ge(s_vec, 1)

            def project(dst, name, src, par=None, odd=None):
                for m in range(NC_):
                    for c in range(NC_):
                        ws = w[name][:, c, m::2] if par else w[name][:, c, m * P:(m + 1) * P]
                        ins = nc.tensor.matmul(dst[:, m * T:(m + 1) * T], ws, src[:, c, :],
                                               start=(c == 0), stop=(c == NC_ - 1))
                return ins

            def step(t):
                u = t.at(1, UNITS)
                if u:
                    done(pe, a_r1, u)
                    done(pe, a_qt, u.back(1))
                    for b in range(UB):
                        for c in range(NC_):
                            ins = nc.tensor.transpose(bank(4)[:, b * D + c * P:b * D + (c + 1) * P],
                                                      A["r1"][:, u.p, c, b * S:(b + 1) * S], ident)
                    ins.then_inc(aT_r1, 1)
                u = t.at(0, UNITS)
                if u:
                    landed(pe, a_in, u, 2)
                    done(pe, a_x1F, u.back(2))
                    to_feature(bank(0), A["x"][:, u.p]).then_inc(aT_x, 1)
                    done(pe, a_x2F, u.back(3))
                    to_feature(bank(1), A["cx"][:, u.p]).then_inc(aT_c, 1)
                    done(pe, a_xF, u)
                    done(pe, a_dec, u.back(1))
                    done(pe, a_thx, u.back(1))
                    done(pe, a_tha, u.back(1))
                    for g in range(2):
                        for c in range(NC_):
                            ins = nc.tensor.matmul(bank(2 + g)[:, c * T:(c + 1) * T], gate_w[:, g, c, :],
                                                   A["xF"][:, u.p, c, :], start=True, stop=True)
                    ins.then_inc(a_gate, 1)
                    done(pe, a_cF, u)
                    done(pe, a_kt, u.back(1))
                    project(bank(5), "L0_xattn_Wk", A["cF"][:, u.p], par=True).then_inc(a_k, 1)
                u = t.at(1, UNITS)
                if u:
                    done(pe, a_x1, u)
                    done(pe, a_xF, u.at(-1, UNITS) or u)
                    to_feature(bank(0), A["x1"][:, u.p]).then_inc(aT_x1, 1)
                    done(pe, a_x1F, u)
                    project(bank(4), "L0_xattn_Wq", A["x1F"][:, u.p], par=True).then_inc(a_q, 1)
                    done(pe, a_qr, u)
                    done(pe, a_kr, u)
                    done(pe, a_lg, u.back(2))
                    for b in range(UB):
                        for c in range(NC_):
                            ins = nc.tensor.matmul(bank(7)[:, b * S:(b + 1) * S],
                                                   A["kr"][:, u.p, c, b * S:(b + 1) * S],
                                                   A["qr"][:, u.p, c, b * S:(b + 1) * S],
                                                   start=(c == 0), stop=(c == NC_ - 1))
                    ins.then_inc(a_score, 1)
                u = t.at(2, UNITS)
                if u:
                    done(pe, a_x2, u)
                    done(pe, a_cF, u.at(-2, UNITS) or u)
                    to_feature(bank(1), A["x2"][:, u.p]).then_inc(aT_x2, 1)
                    done(pe, a_x2F, u)
                    done(pe, a_sc, u.at(-1, UNITS) or u)
                    for b in range(UB):
                        for c in range(NC_):
                            ins = nc.tensor.matmul(bank(7)[:, 256 + b * E0:256 + (b + 1) * E0],
                                                   A["x2F"][:, u.p, c, b * S:(b + 1) * S], w_route[:, c, :],
                                                   start=(c == 0), stop=(c == NC_ - 1))
                    ins.then_inc(a_logit, 1)
                u = t.at(0, UNITS)
                if u:
                    done(pe, a_r2, u.back(2))
                    for b in range(UB):
                        for c in range(NC_):
                            ins = nc.tensor.matmul(bank(6)[:, b * D:(b + 1) * D],
                                                   A["cF"][:, u.p, c, b * S:(b + 1) * S],
                                                   w["L0_xattn_Wv"][:, c, :], start=(c == 0), stop=(c == NC_ - 1))
                    ins.then_inc(a_v, 1)
                u = t.at(1, UNITS)
                if u:
                    done(pe, a_sc, u)
                    done(pe, a_vs, u.at(-1, UNITS) or u)
                    for b in range(UB):
                        ins = nc.tensor.matmul(bank(6)[:, b * D:(b + 1) * D], A["sc"][:, u.p, b, :],
                                               A["v"][:, u.p, b, :], start=True, stop=True)
                    ins.then_inc(a_ret, 1)
            pipelined(pe, UNITS, A_LAG, step)

        def a_scalar(act):
            act.wait_ge(s_setup, 9)

            def step(t):
                u = t.at(0, UNITS)
                if u:
                    done(act, aT_x, u)
                    done(act, a_r1, u.back(2))
                    nc.scalar.activation(A["xF"][:, u.p], chunks(bank(0)), ACT.Copy).then_inc(a_xF, 1)
                    done(act, aT_c, u)
                    done(act, a_v, u.back(2))
                    nc.scalar.activation(A["cF"][:, u.p], chunks(bank(1)), ACT.Copy).then_inc(a_cF, 1)
                    done(act, a_gate, u)
                    done(act, a_g1, u.back(2))
                    for c in range(NC_):
                        ins = nc.scalar.activation(A["tha"][:, u.p, c, :], bank(3)[:, c * T:(c + 1) * T], ACT.Tanh,
                                                   bias=hgate_b[:, 2 + c:3 + c], scale=0.5)
                    ins.then_inc(a_tha, 1)
                    for c in range(NC_):
                        ins = nc.scalar.activation(A["thx"][:, u.p, c, :], bank(2)[:, c * T:(c + 1) * T], ACT.Tanh,
                                                   bias=hgate_b[:, c:c + 1], scale=0.5)
                    ins.then_inc(a_thx, 1)
                    done(act, a_tha, u)
                    done(act, a_m1, u.back(2))
                    for c in range(NC_):
                        ins = nc.scalar.activation(A["a"][:, u.p, c, :], A["tha"][:, u.p, c, :], ACT.Exp,
                                                   bias=ndecay[:, c:c + 1], scale=ndecay[:, c:c + 1])
                    ins.then_inc(a_dec, 1)
                    done(act, a_m2, u)
                    nc.scalar.activation(A["m"][:, u.p], A["m"][:, u.p], ACT.Sqrt).then_inc(a_rt, 1)
                u = t.at(1, UNITS)
                if u:
                    done(act, aT_x1, u)
                    done(act, a_q, u.back(2))
                    nc.scalar.activation(A["x1F"][:, u.p], chunks(bank(0)), ACT.Copy).then_inc(a_x1F, 1)
                u = t.at(2, UNITS)
                if u:
                    done(act, aT_x2, u)
                    done(act, a_logit, u.back(2))
                    nc.scalar.activation(A["x2F"][:, u.p], chunks(bank(1)), ACT.Copy).then_inc(a_x2F, 1)
                    done(act, a_logit, u)
                    nc.scalar.activation(logits[:, bass.ds(u.n * UB, UB), :],
                                         bank(7)[:, 256:256 + UB * E0].rearrange("p (b e) -> p b e", e=E0),
                                         ACT.Copy).then_inc(a_lg, 1)
                u = t.at(0, UNITS)
                if u:
                    done(act, a_v, u)
                    done(act, a_ret, u.back(2))
                    nc.scalar.activation(A["v"][:, u.p], seqs(bank(6)), ACT.Copy).then_inc(a_vs, 1)
            pipelined(act, UNITS, A_LAG, step)

        def a_vector(dve):
            def bc(name, n):
                return table(name)[:, None, :].broadcast_to([P, n, S])

            def xpos(u, src, cos, sin, dst, s_t, s_r):
                t1, t2 = A["t1"], A["t2"]
                q = src.rearrange("p (c b s) -> p c b s", c=NC_, b=UB)
                nc.vector.tensor_tensor(t1[:, :, :].rearrange("p c (b s) -> p (c b) s", b=UB),
                                        src.rearrange("p (n s) -> p n s", s=S), bc(cos, NC_ * UB), ALU.mult)
                for c in range(NC_):
                    ins = nc.vector.tensor_tensor(t2[:, 1 - c, :].rearrange("p (b s) -> p b s", b=UB), q[:, c],
                                                  bc(sin, UB), ALU.mult)
                ins.then_inc(s_t, 1)
                done(dve, s_t, u)
                nc.vector.tensor_tensor(dst[:, 0, :], t1[:, 0, :], t2[:, 0, :], ALU.subtract)
                nc.vector.tensor_tensor(dst[:, 1, :], t1[:, 1, :], t2[:, 1, :], ALU.add).then_inc(s_r, 1)

            def step(t):
                u = t.at(1, UNITS)
                if u:
                    done(dve, aT_r1, u)
                    done(dve, aT_x1, u.back(2))
                    layer_norm(dve, u, seqs(bank(4)), A["x1"][:, u.p], A_st1, ln1)
                u = t.at(0, UNITS)
                if u:
                    p = u.p
                    a4 = A["a"][:, p].rearrange("p c (b s) -> p (c b) s", b=UB)
                    sh4 = A["ash"][:, p].rearrange("p c (b s) -> p (c b) s", b=UB)
                    flat = {n: A[n][:, p].rearrange("p c t -> p (c t)") for n in ("ash", "pp", "w")}
                    done(dve, a_dec, u)
                    done(dve, a_thx, u)
                    nc.vector.tensor_scalar(sh4[:, :, 1:S], a4[:, :, 0:S - 1], 1.0 - A_EPS, None,
                                            ALU.min).then_inc(a_sh, 1)
                    done(dve, a_sh, u)
                    nc.vector.tensor_scalar(A["a"][:, p], A["a"][:, p], 1.0 - A_EPS, None, ALU.min).then_inc(a_min, 1)
                    nc.vector.scalar_tensor_tensor(A["g"][:, p], A["thx"][:, p], 1.0, A["xF"][:, p], ALU.add,
                                                   ALU.mult).then_inc(a_g1, 1)
                    done(dve, a_sh, u)
                    nc.vector.tensor_tensor_scan(flat["pp"], flat["ash"], table("floor"), 1.0, ALU.mult,
                                                 ALU.max).then_inc(a_p, 1)
                    done(dve, a_min, u)
                    nc.vector.scalar_tensor_tensor(A["m"][:, p], A["a"][:, p], -0.25, A["a"][:, p], ALU.mult,
                                                   ALU.mult).then_inc(a_m1, 1)
                    done(dve, a_p, u)
                    nc.vector.reciprocal(A["rp"][:, :, :], A["pp"][:, p]).then_inc(a_rp, 1)
                    done(dve, a_m1, u)
                    nc.vector.tensor_scalar(A["m"][:, p], A["m"][:, p], 0.25, 0.25 * A_EPS, ALU.add,
                                            ALU.max).then_inc(a_m2, 1)
                    done(dve, a_k, u)
                    done(dve, a_score, u.back(2))
                    xpos(u, bank(5), "xpos_k_cos", "xpos_k_sin", A["kr"][:, p], a_kt, a_kr)
                    done(dve, a_rt, u)
                    done(dve, a_g1, u)
                    nc.vector.tensor_tensor(A["g"][:, p], A["m"][:, p], A["g"][:, p], ALU.mult).then_inc(a_g2, 1)
                    done(dve, a_g2, u)
                    done(dve, a_rp, u)
                    nc.vector.scalar_tensor_tensor(A["w"][:, p], A["g"][:, p], SCAN_EPS, A["rp"][:, :, :], ALU.add,
                                                   ALU.mult).then_inc(a_w, 1)
                    done(dve, a_w, u)
                    nc.vector.tensor_tensor_scan(flat["w"], table("keep"), flat["w"], 0.0, ALU.mult,
                                                 ALU.add).then_inc(a_s, 1)
                    done(dve, a_s, u)
                    nc.vector.tensor_tensor(A["m"][:, p], A["pp"][:, p], A["w"][:, p], ALU.mult).then_inc(a_h, 1)
                    done(dve, a_h, u)
                    nc.vector.tensor_tensor(A["r1"][:, p], A["m"][:, p], A["xF"][:, p], ALU.add).then_inc(a_r1, 1)
                u = t.at(1, UNITS)
                if u:
                    done(dve, a_q, u)
                    xpos(u, bank(4), "xpos_q_cos", "xpos_q_sin", A["qr"][:, u.p], a_qt, a_qr)
                u = t.at(2, UNITS)
                if u:
                    done(dve, a_ret, u)
                    nc.vector.tensor_tensor(A["r2"][:, :, :], seqs(bank(6)), A["x1"][:, u.p], ALU.add).then_inc(a_r2, 1)
                    done(dve, a_r2, u)
                    done(dve, aT_x2, u.back(2))
                    landed(dve, a_st, u.back(2))
                    layer_norm(dve, u, A["r2"], A["x2"][:, u.p], A_st2, ln2)
                u = t.at(1, UNITS)
                if u:
                    done(dve, a_score, u)
                    nc.vector.tensor_tensor(A["sc"][:, u.p], bank(7)[:, 0:UB * S].rearrange("p (b s) -> p b s", b=UB),
                                            bc("decay_t", UB), ALU.mult).then_inc(a_sc, 1)
            nc.vector.memset(A["ash"][:, :, :, :], 0.0).then_inc(a_sh0, 1)
            dve.wait_ge(a_sh0, 1)
            pipelined(dve, UNITS, A_LAG, step)
        a_sh0, a_rt = sem("a_sh0"), sem("a_rt")

        def a_gpsimd(pool):
            def step(t):
                u = t.at(1, UNITS)
                if u:
                    rstd(pool, u, A_st1, ln1)
                u = t.at(2, UNITS)
                if u:
                    rstd(pool, u, A_st2, ln2)
            pipelined(pool, UNITS, A_LAG, step)

        phases["gpsimd"].append(a_gpsimd)

        phases["sync"].append(a_sync)
        phases["tensor"].append(a_tensor)
        phases["scalar"].append(a_scalar)
        phases["vector"].append(a_vector)
        KB = TOP0 * B
        R = {}
        arena_x.reset()
        for n in ("eq", "rk", "l2"):
            R[n] = arena_x.take([P, B, E0])
        R["oh"] = arena_x.take([P, TOP0, B, E0])
        R["tot"] = arena_x.take([P, E0, KB])
        R["inc"] = arena_x.take([P, E0, KB])
        R["pos"] = arena_x.take([P, KB, E0])
        R["sel"] = arena_x.take([P, KB, E0])
        for n in ("m1", "m2", "mr", "ex"):
            R[n] = arena_x.take([P, B])
        for n in ("posk", "basek", "valid", "slot", "slot2"):
            R[n] = arena_x.take([P, TOP0, B])
        R["x"] = arena_x.take([P, 2, UB, D])
        R["idx"] = arena_x.take([P, 2, TOP0, UB]).bitcast(I32)

        r_v = sem("r_v")
        r_ex, r_rank, r_slots = sem("r_ex"), sem("r_rank"), sem("r_slots")
        r_in, r_idx, r_sc = sem2("r_in"), sem("r_idx"), sem2("r_sc")
        r_go = sem("r_go")
        RV_GAP, RV_ONEHOT = 8, 9
        per_parity = UNITS // 2

        def r_vector(dve):
            k = [0]

            def then(ins):
                k[0] += 1
                ins.then_inc(r_v, 1)
                dve.wait_ge(r_v, k[0])

            def over_e(ap, n=B):
                return ap[:, :, None].broadcast_to([P, n, E0])

            def first_max(src, m, oh):
                then(nc.vector.tensor_reduce(m, src, AX, ALU.max))
                then(nc.vector.tensor_tensor(R["eq"], src, over_e(m), ALU.is_equal))
                then(nc.vector.tensor_tensor(R["rk"], R["eq"], table("rank")[:, None, :].broadcast_to([P, B, E0]),
                                             ALU.mult))
                then(nc.vector.tensor_reduce(R["mr"], R["rk"], AX, ALU.max))
                then(nc.vector.tensor_tensor(oh, R["rk"], over_e(R["mr"]), ALU.is_equal))

            dve.wait_ge(a_lg, UNITS)
            dve.wait_ge(aT_x2, UNITS)
            first_max(logits[:, :, :], R["m1"], R["oh"][:, 0])
            then(nc.vector.scalar_tensor_tensor(R["l2"], R["oh"][:, 0], -BIG, logits[:, :, :], ALU.mult, ALU.add))
            first_max(R["l2"], R["m2"], R["oh"][:, 1])
            then(nc.vector.tensor_tensor(R["m2"], R["m2"], R["m1"], ALU.subtract))
            k_gap = k[0]
            dve.wait_ge(r_ex, 1)
            then(nc.vector.tensor_scalar(R["m1"], R["ex"], 1.0, None, ALU.add))
            then(nc.vector.reciprocal(gates[:, 0, :], R["m1"]))
            then(nc.vector.tensor_tensor(gates[:, 1, :], gates[:, 0, :], R["ex"], ALU.mult))
            dve.wait_ge(r_rank, 1)
            then(nc.vector.tensor_copy(R["tot"], bank(1).rearrange("p (k e) -> p e k", e=E0)))
            tot, inc = (R[n].rearrange("p e k -> p (e k)") for n in ("tot", "inc"))
            then(nc.vector.tensor_tensor_scan(inc, table("keep_seg"), tot, 0.0, ALU.mult, ALU.add))
            then(nc.vector.tensor_tensor(tot, inc, tot, ALU.subtract))
            then(nc.vector.tensor_tensor(R["pos"], bank(0).rearrange("p (k e) -> p k e", e=E0),
                                         R["tot"].rearrange("p e k -> p k e"), ALU.add))
            oh = R["oh"].rearrange("p c b e -> p (c b) e")
            flat = {n: R[n].rearrange("p c b -> p (c b)") for n in ("posk", "basek", "valid", "slot", "slot2")}
            then(nc.vector.tensor_tensor(R["sel"], R["pos"], oh, ALU.mult))
            then(nc.vector.tensor_reduce(flat["posk"], R["sel"], AX, ALU.add))
            then(nc.vector.tensor_tensor(R["sel"], oh, table("base")[:, None, :].broadcast_to([P, KB, E0]), ALU.mult))
            then(nc.vector.tensor_reduce(flat["basek"], R["sel"], AX, ALU.add))
            then(nc.vector.tensor_scalar(flat["valid"], flat["posk"], float(CAP), None, ALU.is_lt))
            then(nc.vector.tensor_tensor(gates[:, :, :], gates[:, :, :], R["valid"], ALU.mult))
            then(nc.vector.tensor_tensor(flat["slot"], flat["posk"], flat["valid"], ALU.mult))
            then(nc.vector.tensor_tensor(flat["slot"], flat["slot"], flat["basek"], ALU.add))
            then(nc.vector.tensor_copy(slot_g[:, :, :], R["slot"]))
            then(nc.vector.tensor_scalar(flat["slot2"], flat["valid"], -4.0 * SLOTS, 4.0 * SLOTS, ALU.mult, ALU.add))
            then(nc.vector.tensor_tensor(flat["slot2"], flat["slot2"], flat["slot"], ALU.add))
            nc.vector.tensor_copy(slot_s[:, :, :], R["slot2"]).then_inc(r_slots, 1)
            return k_gap

        def r_scalar(act):
            act.wait_ge(r_v, 12)
            nc.scalar.activation(R["ex"], R["m2"], ACT.Exp).then_inc(r_ex, 1)

        def r_tensor(pe):
            pe.wait_ge(r_v, 11)
            pe.wait_ge(a_x1F, UNITS)
            pe.wait_ge(a_x2F, UNITS)
            oh = R["oh"].rearrange("p c b e -> p (c b e)")
            nc.tensor.matmul(bank(0), table("before"), oh, start=True, stop=True)
            nc.tensor.matmul(bank(1), table("ones"), oh, start=True, stop=True).then_inc(r_rank, 1)

        def r_sync(sp):
            sp.wait_ge(a_st[0], 16 * per_parity)
            sp.wait_ge(a_st[1], 16 * per_parity)
            sp.wait_ge(a_r1, UNITS)
            sp.wait_ge(a_score, UNITS)

            def step(t):
                if not (t.fixed and t.n < 2):
                    landed(sp, r_sc, t.back(2), 4)
                sp.dma_start(R["x"][:, t.p], x2_u[t.n]).then_inc(r_in[t.p], 16)
            pipelined(sp, UNITS, 0, step)

        def r_gpsimd(pool):
            pool.wait_ge(s_prefill, 16 * (SLOTS * D // (P * ZW)))
            pool.wait_ge(r_slots, 1)

            def step(t):
                landed(pool, r_in, t)
                landed(pool, r_sc, t.back(2), 4)
                carry(pool, 0)
                nc.gpsimd.tensor_copy(R["idx"][:, t.p], slot_s[:, :, bass.ds(t.n * UB, UB)]).then_inc(r_idx, 1)
                done(pool, r_idx, t)
                carry(pool, 1)
                for c in range(TOP0):
                    for b in range(UB):
                        nc.gpsimd.indirect_dma_start(
                            out=disp_d, out_offset=bass.IndirectOffsetOnAxis(ap=R["idx"][:, t.p, c, b:b + 1], axis=0),
                            in_=R["x"][:, t.p, b, :], in_offset=None, bounds_check=SLOTS - 1,
                            oob_is_err=False).then_inc(r_sc[t.p], 16)
            pipelined(pool, UNITS, 0, step)

        add("vector", r_vector)
        add("scalar", r_scalar)
        add("tensor", r_tensor)
        add("sync", r_sync)
        add("gpsimd", r_gpsimd)

        MT = 512
        MS = MT // P
        TILES = SLOTS // MT
        HC = HID0 // P
        M = {}
        arena_y.reset()
        M["w1"] = arena_y.take([P, 2, NC_, HID0])
        M["w2"] = arena_y.take([P, 2, HC, D])
        M["x"] = arena_x.take([P, 2, MS, D])
        M["xF"] = arena_x.take([P, 2, NC_, MT])
        M["h"] = arena_x.take([P, HC, MT])
        M["y"] = arena_x.take([P, 2, MS, D])
        b1_e = sb("b1_e", [P, 2, HC])
        m_w, m_b1 = sem2("m_w"), sem("m_b1")
        m_in, m_T, m_xF = sem2("m_in"), sem("m_T"), sem("m_xF")
        m_hp, m_hs, m_hv, m_yp, m_y = sem("m_hp"), sem("m_hs"), sem("m_hv"), sem("m_yp"), sem("m_y")
        m_st = sem2("m_st")
        disp_t = disp_d.rearrange("(n q p) d -> n p q d", p=P, q=MS)
        y_t = y_d.rearrange("(n q p) d -> n p q d", p=P, q=MS)

        def m_sync(sp):
            for k in range(2):
                sp.wait_ge(r_sc[k], 16 * 4 * per_parity)

            def step(t):
                if t.c % 2 == 0:
                    e = t.div(2)
                    done(sp, m_yp, t.back(3))
                    sp.dma_start(M["w1"][:, (t.c // 2) % 2], w1_e[e]).then_inc(m_w[(t.c // 2) % 2], 16)
                    sp.dma_start(M["w2"][:, (t.c // 2) % 2], w2_e[e]).then_inc(m_w[(t.c // 2) % 2], 16)
                u = t.at(0, TILES)
                if u:
                    done(sp, m_T, u.back(2))
                    sp.dma_start(M["x"][:, u.p], disp_t[u.n]).then_inc(m_in[u.p], 16)
                u = t.at(2, TILES)
                if u:
                    done(sp, m_y, u, 2)
                    sp.dma_start(y_t[u.n], M["y"][:, u.p]).then_inc(m_st[u.p], 16)

            def guarded(t):
                if t.fixed and t.n >= TILES:
                    u = t.at(2, TILES)
                    done(sp, m_y, u, 2)
                    sp.dma_start(y_t[u.n], M["y"][:, u.p]).then_inc(m_st[u.p], 16)
                else:
                    step(t)
            pipelined(sp, TILES, 2, guarded, unroll=4)

        w1_e = a["L0_ffn_w1"].rearrange("e (c p) h -> e p c h", p=P)
        w2_e = a["L0_ffn_w2"].rearrange("e (c p) d -> e p c d", p=P)

        def m_tensor(pe):
            pe.wait_ge(r_slots, 1)
            for s in (a_dec, a_thx, a_qr, a_kr, a_r2, a_sc, a_lg):
                pe.wait_ge(s, UNITS)

            def step(t):
                u = t.at(1, TILES)
                if u:
                    wb = (u.c // 2) % 2
                    pe.wait_ge(m_w[wb], (u.div(4) + 1) * 32)
                    done(pe, m_xF, u, 2)
                    for m in range(HC):
                        if m >= 4:
                            pe.wait_ge((m_hs, m_hv)[m % 2], u.n * 4 + (m - 4) // 2 + 1)
                        else:
                            done(pe, (m_hs, m_hv)[m % 2], u.back(1), 4)
                        for c in range(NC_):
                            ins = nc.tensor.matmul(bank(2 + m % 4), M["w1"][:, wb, c, m * P:(m + 1) * P],
                                                   M["xF"][:, u.p, c, :], start=(c == 0), stop=(c == NC_ - 1))
                        ins.then_inc(m_hp, 1)
                u = t.at(0, TILES)
                if u:
                    landed(pe, m_in, u)
                    done(pe, m_xF, u.back(1), 2)
                    for c in range(NC_):
                        for q in range(MS):
                            ins = nc.tensor.transpose(bank(c)[:, q * P:(q + 1) * P],
                                                      M["x"][:, u.p, q, c * P:(c + 1) * P], ident)
                    ins.then_inc(m_T, 1)
                u = t.at(1, TILES)
                if u:
                    wb = (u.c // 2) % 2
                    done(pe, m_hs, u, 4)
                    done(pe, m_hv, u, 4)
                    done(pe, m_y, u.back(1), 2)
                    for q in range(MS):
                        for m in range(HC):
                            ins = nc.tensor.matmul(bank(6 + q // 2)[:, (q % 2) * D:(q % 2 + 1) * D],
                                                   M["h"][:, m, q * P:(q + 1) * P], M["w2"][:, wb, m, :],
                                                   start=(m == 0), stop=(m == HC - 1))
                    ins.then_inc(m_yp, 1)
            pipelined(pe, TILES, 1, step, unroll=4)

        def m_scalar(act):
            def step(t):
                u = t.at(1, TILES)
                if u:
                    if u.c % 2 == 0:
                        act.wait_ge(m_b1, u.div(2) + 1)
                    done(act, m_yp, u.back(1))
                    for m in range(0, HC, 2):
                        act.wait_ge(m_hp, u.n * HC + (m + 1))
                        nc.scalar.activation(M["h"][:, m, :], bank(2 + m % 4), ACT.Relu,
                                             bias=b1_e[:, (u.c // 2) % 2, m:m + 1]).then_inc(m_hs, 1)
                u = t.at(0, TILES)
                if u:
                    done(act, m_T, u)
                    done(act, m_hp, u.back(2), HC)
                    for c in range(NC_):
                        nc.scalar.activation(M["xF"][:, u.p, c, :], bank(c), ACT.Copy).then_inc(m_xF, 1)
            pipelined(act, TILES, 1, step, unroll=4)

        def m_vector(dve):
            def step(t):
                u = t.at(1, TILES)
                if u:
                    if u.c % 2 == 0:
                        done(dve, m_hs, u.back(3), 4)
                        nc.vector.tensor_scalar(b1_e[:, (u.c // 2) % 2, :],
                                                vec[:, bass.ds(u.div(2) * HC + V_B1, HC)], 0.0, None,
                                                ALU.add).then_inc(m_b1, 1)
                        dve.wait_ge(m_b1, u.div(2) + 1)
                    done(dve, m_yp, u.back(1))
                    for m in range(1, HC, 2):
                        dve.wait_ge(m_hp, u.n * HC + (m + 1))
                        nc.vector.tensor_scalar(M["h"][:, m, :], bank(2 + m % 4),
                                                b1_e[:, (u.c // 2) % 2, m:m + 1], 0.0, ALU.add,
                                                ALU.max).then_inc(m_hv, 1)
                    done(dve, m_yp, u)
                    landed(dve, m_st, u.back(2))
                    for k in range(2):
                        nc.vector.tensor_tensor(M["y"][:, u.p, 2 * k:2 * k + 2, :], seqs(bank(6 + k)),
                                                b2_b[:, bass.ds(u.div(2), 1), :].broadcast_to([P, 2, D]),
                                                ALU.add).then_inc(m_y, 1)
            pipelined(dve, TILES, 1, step, unroll=4)

        add("sync", m_sync)
        add("tensor", m_tensor)
        add("scalar", m_scalar)
        add("vector", m_vector)
        def m_end(sp):
            for k in range(2):
                sp.wait_ge(m_st[k], 16 * (TILES // 2))

        add("sync", m_end)
        run_layer()

        arena_y.reset()
        C = {}
        for n in ("x2", "v", "x4"):
            C[n] = arena_y.take([P, 2, UB, D])
        C["x3"] = arena_y.take([P, 4, UB, D])
        C["y"] = arena_y.take([P, 2, TOP0, UB, D])
        C["x3F"] = arena_y.take([P, NC_, T])
        for n in ("q", "k"):
            C[n] = arena_y.take([P, H1, T])
        C["t2q"] = arena_y.take([P, H1, T])
        C["t2k"] = C["t2q"]
        C["e"] = arena_y.take([P, 2, UB * H1, S])
        C["pT"] = arena_y.take([P, UB * H1, S])
        C["oF"] = arena_y.take([P, H1, T])
        C["r"] = arena_y.take([P, UB, D])
        C["r4"] = arena_y.take([P, UB, D])
        C["mx"] = arena_y.take([P, UB * H1])
        C["sum"] = arena_y.take([P, UB * H1])
        C["rec"] = arena_y.take([P, UB * H1])
        c_idx_t = sb("c_idx_t", [P, 2, TOP0, UB], I32)
        C_st3, C_st4 = sb("C_st3", [P, UB, 10]), sb("C_st4", [P, UB, 10])
        c_in, c_y, c_st = sem2("c_in"), sem2("c_y"), sem2("c_st")
        c_idx, c_mix, c_x3T, c_q, c_k, c_v, c_S, c_pT, c_o, c_wo = (
            sem("c_" + n) for n in ("idx", "mix", "x3T", "q", "k", "v", "S", "pT", "o", "wo"))
        c_x3F, c_q2, c_k2, c_vs, c_ex, c_pTs, c_os = (
            sem("c_" + n) for n in ("x3F", "q2", "k2", "vs", "ex", "pTs", "os"))
        c_qt, c_qr, c_kt, c_kr, c_mx, c_sub, c_sum, c_p, c_r4 = (
            sem("c_" + n) for n in ("qt", "qr", "kt", "kr", "mx", "sub", "sum", "p", "r4"))
        ln3 = [sem("ln3_" + n) for n in ("st", "ag", "rs", "out")]
        ln4 = [sem("ln4_" + n) for n in ("st", "ag", "rs", "out")]
        c_x3, c_x4 = ln3[3], ln4[3]
        C_LAG = 3

        def c_sync(sp):

            def step(t):
                u = t.at(0, UNITS)
                if u:
                    done(sp, c_mix, u.back(2), 2)
                    sp.dma_start(C["x2"][:, u.p], x2_u[u.n]).then_inc(c_in[u.p], 16)
                u = t.at(3, UNITS)
                if u:
                    done(sp, c_x4, u)
                    sp.dma_start(x4_u[u.n], C["x4"][:, u.p]).then_inc(c_st[u.p], 16)
            pipelined(sp, UNITS, C_LAG, step, unroll=4)

        def c_gpsimd(pool):

            def step(t):
                u = t.at(0, UNITS)
                if u:
                    landed(pool, c_y, u.back(2), 4)
                    nc.gpsimd.tensor_copy(c_idx_t[:, u.p], slot_g[:, :, bass.ds(u.n * UB, UB)]).then_inc(c_idx, 1)
                    done(pool, c_idx, u)
                    carry(pool, 2)
                    done(pool, c_mix, u.back(2), 2)
                    carry(pool, 3)
                    for k in range(TOP0):
                        for b in range(UB):
                            nc.gpsimd.indirect_dma_start(
                                out=C["y"][:, u.p, k, b, :], out_offset=None, in_=y_d,
                                in_offset=bass.IndirectOffsetOnAxis(ap=c_idx_t[:, u.p, k, b:b + 1], axis=0),
                                ).then_inc(c_y[u.p], 16)
                    rstd(pool, u, C_st3, ln3)
                u = t.at(3, UNITS)
                if u:
                    rstd(pool, u, C_st4, ln4)
            pipelined(pool, UNITS, C_LAG, step, unroll=4)

        def heads(ap):
            return ap.rearrange("p (n s) -> p n s", s=S)

        def c_tensor(pe):

            def step(t):
                u = t.at(2, UNITS)
                if u:
                    done(pe, c_p, u)
                    done(pe, c_pTs, u.back(1))
                    for n in range(UB * H1):
                        ins = nc.tensor.transpose(bank(5)[:, n * S:(n + 1) * S], C["e"][:, u.p, n, :], ident)
                    ins.then_inc(c_pT, 1)
                u = t.at(1, UNITS)
                if u:
                    done(pe, c_qr, u)
                    done(pe, c_kr, u)
                    done(pe, c_q2, u)
                    done(pe, c_k2, u)
                    done(pe, c_sub, u.back(1))
                    nc.tensor.matmul(bank(4), ident_bf[:, :],
                                     causal_bf[:, None, :].broadcast_to([P, UB * H1, S]), start=True, stop=False,
                                     skip_group_check=True)
                    for b in range(UB):
                        for h in range(H1):
                            n = b * H1 + h
                            ins = nc.tensor.matmul(bank(4)[:, n * S:(n + 1) * S], C["q"][:, h, b * S:(b + 1) * S],
                                                   C["k"][:, h, b * S:(b + 1) * S], start=False,
                                                   stop=(n == UB * H1 - 1), skip_group_check=True)
                    ins.then_inc(c_S, 1)
                u = t.at(2, UNITS)
                if u:
                    done(pe, c_pTs, u)
                    done(pe, c_os, u.back(1))
                    for b in range(UB):
                        for h in range(H1):
                            ins = nc.tensor.matmul(bank(6)[:, h * T + b * S:h * T + (b + 1) * S],
                                                   C["v"][:, u.p, b, h * P:(h + 1) * P],
                                                   C["pT"][:, b * H1 + h, :], start=True, stop=True)
                    ins.then_inc(c_o, 1)
                u = t.at(0, UNITS)
                if u:
                    done(pe, c_x3, u)
                    done(pe, c_x3F, u.back(1))
                    to_feature(bank(0), C["x3"][:, u.c % 4]).then_inc(c_x3T, 1)
                u = t.at(2, UNITS)
                if u:
                    done(pe, c_os, u)
                    done(pe, c_r4, u.back(1))
                    for b in range(UB):
                        for h in range(H1):
                            ins = nc.tensor.matmul(bank(7)[:, b * D:(b + 1) * D], C["oF"][:, h, b * S:(b + 1) * S],
                                                   w["L1_attn_wo"][:, h, :], start=(h == 0), stop=(h == H1 - 1))
                    ins.then_inc(c_wo, 1)
                u = t.at(0, UNITS)
                if u:
                    done(pe, c_x3F, u)
                    for name, k, s_out, read in (("L1_attn_wq", 1, c_q, (c_qt, c_q2)), ("L1_attn_wk", 2, c_k, (c_kt, c_k2))):
                        for r in read:
                            done(pe, r, u.back(1))
                        for h in range(H1):
                            for c in range(NC_):
                                ins = nc.tensor.matmul(bank(k)[:, h * T:(h + 1) * T], w[name][:, c, h * P:(h + 1) * P],
                                                       C["x3F"][:, c, :], start=(c == 0), stop=(c == NC_ - 1))
                        ins.then_inc(s_out, 1)
                    done(pe, c_vs, u.back(1))
                    for b in range(UB):
                        for c in range(NC_):
                            ins = nc.tensor.matmul(bank(3)[:, b * D:(b + 1) * D], C["x3F"][:, c, b * S:(b + 1) * S],
                                                   w["L1_attn_wv"][:, c, :], start=(c == 0), stop=(c == NC_ - 1))
                    ins.then_inc(c_v, 1)
            pipelined(pe, UNITS, C_LAG, step, unroll=4)

        def c_scalar(act):
            def step(t):
                u = t.at(1, UNITS)
                if u:
                    done(act, c_qt, u)
                    done(act, c_S, u.back(1))
                    nc.scalar.activation(C["q"][64:P], bank(1)[64:P, :].rearrange("p (h t) -> p h t", h=H1),
                                         ACT.Copy).then_inc(c_q2, 1)
                    done(act, c_kt, u)
                    nc.scalar.activation(C["k"][64:P], bank(2)[64:P, :].rearrange("p (h t) -> p h t", h=H1),
                                         ACT.Copy).then_inc(c_k2, 1)
                u = t.at(2, UNITS)
                if u:
                    done(act, c_pT, u)
                    done(act, c_o, u.back(1))
                    nc.scalar.activation(C["pT"], heads(bank(5)), ACT.Copy).then_inc(c_pTs, 1)
                    done(act, c_o, u)
                    done(act, c_wo, u.back(1))
                    nc.scalar.activation(C["oF"], chunks(bank(6)), ACT.Copy).then_inc(c_os, 1)
                u = t.at(0, UNITS)
                if u:
                    done(act, c_x3T, u)
                    done(act, c_v, u.back(1))
                    nc.scalar.activation(C["x3F"], chunks(bank(0)), ACT.Copy).then_inc(c_x3F, 1)
                u = t.at(1, UNITS)
                if u:
                    done(act, c_sub, u)
                    nc.scalar.activation(C["e"][:, u.p], C["e"][:, u.p], ACT.Exp, scale=1.0 / P).then_inc(c_ex, 1)
                u = t.at(0, UNITS)
                if u:
                    done(act, c_v, u)
                    done(act, c_o, u.back(2))
                    nc.scalar.activation(C["v"][:, u.p], seqs(bank(3)), ACT.Copy).then_inc(c_vs, 1)
            pipelined(act, UNITS, C_LAG, step, unroll=4)

        def c_vector(dve):
            def rope(u, src, dst, t2, s_t, s_r):
                s3 = heads(src)
                d3, t3 = heads(dst.rearrange("p h t -> p (h t)")), heads(t2.rearrange("p h t -> p (h t)"))

                def tb(name, lo, hi):
                    return table(name)[lo:hi, None, :].broadcast_to([hi - lo, UB * H1, S])
                nc.vector.tensor_tensor(d3[0:64], s3[0:64], tb("rope_cos", 0, 64), ALU.mult)
                nc.vector.tensor_tensor(t3[0:32], s3[32:64], tb("rope_sin", 32, 64), ALU.mult)
                nc.vector.tensor_tensor(t3[32:64], s3[0:32], tb("rope_sin", 0, 32), ALU.mult).then_inc(s_t, 1)
                done(dve, s_t, u)
                nc.vector.tensor_tensor(d3[0:64], d3[0:64], t3[0:64], ALU.add).then_inc(s_r, 1)

            def step(t):
                u = t.at(2, UNITS)
                if u:
                    e = C["e"][:, u.p]
                    done(dve, c_ex, u)
                    nc.vector.tensor_reduce(C["sum"], e, AX, ALU.add).then_inc(c_sum, 1)
                    dve.wait_ge(c_sum, u.n * 2 + 1)
                    nc.vector.reciprocal(C["rec"], C["sum"]).then_inc(c_sum, 1)
                    dve.wait_ge(c_sum, u.n * 2 + 2)
                    nc.vector.tensor_tensor(e, e, C["rec"][:, :, None].broadcast_to([P, UB * H1, S]),
                                            ALU.mult).then_inc(c_p, 1)
                u = t.at(1, UNITS)
                if u:
                    done(dve, c_q, u)
                    done(dve, c_S, u.back(1))
                    rope(u, bank(1), C["q"], C["t2q"], c_qt, c_qr)
                    done(dve, c_k, u)
                    done(dve, c_qr, u)
                    rope(u, bank(2), C["k"], C["t2k"], c_kt, c_kr)
                u = t.at(0, UNITS)
                if u:
                    landed(dve, c_in, u)
                    landed(dve, c_y, u, 4)
                    done(dve, c_x3, u.back(1))
                    for k in range(TOP0):
                        for b in range(UB):
                            ins = nc.vector.scalar_tensor_tensor(
                                C["r"][:, b, :], C["y"][:, u.p, k, b, :], gates[:, k, bass.ds(u.n * UB + b, 1)],
                                C["x2"][:, u.p, b, :] if k == 0 else C["r"][:, b, :], ALU.mult, ALU.add)
                        ins.then_inc(c_mix, 1)
                        dve.wait_ge(c_mix, u.n * 2 + (k + 1))
                    layer_norm(dve, u, C["r"], C["x3"][:, u.c % 4], C_st3, ln3)
                u = t.at(3, UNITS)
                if u:
                    done(dve, c_wo, u)
                    done(dve, c_x4, u.back(1))
                    nc.vector.tensor_tensor(C["r4"], seqs(bank(7)), C["x3"][:, u.c % 4], ALU.add).then_inc(c_r4, 1)
                    done(dve, c_r4, u)
                    landed(dve, c_st, u.back(2))
                    layer_norm(dve, u, C["r4"], C["x4"][:, u.p], C_st4, ln4)
                u = t.at(1, UNITS)
                if u:
                    done(dve, c_S, u)
                    done(dve, c_pT, u.back(2))
                    nc.vector.tensor_reduce(C["mx"], heads(bank(4)), AX, ALU.max).then_inc(c_mx, 1)
                    done(dve, c_mx, u)
                    nc.vector.tensor_tensor(C["e"][:, u.p], heads(bank(4)),
                                            C["mx"][:, :, None].broadcast_to([P, UB * H1, S]),
                                            ALU.subtract).then_inc(c_sub, 1)
            pipelined(dve, UNITS, C_LAG, step, unroll=4)

        add("sync", c_sync)
        add("gpsimd", c_gpsimd)
        add("tensor", c_tensor)
        add("scalar", c_scalar)
        add("vector", c_vector)
        arena_x.reset()
        VW = 2 * HD
        X = {}
        X["x4"] = arena_x.take([P, 2, UB, D])
        X["cx"] = arena_x.take([P, 2, UB, D])
        X["xb"] = arena_x.take([P, 4, UB, D])
        X["x4F"] = arena_x.take([P, NC_, T])
        X["cF"] = arena_x.take([P, NC_, T])
        X["q"] = arena_x.take([P, 2, NC_, T])
        X["k"] = arena_x.take([P, 2, 2, NC_ * T])
        X["v"] = arena_x.take([P, 2, UB, NH, VW])
        X["e"] = arena_x.take([P, UB, NH, S])
        X["eT"] = arena_x.take([P, 2, NH * S])
        X["aF"] = arena_x.take([P, NC_, T])
        X["x5"] = arena_x.take([P, 2, UB, D])
        X["r"] = arena_x.take([P, UB, D])
        X["mx"] = arena_x.take([P, 2, NH])
        X["rec"] = arena_x.take([P, NC_, S])
        X["half"] = arena_x.take([P, 2, VW])
        ARENA_X_E = arena_x.at
        X_st = sb("X_st", [P, UB, 10])
        x_in, x_st = sem2("x_in"), sem2("x_st")
        x_xT, x_cT, x_q, x_k, x_v, x_S, x_eT, x_pv, x_wo = (
            sem("x_" + n) for n in ("xT", "cT", "q", "k", "v", "S", "eT", "pv", "wo"))
        x_xF, x_cF, x_qs, x_ks, x_ex, x_eTs = (
            sem("x_" + n) for n in ("xF", "cF", "qs", "ks", "ex", "eTs"))
        x_mask = sem("x_mask")
        x_vs, x_mx, x_sub, x_rec, x_at, x_r, x_xb, x_one = (
            sem("x_" + n) for n in ("vs", "mx", "sub", "rec", "at", "r", "xb", "one"))
        ln5 = [sem("ln5_" + n) for n in ("st", "ag", "rs", "out")]
        x_x5 = ln5[3]
        E_LAG = 3

        def seq_done(eng, s, u, b, per=1, k=None):
            if u.fixed and u.n < 0:
                return
            if b < 0:
                u, b = u.back(1), b + 2
                if u.fixed and u.n < 0:
                    return
            eng.wait_ge(s, u.n * (2 * per) + (b * per + (per if k is None else k)))

        def e_sync(sp):
            sp.wait_ge(c_st[0], 16 * per_parity)
            sp.wait_ge(c_st[1], 16 * per_parity)
            d_weights(sp)

            def step(t):
                u = t.at(0, UNITS)
                if u:
                    done(sp, x_xb, u.back(2))
                    done(sp, x_xT, u.back(2))
                    sp.dma_start(X["x4"][:, u.p], x4_u[u.n]).then_inc(x_in[u.p], 16)
                    done(sp, x_cT, u.back(2))
                    sp.dma_start(X["cx"][:, u.p], ctx_u[u.n]).then_inc(x_in[u.p], 16)
                u = t.at(3, UNITS)
                if u:
                    done(sp, x_x5, u)
                    sp.dma_start(x5_u[u.n], X["x5"][:, u.p]).then_inc(x_st[u.p], 16)
            pipelined(sp, UNITS, E_LAG, step, unroll=4)

        def e_gpsimd(pool):

            def step(t):
                u = t.at(2, UNITS)
                if u:
                    rstd(pool, u, X_st, ln5)
                u = t.at(0, UNITS)
                if u:
                    landed(pool, x_in, u, 2)
                    done(pool, x_r, u.back(4))
                    for b in range(UB):
                        ins = nc.gpsimd.tensor_tensor(X["xb"][:, u.c % 4, b, :], X["x4"][:, u.p, b, :], bo_b[:, :],
                                                      ALU.add)
                    ins.then_inc(x_xb, 1)
            pipelined(pool, UNITS, E_LAG, step, unroll=4)

        def e_tensor(pe):
            pe.wait_ge(c_x3F, UNITS)
            pe.wait_ge(c_q2, UNITS)
            pe.wait_ge(c_k2, UNITS)
            pe.wait_ge(c_vs, UNITS)
            pe.wait_ge(c_sub, UNITS)
            pe.wait_ge(c_pTs, UNITS)
            pe.wait_ge(c_os, UNITS)
            pe.wait_ge(c_r4, UNITS)

            def scores(u, b):
                seq_done(pe, x_sub, u, b - 1)
                for quad in range(4):
                    ins = nc.tensor.matmul(bank(quad), ones_row[:, :],
                                           mask_row[:, None, bass.ds(u.n * T + b * S, S)].broadcast_to([1, 4, S]),
                                           start=True, stop=False, skip_group_check=True)
                ins.then_inc(x_mask, 1)
                seq_done(pe, x_mask, u, b)
                for c in range(NC_):
                    for par in range(2):
                        for quad in range(4):
                            rows = slice(32 * quad, 32 * quad + 32)
                            at = (2 * c + par) * S
                            ins = nc.tensor.matmul(bank(quad)[:, at:at + S],
                                                   X["q"][rows, u.p, c, b * S:(b + 1) * S],
                                                   X["k"][rows, u.p, par, c * T + b * S:c * T + (b + 1) * S],
                                                   start=False, stop=(c == 1 and par == 1), skip_group_check=True)
                ins.then_inc(x_S, 1)

            def attend(u, b):
                seq_done(pe, x_ex, u, b)
                for g in range(4):
                    seq_done(pe, x_eTs, u, b, 4, g - 1) if g >= 2 else seq_done(pe, x_eTs, u, b - 1, 4, g + 3)
                    for k in range(4):
                        ins = nc.tensor.transpose(bank(4 + g % 2)[:, k * S:(k + 1) * S], X["e"][:, b, 4 * g + k, :],
                                                  ident)
                    ins.then_inc(x_eT, 1)

            def values(u, b):
                seq_done(pe, x_eTs, u, b, 4)
                for c in range(NC_):
                    for par in range(2):
                        for kind in range(2):
                            for quad in range(4):
                                at = (4 * quad + 2 * c + par) * S
                                left = (X["v"][:, u.p, b, 8 * c + 2 * quad + par, :], X["half"][:, par, :])[kind]
                                ins = nc.tensor.matmul(
                                    bank(7)[32 * quad:32 * quad + 32, (kind * NC_ + c) * S:(kind * NC_ + c + 1) * S],
                                    left, X["eT"][:, b, at:at + S], start=(c == par == kind == 0), stop=(c == par == kind == 1),
                                    skip_group_check=True)
                ins.then_inc(x_pv, 1)

            def step(t):
                u0, u1, u2 = t.at(0, UNITS), t.at(1, UNITS), t.at(2, UNITS)
                if u1:
                    done(pe, x_qs, u1)
                    done(pe, x_ks, u1, 4)
                    scores(u1, 0)
                if u0:
                    landed(pe, x_in, u0, 2)
                    done(pe, x_vs, u0.back(1))
                    done(pe, x_r, u0.back(3))
                    to_feature(bank(6), X["x4"][:, u0.p]).then_inc(x_xT, 1)
                if u2:
                    attend(u2, 1)
                    seq_done(pe, x_at, u2, 0)
                    values(u2, 1)
                if u0:
                    done(pe, x_xF, u0)
                    for m in range(NC_):
                        for c in range(NC_):
                            ins = nc.tensor.matmul(bank(6)[:, m * T:(m + 1) * T],
                                                   w["L1_xattn_Wq"][:, c, m * P:(m + 1) * P], X["x4F"][:, c, :],
                                                   start=(c == 0), stop=(c == NC_ - 1))
                    ins.then_inc(x_q, 1)
                    done(pe, x_ks, u0.back(1), 4)
                    seq_done(pe, x_at, u0.back(2), 1)
                    to_feature(bank(7), X["cx"][:, u0.p]).then_inc(x_cT, 1)
                if u2:
                    if u0:
                        done(pe, x_qs, u0)
                    else:
                        done(pe, x_r, u2.back(1))
                    seq_done(pe, x_at, u2, 1)
                    for b in range(UB):
                        for c in range(NC_):
                            ins = nc.tensor.matmul(bank(6)[:, b * D:(b + 1) * D], X["aF"][:, c, b * S:(b + 1) * S],
                                                   w["L1_xattn_Wo"][:, c, :], start=(c == 0), stop=(c == NC_ - 1))
                    ins.then_inc(x_wo, 1)
                if u0:
                    done(pe, x_cF, u0)
                    for m in range(NC_):
                        for c in range(NC_):
                            ins = nc.tensor.matmul(bank(7)[:, m * T:(m + 1) * T],
                                                   w["L1_xattn_Wk"][:, c, m * P:(m + 1) * P], X["cF"][:, c, :],
                                                   start=(c == 0), stop=(c == NC_ - 1))
                    ins.then_inc(x_k, 1)
                    done(pe, x_qs, u0)
                    if u2:
                        done(pe, x_r, u2)
                    for b in range(UB):
                        for c in range(NC_):
                            ins = nc.tensor.matmul(bank(6)[:, b * D:(b + 1) * D], X["cF"][:, c, b * S:(b + 1) * S],
                                                   w["L1_xattn_Wv"][:, c, :], start=(c == 0), stop=(c == NC_ - 1))
                    ins.then_inc(x_v, 1)
                if u1:
                    scores(u1, 1)
                    attend(u1, 0)
                    if u0:
                        done(pe, x_ks, u0, 4)
                    elif u2:
                        seq_done(pe, x_at, u2, 1)
                    done(pe, x_vs, u1)
                    values(u1, 0)
            pipelined(pe, UNITS, E_LAG, step, unroll=4)

        def e_scalar(act):

            def turned(u, b):
                for g in range(4):
                    seq_done(act, x_eT, u, b, 4, g + 1)
                    if g == 0:
                        seq_done(act, x_pv, u.back(1), b)
                    nc.scalar.activation(X["eT"][:, b, g * 512:(g + 1) * 512], bank(4 + g % 2), ACT.Copy)\
                        .then_inc(x_eTs, 1)

            def step(t):
                u0, u1, u2 = t.at(0, UNITS), t.at(1, UNITS), t.at(2, UNITS)
                if u0:
                    done(act, x_xT, u0)
                    done(act, x_q, u0.back(1))
                    nc.scalar.activation(X["x4F"], chunks(bank(6)), ACT.Copy).then_inc(x_xF, 1)
                if u2:
                    turned(u2, 1)
                if u0:
                    done(act, x_q, u0)
                    seq_done(act, x_S, u0.back(2), 1)
                    for c in range(NC_):
                        ins = nc.scalar.activation(X["q"][:, u0.p, c, :], bank(6)[:, c * T:(c + 1) * T], ACT.Identity,
                                                   bias=vec[:, V_BQ + c:V_BQ + c + 1])
                    ins.then_inc(x_qs, 1)
                    done(act, x_cT, u0)
                    done(act, x_v, u0.back(1))
                    nc.scalar.activation(X["cF"], chunks(bank(7)), ACT.Copy).then_inc(x_cF, 1)
                if u1:
                    seq_done(act, x_sub, u1, 0)
                    nc.scalar.activation(X["e"][:, 0], X["e"][:, 0], ACT.Exp, scale=HD ** -0.5).then_inc(x_ex, 1)
                if u0:
                    done(act, x_k, u0)
                    for par, name in enumerate(("even_heads", "odd_heads")):
                        for c in range(NC_):
                            nc.scalar.activation(X["k"][:, u0.p, par, c * T:(c + 1) * T], bank(7)[:, c * T:(c + 1) * T],
                                                 ACT.Identity, bias=kb_par[:, par, c:c + 1],
                                                 scale=table(name)).then_inc(x_ks, 1)
                if u1:
                    turned(u1, 0)
                    seq_done(act, x_sub, u1, 1)
                    nc.scalar.activation(X["e"][:, 1], X["e"][:, 1], ACT.Exp, scale=HD ** -0.5).then_inc(x_ex, 1)
            pipelined(act, UNITS, E_LAG, step, unroll=4)

        def e_vector(dve):
            nc.vector.memset(X["v"].rearrange("p a b h o -> p (a b h o)"), 0.0).then_inc(x_one, 1)
            nc.vector.memset(X["half"].rearrange("p a o -> p (a o)"), 0.0).then_inc(x_one, 1)
            dve.wait_ge(x_one, 2)
            for par in range(2):
                nc.vector.memset(X["half"][:, par, par * HD:(par + 1) * HD], 1.0).then_inc(x_one, 1)

            def less_max(u, b):
                s3 = psum[:, 0:4, :].rearrange("p q (k s) -> p (q k) s", s=S)
                seq_done(dve, x_S, u, b)
                seq_done(dve, x_eT, u.back(1), b, 4)
                nc.vector.tensor_reduce(X["mx"][:, b, :], s3, AX, ALU.max).then_inc(x_mx, 1)
                seq_done(dve, x_mx, u, b)
                nc.vector.tensor_tensor(X["e"][:, b], s3, X["mx"][:, b, :, None].broadcast_to([P, NH, S]),
                                        ALU.subtract).then_inc(x_sub, 1)

            def normalise(u, b):
                seq_done(dve, x_pv, u, b)
                seq_done(dve, x_at, u, b - 1)
                nc.vector.reciprocal(X["rec"], bank(7)[:, D:2 * D].rearrange("p (c s) -> p c s", c=NC_)).then_inc(x_rec, 1)
                seq_done(dve, x_rec, u, b)
                nc.vector.tensor_tensor(X["aF"][:, :, b * S:(b + 1) * S],
                                        bank(7)[:, 0:D].rearrange("p (c s) -> p c s", c=NC_), X["rec"],
                                        ALU.mult).then_inc(x_at, 1)

            def step(t):
                u0, u1, u2 = t.at(0, UNITS), t.at(1, UNITS), t.at(2, UNITS)
                if u1:
                    less_max(u1, 0)
                if u2:
                    normalise(u2, 1)
                    done(dve, x_wo, u2)
                    done(dve, x_xb, u2)
                    done(dve, x_x5, u2.back(1))
                    nc.vector.tensor_tensor(X["r"], seqs(bank(6)), X["xb"][:, u2.c % 4], ALU.add).then_inc(x_r, 1)
                    done(dve, x_r, u2)
                    ln_stats(dve, u2, X["r"], X_st, ln5)
                if u0:
                    done(dve, x_v, u0)
                    seq_done(dve, x_pv, u0.back(2), 1)
                    for par in range(2):
                        ins = nc.vector.tensor_tensor(
                            X["v"][:, u0.p].rearrange("p b (i k) o -> p (b i) k o", k=2)[:, :, par,
                                                                                       par * HD:(par + 1) * HD],
                            bank(6).rearrange("p (i k d) -> p i k d", k=2, d=HD)[:, :, par, :],
                            bv2_b[:, :].rearrange("p (i k d) -> p i k d", k=2, d=HD)[:, :, par, :], ALU.add)
                    ins.then_inc(x_vs, 1)
                if u2:
                    landed(dve, x_st, u2.back(2))
                    ln_apply(dve, u2, X["r"], X["x5"][:, u2.p], X_st, ln5)
                if u1:
                    less_max(u1, 1)
                    normalise(u1, 0)
            pipelined(dve, UNITS, E_LAG, step, unroll=4)

        add("sync", e_sync)
        add("gpsimd", e_gpsimd)
        add("tensor", e_tensor)
        add("scalar", e_scalar)
        add("vector", e_vector)

        HIDD = NE1 * PD
        HJ = HIDD // P
        N_TOP, TOP_LESS = 18, 2
        SL = HJ // 2
        arena_x.reset()
        arena_y.reset()
        K = {}
        K["vd"] = arena_y.take([P, NC_, HIDD])
        K["vu"] = arena_y.take([P, HJ, D])
        K["x5"] = arena_x.take([P, 4, UB, D])
        K["x5F"] = arena_x.take([P, 2, NC_, T])
        K["r"] = arena_x.take([P, UB, D])
        K["th"] = arena_x.take([P, 2, 2, T])
        K["t"] = arena_x.take([P, 2, 2, T])
        K["g"] = arena_x.take([P, 2, 2, T])
        K["hF"] = arena_x.take([P, T])[0:PD, :]
        for n in ("sim", "gt", "eq", "cum", "ex", "rem"):
            K[n] = arena_x.take([P, UB, NE1])
        K["mx8"] = arena_x.take([P, UB, 8])
        K["ngt"] = arena_x.take([P, UB])
        K["sum"] = arena_x.take([P, UB])
        expand = arena_x.take([P, HIDD // 2]).bitcast(BF16)
        parts = arena_x.take([P, UB, 4 * NE1 // 2]).bitcast(BF16)
        wT = arena_x.take([P, 2, T // 2]).bitcast(BF16)
        K_st = arena_x.take([P, UB, 10])
        keep_ex = arena_x.take([P, UB, NE1])
        d_w = sem("d_w")
        d_in, d_st = sem2("d_in"), sem2("d_st")
        d_xT, d_h, d_sim, d_z, d_wb, d_up, d_wTp = (sem("d_" + n) for n in ("xT", "h", "sim", "z", "wb", "up", "wTp"))
        d_xF, d_hF, d_sims, d_th, d_ex, d_wT = (sem("d_" + n) for n in ("xF", "hF", "sims", "th", "ex", "wT"))
        d_one, d_top, d_t, d_g, d_r = (sem("d_" + n) for n in ("one", "top", "t", "g", "r"))
        ln6 = [sem("ln6_" + n) for n in ("st", "ag", "rs", "out")]
        d_out = ln6[3]
        D_LAG = 2

        def slice_done(eng, s, u, k):
            seq_done(eng, s, u, k // 4, 4, k % 4 + 1)

        def d_weights(eng):
            eng.dma_start(K["vd"], a["down"].rearrange("(c p) h -> p c h", p=P)).then_inc(d_w, 16)
            eng.dma_start(K["vu"], a["up"].rearrange("(j p) d -> p j d", p=P)).then_inc(d_w, 16)

        def d_sync(sp):
            for k in range(2):
                sp.wait_ge(x_st[k], 16 * per_parity)

            def step(t):
                u = t.at(0, UNITS)
                if u:
                    landed(sp, d_st, u.back(4))
                    done(sp, d_xT, u.back(2))
                    sp.dma_start(K["x5"][:, u.c % 4], x5_u[u.n]).then_inc(d_in[u.p], 16)
                u = t.at(2, UNITS)
                if u:
                    done(sp, d_out, u)
                    sp.dma_start(out_u[u.n], K["x5"][:, u.c % 4]).then_inc(d_st[u.p], 16)
            pipelined(sp, UNITS, D_LAG, step, unroll=4)
            for k in range(2):
                sp.wait_ge(d_st[k], 16 * per_parity)

        def d_gpsimd(pool):
            def step(t):
                u = t.at(2, UNITS)
                if u:
                    rstd(pool, u, K_st, ln6)
            pipelined(pool, UNITS, D_LAG, step, unroll=4)

        def d_tensor(pe):
            pe.wait_ge(d_w, 32)
            pe.wait_ge(d_one, 5)
            pe.wait_ge(x_r, UNITS)
            seq_done(pe, x_eTs, Unit(0, UNITS - 1), 1, 4)

            def up(u, s):
                slice_done(pe, d_g, u, s)
                for k in range(2):
                    for b in range(UB):
                        ins = nc.tensor.matmul(bank(4 + u.p)[:, b * D:(b + 1) * D],
                                               K["g"][:, s % 2, k, b * S:(b + 1) * S], K["vu"][:, 2 * s + k, :],
                                               start=(s == 0 and k == 0 and b == 0), stop=(s == SL - 1 and k == 1),
                                               skip_group_check=True)
                ins.then_inc(d_up, 1)

            def step(t):
                u0, u1, u2 = t.at(0, UNITS), t.at(1, UNITS), t.at(2, UNITS)
                for s in range(SL):
                    if u1:
                        if s == 0:
                            done(pe, d_xF, u1)
                        slice_done(pe, d_t, u1, s - 2)
                        for k in range(2):
                            j = 2 * s + k
                            for c in range(NC_):
                                ins = nc.tensor.matmul(bank(s % 2)[:, k * T:(k + 1) * T],
                                                       K["vd"][:, c, j * P:(j + 1) * P], K["x5F"][:, u1.p, c, :],
                                                       start=(c == 0), stop=(c == NC_ - 1))
                        ins.then_inc(d_z, 1)
                        if s == 0:
                            done(pe, d_wT, u1, 2)
                        slice_done(pe, d_g, u1, s - 2)
                        for k in range(2):
                            j = 2 * s + k
                            for part in range(2):
                                ins = nc.tensor.matmul(bank(2 + s % 2)[:, k * T:(k + 1) * T],
                                                       expand[:, j * P:(j + 1) * P], wT[:, part, :],
                                                       start=(part == 0), stop=(part == 1))
                        ins.then_inc(d_wb, 1)
                    if s >= 2 and u1:
                        if s == 2:
                            done(pe, d_r, u1.back(2))
                        up(u1, s - 2)
                    if s < 2 and u2:
                        up(u2, SL + s - 2)
                    if not u0:
                        continue
                    if s == 0:
                        landed(pe, d_in, u0)
                        done(pe, d_wT, u0.back(1), 2)
                        to_feature(bank(6), K["x5"][:, u0.c % 4]).then_inc(d_xT, 1)
                    if s == 1:
                        done(pe, d_xF, u0)
                        done(pe, d_sims, u0.back(1))
                        for c in range(NC_):
                            ins = nc.tensor.matmul(bank(7)[0:PD, 0:T], w_hash[:, c, :], K["x5F"][:, u0.p, c, :],
                                                   start=(c == 0), stop=(c == NC_ - 1))
                        ins.then_inc(d_h, 1)
                    if s == 2:
                        done(pe, d_hF, u0)
                        for b in range(UB):
                            ins = nc.tensor.matmul(bank(7)[:, T + b * NE1:T + (b + 1) * NE1],
                                                   K["hF"][:, b * S:(b + 1) * S], w_keys[:, :], start=True, stop=True)
                        ins.then_inc(d_sim, 1)
                    if s == SL - 1:
                        done(pe, d_top, u0, N_TOP)
                        for part in range(2):
                            for b in range(UB):
                                ins = nc.tensor.transpose(
                                    bank(6)[:, part * P:(part + 1) * P].bitcast(BF16)[:, b * S:(b + 1) * S],
                                    parts[:, b, part * P:(part + 1) * P], ident_bf[:, :])
                        ins.then_inc(d_wTp, 1)
            pipelined(pe, UNITS, D_LAG, step, unroll=4)

        def d_scalar(act):
            def step(t):
                u0, u1 = t.at(0, UNITS), t.at(1, UNITS)
                for s in range(SL):
                    if u1:
                        slice_done(act, d_z, u1, s)
                        slice_done(act, d_t, u1, s - 2)
                        nc.scalar.activation(K["th"][:, s % 2], bank(s % 2).rearrange("p (k t) -> p k t", k=2), ACT.Tanh,
                                             scale=0.5).then_inc(d_th, 1)
                    if not u0:
                        continue
                    if s == 0:
                        done(act, d_xT, u0)
                        slice_done(act, d_z, u0.back(2), SL - 1)
                        nc.scalar.activation(K["x5F"][:, u0.p], chunks(bank(6)), ACT.Copy).then_inc(d_xF, 1)
                    if s == 1:
                        done(act, d_h, u0)
                        done(act, d_sim, u0.back(1))
                        nc.scalar.activation(K["hF"], bank(7)[0:PD, 0:T], ACT.Copy).then_inc(d_hF, 1)
                    if s == 2:
                        done(act, d_sim, u0)
                        done(act, d_top, u0.back(1), N_TOP)
                        nc.scalar.activation(K["sim"], bank(7)[:, T:T + UB * NE1].rearrange("p (b e) -> p b e", b=UB),
                                             ACT.Copy).then_inc(d_sims, 1)
                    if s == 4:
                        act.wait_ge(d_top, u0.n * N_TOP + TOP_LESS)
                        nc.scalar.activation(K["ex"], K["ex"], ACT.Exp).then_inc(d_ex, 1)
                    if s == SL - 1:
                        done(act, d_wTp, u0)
                        slice_done(act, d_wb, u1, SL - 1) if u1 else None
                        for part in range(2):
                            nc.scalar.activation(wT[:, part, :], bank(6)[:, part * P:(part + 1) * P].bitcast(BF16),
                                                 ACT.Copy).then_inc(d_wT, 1)
            pipelined(act, UNITS, D_LAG, step, unroll=4)

        def d_vector(dve):
            dve.wait_ge(x_st[0], 16 * per_parity)
            dve.wait_ge(x_st[1], 16 * per_parity)
            for lo in (0, NE1):
                rows = slice(lo, lo + NE1)
                nc.vector.tensor_scalar(expand[rows, :].rearrange("p (e r) -> p e r", r=PD),
                                        ident[rows, lo:lo + NE1, None].broadcast_to([NE1, NE1, PD]), 1.0, None,
                                        ALU.mult).then_inc(d_one, 1)
            nc.vector.memset(parts[:, :, 3 * NE1:], 0.0).then_inc(d_one, 1)
            nc.vector.memset(keep_ex[:, :, 1:], 1.0).then_inc(d_one, 1)
            nc.vector.memset(keep_ex[:, :, 0:1], 0.0).then_inc(d_one, 1)
            dve.wait_ge(d_one, 5)

            def choose(u):
                steps = [0]

                def after(ins):
                    ins.then_inc(d_top, 1)
                    steps[0] += 1

                def ready():
                    dve.wait_ge(d_top, u.n * N_TOP + steps[0])

                def per_b(ap, k=0):
                    return ap[:, :, k:k + 1].broadcast_to([P, UB, NE1])

                done(dve, d_sims, u)
                nc.vector.memset(wait_cell[:, :], 0.0)
                for b in range(UB):
                    ins = nc.vector.max(K["mx8"][:, b, :], K["sim"][:, b, :])
                after(ins)
                ready()
                after(nc.vector.tensor_tensor(K["ex"], K["sim"], per_b(K["mx8"]), ALU.subtract))
                after(nc.vector.tensor_tensor(K["gt"], K["sim"], per_b(K["mx8"], TOP1 - 1), ALU.is_gt))
                after(nc.vector.tensor_tensor(K["eq"], K["sim"], per_b(K["mx8"], TOP1 - 1), ALU.is_equal))
                ready()
                after(nc.vector.tensor_reduce(K["ngt"], K["gt"], AX, ALU.add))
                after(nc.vector.tensor_tensor_scan(K["cum"].rearrange("p b e -> p (b e)"), keep_ex.rearrange("p b e -> p (b e)"),
                                                   K["eq"].rearrange("p b e -> p (b e)"), 0.0, ALU.mult, ALU.add))
                ready()
                after(nc.vector.tensor_tensor(K["cum"], K["cum"], K["ngt"][:, :, None].broadcast_to([P, UB, NE1]),
                                              ALU.add))
                ready()
                after(nc.vector.scalar_tensor_tensor(K["eq"], K["cum"], float(TOP1), K["eq"], ALU.is_le, ALU.mult))
                ready()
                after(nc.vector.tensor_tensor(K["gt"], K["gt"], K["eq"], ALU.add))
                ready()
                done(dve, d_ex, u)
                after(nc.vector.tensor_tensor(K["ex"], K["ex"], K["gt"], ALU.mult))
                ready()
                after(nc.vector.tensor_reduce(K["sum"], K["ex"], AX, ALU.add))
                ready()
                after(nc.vector.reciprocal(K["sum"], K["sum"]))
                ready()
                after(nc.vector.tensor_scalar(K["sum"], K["sum"], scale_b[:, 0:1], 0.5, ALU.mult, ALU.mult))
                ready()
                after(nc.vector.tensor_tensor(K["ex"], K["ex"], K["sum"][:, :, None].broadcast_to([P, UB, NE1]),
                                              ALU.mult))
                ready()
                done(dve, d_wTp, u.back(1))
                after(nc.vector.tensor_scalar(parts[:, :, 0:NE1], K["ex"], 1.0, None, ALU.mult))
                ready()
                after(nc.vector.tensor_tensor(K["rem"], K["ex"], parts[:, :, 0:NE1], ALU.subtract))
                ready()
                after(nc.vector.tensor_scalar(parts[:, :, NE1:2 * NE1], K["rem"], 1.0, None, ALU.mult))
                ready()
                after(nc.vector.tensor_tensor(parts[:, :, 2 * NE1:3 * NE1], K["rem"], parts[:, :, NE1:2 * NE1],
                                              ALU.subtract))
                assert steps[0] == N_TOP, steps

            def step(t):
                u0, u1, u2 = t.at(0, UNITS), t.at(1, UNITS), t.at(2, UNITS)
                for s in range(SL):
                    if u1:
                        slice_done(dve, d_th, u1, s)
                        slice_done(dve, d_g, u1, s - 2)
                        z = bank(s % 2).rearrange("p (k t) -> p k t", k=2)
                        nc.vector.scalar_tensor_tensor(K["t"][:, s % 2], K["th"][:, s % 2], 1.0, z, ALU.add,
                                                       ALU.mult).then_inc(d_t, 1)
                        slice_done(dve, d_t, u1, s)
                        slice_done(dve, d_wb, u1, s)
                        slice_done(dve, d_up, u1, s - 2)
                        nc.vector.tensor_tensor(K["g"][:, s % 2], K["t"][:, s % 2],
                                                bank(2 + s % 2).rearrange("p (k t) -> p k t", k=2),
                                                ALU.mult).then_inc(d_g, 1)
                    if s == 3 and u0:
                        choose(u0)
                    if s == 2 and u2:
                        slice_done(dve, d_up, u2, SL - 1)
                        done(dve, d_out, u2.back(1))
                        nc.vector.scalar_tensor_tensor(K["r"], K["x5"][:, u2.c % 4], 2.0, seqs(bank(4 + u2.p)),
                                                       ALU.mult, ALU.add).then_inc(d_r, 1)
                        done(dve, d_r, u2)
                        layer_norm(dve, u2, K["r"], K["x5"][:, u2.c % 4], K_st, ln6)
            pipelined(dve, UNITS, D_LAG, step, unroll=4)

        add("sync", d_sync)
        add("gpsimd", d_gpsimd)
        add("tensor", d_tensor)
        add("scalar", d_scalar)
        add("vector", d_vector)
        run_layer()


def kernel(**inputs):
    import concourse.bacc as _bacc
    from concourse.bass_utils import run_bass_kernel_spmd as _run

    nc = _bacc.Bacc("TRN2", target_bir_lowering=False, num_devices=1)
    table, where = constants()
    given = {k: np.asarray(v) for k, v in inputs.items()}
    given["mask"] = given.pop("mask_BxS2_bk0")
    given["hash_t"] = given.pop("L1_ffn_hasher_w").T
    given["keys_t"] = given.pop("L1_ffn_keys").T
    given["down"] = given.pop("L1_ffn_values_down").transpose(1, 0, 2).reshape(D, NE1 * PD)
    given["up"] = given.pop("L1_ffn_values_up").reshape(NE1 * PD, D)
    given["constants"] = table
    arrays, args = {}, {}
    for name, v in given.items():
        v = np.ascontiguousarray(v)
        arrays[f"in_{name}"] = v
        args[name] = nc.dram_tensor(f"in_{name}", v.shape, mybir.dt.from_np(v.dtype), kind="ExternalInput").ap()
    out = nc.dram_tensor("out_0", (B, S, D), F32, kind="ExternalOutput").ap()
    decoder(nc, args, where, out)
    return _run(nc, [arrays], core_ids=[0]).results[0]["out_0"]
```

```python
from contextlib import ExitStack

import numpy as np
import concourse.bass as bass
from concourse import mybir

F32 = mybir.dt.float32
BF16 = mybir.dt.bfloat16
F32R = mybir.dt.float32r
I32 = mybir.dt.int32
U8 = mybir.dt.uint8
ALU = mybir.AluOpType
ACT = mybir.ActivationFunctionType
AX = mybir.AxisListType.X

P = 128
B, S, D = 32, 128, 256
NC_ = D // P
UB = 2
T = UB * S
UNITS = B // UB
LN_EPS = 1e-5
BIG = 1e30

E0, HID0, TOP0 = 8, 1024, 2
CAP = TOP0 * B * S // E0
SLOTS = E0 * CAP
BW = 32
MIN_DECAY, A_EPS, SCAN_EPS = 0.001, 1e-5, 1e-7
GAMMA, THETA, SCALE_BASE = 0.96875, 10000.0, 512.0
H1 = 2
NH, HD = 16, 16
NE1, PD, TOP1 = 64, 32, 4


def constants():
    f = np.float32
    pos = np.arange(S, dtype=f)
    half = D // 2
    scale_vec = (np.arange(0, D, 2, dtype=f) + f(0.4 * D)) / f(1.4 * D)
    scale = (scale_vec[None, :] ** (pos / f(SCALE_BASE))[:, None]).astype(f)
    freqs = (f(1.0) / f(THETA) ** (np.arange(half, dtype=f) / f(half))).astype(f)
    ang = pos[:, None] * freqs[None, :]
    sin, cos = np.sin(ang).astype(f), np.cos(ang).astype(f)
    inv = (f(1.0) / scale).astype(f)
    diff = pos[:, None] - pos[None, :]
    decay = np.where(diff >= 0, f(GAMMA) ** diff, 0).astype(f)
    rot = 32
    rang = pos[:, None] * np.power(f(10000.0), -np.arange(rot, dtype=f) / f(rot)).astype(f)[None, :]
    rsin, rcos = np.sin(rang).astype(f), np.cos(rang).astype(f)
    rope_c = np.zeros((P, S), f)
    rope_c[0:32], rope_c[32:64] = rcos.T, rcos.T
    rope_s = np.zeros((P, S), f)
    rope_s[0:32], rope_s[32:64] = rsin.T, -rsin.T
    first = (np.arange(NC_ * T) % S) == 0
    odd = ((np.arange(P) // HD) % 2).astype(f)
    seg = np.arange(E0 * TOP0 * B) % (TOP0 * B) != 0

    def row(a):
        return np.broadcast_to(np.asarray(a, f), (P, len(a)))

    tables = {
        "ident": np.eye(P, dtype=f),
        "xpos_q_cos": (cos * scale).T, "xpos_q_sin": (sin * scale).T,
        "xpos_k_cos": (cos * inv).T, "xpos_k_sin": (sin * inv).T,
        "decay_t": decay.T,
        "rope_cos": rope_c, "rope_sin": rope_s,
        "causal": np.where(diff >= 0, 0, -BIG).astype(f),
        "before": (diff.T > 0).astype(f),
        "ones": np.ones((P, P), f),
        "floor": row(np.where(first, 1.0, SCAN_EPS)),
        "keep": row(np.where(first, 0.0, 1.0)),
        "keep_seg": row(seg.astype(f)),
        "rank": row(E0 - np.arange(E0)),
        "base": row(np.arange(E0) * CAP),
        "even_heads": (1 - odd)[:, None], "odd_heads": odd[:, None],
    }
    at, parts, where = 0, [], {}
    for name, a in tables.items():
        where[name] = (at, a.shape[1])
        at += a.shape[1]
        parts.append(np.asarray(a, f))
    return np.ascontiguousarray(np.concatenate(parts, axis=1)), where


class Arena:

    def __init__(self, nc, start, tile, size):
        self.nc, self.start, self.tile, self.size, self.at = nc, start, tile, size, 0

    def reset(self, at=0):
        self.at = at

    def take(self, shape, rounded=None):
        n = int(np.prod(shape[1:]))
        assert self.at + n <= self.size, (self.at + n, self.size)
        self.at += n
        if rounded:
            return self.view(rounded, self.at - n, shape)
        return self.shaped(self.tile[:, self.at - n:self.at], shape)

    def view(self, name, at, shape):
        n = int(np.prod(shape[1:]))
        tile = self.nc.alloc_sbuf_tensor_at(name, [P, n], F32R, offset=self.start + 4 * at)
        return self.shaped(tile[:, :], shape)

    @staticmethod
    def shaped(ap, shape):
        if len(shape) > 2:
            names = "abcdef"[:len(shape) - 1]
            ap = ap.rearrange("p (" + " ".join(names) + ") -> p " + " ".join(names),
                              **dict(zip(names, shape[1:])))
        return ap


class Unit:

    def __init__(self, i, c, m=2):
        self.i, self.c, self.m = i, c, m
        self.fixed = isinstance(i, int)

    @property
    def n(self):
        return self.c if self.fixed else self.i * self.m + self.c

    def div(self, k):
        return self.c // k if self.fixed else self.i * (self.m // k) + self.c // k

    @property
    def p(self):
        return self.c % 2

    def back(self, k):
        return Unit(self.i, self.c - k, self.m)

    def at(self, k, count):
        u = self.back(k)
        return u if not u.fixed or 0 <= u.n < count else None


def pipelined(eng, count, lag, step, unroll=2, peel=0):
    head = lag + 2
    head += (count - head) % unroll
    for t in range(head):
        step(Unit(0, t, unroll))
    with eng.Fori(0, (count - head - peel) // unroll) as i:
        for j in range(unroll):
            step(Unit(i, head + j, unroll))
    for t in range(count - peel, count + lag):
        step(Unit(0, t, unroll))


def done(eng, sem, u, per=1):
    if u.fixed and u.n < 0:
        return
    eng.wait_ge(sem, (u.n + 1) * per)


def landed(eng, sems, u, per=1):
    if u.fixed and u.n < 0:
        return
    eng.wait_ge(sems[u.p], (u.div(2) + 1) * (16 * per))


def decoder(nc, a, where, out):
    ctx = ExitStack()
    with ctx:
        def sb(name, shape, dt=F32):
            return ctx.enter_context(nc.sbuf_tensor(name, shape, dt))

        in_use = []

        def sem(name):
            in_use.append(nc.alloc_semaphore(name))
            return in_use[-1]

        def sem2(name):
            return [sem(name + "_0"), sem(name + "_1")]

        psum = ctx.enter_context(nc.psum_tensor("psum", [P, 8, 512], F32))

        def bank(k):
            return psum[:, k, :]

        def units(ap):
            return ap.rearrange("(u b) s d -> u s b d", b=UB)

        ZW = 512
        x2_d = nc.dram_tensor("x2_d", [B, S, D], F32, kind="Internal").ap()
        x4_d = nc.dram_tensor("x4_d", [B, S, D], F32, kind="Internal").ap()
        x5_d = nc.dram_tensor("x5_d", [B, S, D], F32, kind="Internal").ap()
        disp_d = nc.dram_tensor("disp_d", [SLOTS, D], F32, kind="Internal").ap()
        y_d = nc.dram_tensor("y_d", [SLOTS, D], F32, kind="Internal").ap()
        x_u, ctx_u, out_u = units(a["x"]), units(a["ctx_1024"]), units(out)
        x2_u, x4_u, x5_u = units(x2_d), units(x4_d), units(x5_d)

        n_const = a["constants"].shape[1]
        const = sb("const", [P, n_const])

        def table(name):
            at, n = where[name]
            return const[:, at:at + n]

        ident = table("ident")
        gate_w = sb("gate_w", [P, 2, NC_, P])
        w = {n: sb(n, [P, NC_, D]) for n in
             ("L0_xattn_Wq", "L0_xattn_Wk", "L0_xattn_Wv", "L1_attn_wq", "L1_attn_wk", "L1_attn_wv",
              "L1_attn_wo", "L1_xattn_Wq", "L1_xattn_Wk", "L1_xattn_Wv", "L1_xattn_Wo")}
        w_route = sb("w_route", [P, NC_, E0])
        w_hash = sb("w_hash", [P, NC_, PD])
        w_keys = sb("w_keys", [PD, NE1])
        VEC_ROWS = 10 + E0 * HID0 // P
        vec_rows = sb("vec_rows", [VEC_ROWS, P])
        vec = sb("vec", [P, VEC_ROWS])
        V_A, V_BIN, V_BA, V_BQ, V_BK, V_B1 = 0, 2, 4, 6, 8, 10
        hgate_b = sb("hgate_b", [P, 4])
        sp_tmp = sb("sp_tmp", [P, 3, NC_])
        ndecay = sb("ndecay", [P, NC_])
        kb_par = sb("kb_par", [P, 2, NC_])
        bv2_b = sb("bv2_b", [P, UB * D])
        bo_b = sb("bo_b", [P, D])
        b2_b = sb("b2_b", [P, E0, D])
        scale_b = sb("scale_b", [P, 1])
        ARENA_X, ARENA_Y = 23040, 14464
        arena_x = Arena(nc, -(-nc.sbuf_base // 32) * 32, sb("arena_x", [P, ARENA_X]), ARENA_X)
        arena_y = Arena(nc, -(-nc.sbuf_base // 32) * 32, sb("arena_y", [P, ARENA_Y]), ARENA_Y)
        mask_u8 = arena_y.take([P, B * S // 4])[0:1, :].bitcast(U8)
        mask_row = sb("mask_row", [1, B * S], BF16)
        ones_row = sb("ones_row", [1, P], BF16)
        ident_bf = sb("ident_bf", [P, P], BF16)
        causal_bf = sb("causal_bf", [P, P], BF16)
        zeros = sb("zeros", [P, ZW])
        wait_cell = sb("wait_cell", [1, 1])
        minus_half = sb("minus_half", [P, UB, 1])
        logits = sb("logits", [P, B, E0])
        gates = sb("gates", [P, TOP0, B])
        slot_g = sb("slot_g", [P, TOP0, B], I32)
        slot_s = sb("slot_s", [P, TOP0, B], I32)

        s_const, s_zero, s_prefill = sem("s_const"), sem("s_zero"), sem("s_prefill")
        s_vecT, s_vec, s_setup = sem("s_vecT"), sem("s_vec"), sem("s_setup")
        s_act_setup = sem("s_act_setup")

        s_pow = sem("s_pow")
        loads = [(const[:, :], a["constants"])]
        vec_src = [("L0_attn_a_param", 2), ("L0_attn_b_in", 2), ("L0_attn_b_a", 2),
                   ("L1_xattn_bq", 2), ("L1_xattn_bk", 2), ("L0_ffn_b1", E0 * HID0 // P)]
        at = 0
        for name, n in vec_src:
            v = a[name]
            if len(v.shape) == 2:
                v = v.rearrange("a b -> (a b)")
            loads.append((vec_rows[at:at + n, :], v.rearrange("(r p) -> r p", p=P)))
            at += n
        diag = []
        for g, name in enumerate(("L0_attn_w_in", "L0_attn_w_a")):
            for h in range(D // BW):
                c, r = divmod(h, P // BW)
                diag.append((gate_w[r * BW:(r + 1) * BW, g, c, r * BW:(r + 1) * BW], a[name][h]))
        for name in ("L0_xattn_Wq", "L0_xattn_Wk", "L0_xattn_Wv"):
            loads.append((w[name][:, :, :], a[name].rearrange("(c p) n -> p c n", p=P)))
        loads.append((w_route[:, :, :], a["L0_ffn_wg"].rearrange("(c p) n -> p c n", p=P)))
        N_EARLY = len(loads) + len(diag)
        late = []
        for name in ("L1_attn_wq", "L1_attn_wk", "L1_attn_wv"):
            late.append((w[name][:, :, :], a[name].rearrange("(c p) h n -> p c (h n)", p=P)))
        late.append((w["L1_attn_wo"][:, :, :], a["L1_attn_wo"].rearrange("h p n -> p h n")))
        for name in ("L1_xattn_Wq", "L1_xattn_Wk", "L1_xattn_Wv", "L1_xattn_Wo"):
            late.append((w[name][:, :, :], a[name].rearrange("(c p) n -> p c n", p=P)))
        late.append((w_hash[:, :, :], a["hash_t"].rearrange("(c p) n -> p c n", p=P)))
        late.append((w_keys[:, :], a["keys_t"]))
        for b in range(UB):
            late.append((bv2_b[:, b * D:(b + 1) * D],
                         a["L1_xattn_bv"].rearrange("(a n) -> a n", a=1).broadcast_to([P, D])))
        late.append((bo_b[:, :], a["L1_xattn_bo"].rearrange("(a n) -> a n", a=1).broadcast_to([P, D])))
        late.append((b2_b[:, :, :], a["L0_ffn_b2"].rearrange("(a e) n -> a e n", a=1).broadcast_to([P, E0, D])))
        late.append((scale_b[:, :], a["L1_ffn_scale"].rearrange("(a n) -> a n", a=1).broadcast_to([P, 1])))
        late.append((mask_u8[:, :], a["mask"].rearrange("(a b) s -> a (b s)", a=1)))
        s_late = sem("s_late")
        N_LATE = len(late)

        phases = {"sync": [], "tensor": [], "scalar": [], "vector": [], "gpsimd": []}

        def run_layer():
            with nc.Block() as block:
                @block.sync
                def _(eng):
                    for part in phases["sync"]:
                        part(eng)

                @block.tensor
                def _(eng):
                    for part in phases["tensor"]:
                        part(eng)

                @block.scalar
                def _(eng):
                    for part in phases["scalar"]:
                        part(eng)

                @block.vector
                def _(eng):
                    for part in phases["vector"]:
                        part(eng)

                @block.gpsimd
                def _(eng):
                    for part in phases["gpsimd"]:
                        part(eng)
            nc.clear_and_free_semaphores(list(in_use))
            nc.all_engine_barrier()
            in_use.clear()
            for parts in phases.values():
                parts.clear()

        def setup_sync(sp):
            for dst, src in loads:
                sp.dma_start(dst, src).then_inc(s_const, 16)
            sp.wait_ge(s_zero, 1)
            for dst, src in diag:
                sp.dma_start(dst, src).then_inc(s_const, 16)
            for dst, src in late:
                sp.dma_start(dst, src).then_inc(s_late, 16)

        def setup_pool(pool):
            nc.gpsimd.memset(gate_w[:, :, :, :], 0.0).then_inc(s_zero, 1)
            nc.gpsimd.memset(zeros[:, :], 0.0).then_inc(s_zero, 1)
            nc.gpsimd.memset(pool_cell[:, :], 0.0).then_inc(s_pow, 1)
            nc.gpsimd.memset(minus_half[:, :, :], -0.5).then_inc(s_pow, 1)
            pool.wait_ge(s_pow, 2)

        def setup_scalar(act):
            act.wait_ge(s_zero, 2)
            for k in range(SLOTS * D // (P * ZW)):
                n = P * ZW // D
                act.dma_start(disp_d[k * n:(k + 1) * n, :].rearrange("(p r) d -> p (r d)", p=P),
                              zeros[:, :]).then_inc(s_prefill, 16)
            act.wait_ge(s_vec, 1)
            nc.scalar.activation(sp_tmp[:, 0, :], vec[:, V_A:V_A + 2], ACT.Abs).then_inc(s_act_setup, 1)
            act.wait_ge(s_act_setup, 1)
            nc.scalar.activation(sp_tmp[:, 1, :], sp_tmp[:, 0, :], ACT.Exp, scale=-1.0).then_inc(s_act_setup, 1)
            act.wait_ge(s_act_setup, 2)
            nc.scalar.activation(sp_tmp[:, 2, :], sp_tmp[:, 1, :], ACT.Ln, bias=1.0).then_inc(s_act_setup, 1)

        def setup_tensor(pe):
            pe.wait_ge(s_const, 16 * N_EARLY)
            nc.tensor.transpose(bank(7)[:, 0:VEC_ROWS], vec_rows[:, :], ident[0:VEC_ROWS, 0:VEC_ROWS]).then_inc(s_vecT, 1)

        def setup_vector(dve):
            dve.wait_ge(s_vecT, 1)
            nc.vector.tensor_copy(vec[:, :], bank(7)[:, 0:VEC_ROWS]).then_inc(s_vec, 1)
            dve.wait_ge(s_vec, 1)
            nc.vector.tensor_scalar(hgate_b[:, :], vec[:, V_BIN:V_BIN + 4], 0.5, None, ALU.mult).then_inc(s_setup, 1)
            nc.vector.tensor_scalar(kb_par[:, 0, :], vec[:, V_BK:V_BK + 2], table("even_heads"), None,
                                    ALU.mult).then_inc(s_setup, 1)
            nc.vector.tensor_scalar(kb_par[:, 1, :], vec[:, V_BK:V_BK + 2], table("odd_heads"), None,
                                    ALU.mult).then_inc(s_setup, 1)
            nc.vector.tensor_scalar(ndecay[:, :], vec[:, V_A:V_A + 2], 0.0, MIN_DECAY, ALU.max,
                                    ALU.add).then_inc(s_setup, 1)
            nc.vector.tensor_copy(ident_bf[:, :], ident).then_inc(s_setup, 1)
            nc.vector.tensor_copy(causal_bf[:, :], table("causal")).then_inc(s_setup, 1)
            nc.vector.memset(ones_row[:, :], 1.0).then_inc(s_setup, 1)
            dve.wait_ge(s_act_setup, 3)
            dve.wait_ge(s_setup, 4)
            nc.vector.tensor_tensor(ndecay[:, :], ndecay[:, :], sp_tmp[:, 2, :], ALU.add).then_inc(s_setup, 1)
            dve.wait_ge(s_setup, 8)
            nc.vector.tensor_scalar(ndecay[:, :], ndecay[:, :], -0.5, None, ALU.mult).then_inc(s_setup, 1)
            dve.wait_ge(s_late, 16 * N_LATE)
            nc.vector.tensor_scalar(mask_row[:, :], mask_u8[:, :], -BIG, None, ALU.mult).then_inc(s_setup, 1)
        N_SETUP = 10

        phases["sync"].append(setup_sync)
        phases["gpsimd"].append(setup_pool)
        phases["scalar"].append(setup_scalar)
        phases["tensor"].append(setup_tensor)
        phases["vector"].append(setup_vector)

        def ln_stats(dve, u, src, stats, sems):
            s_st, s_ag, s_rs, s_out = sems
            for b in range(UB):
                ins = nc.vector.bn_stats(stats[:, b, 0:6], src[:, b, :])
            ins.then_inc(s_st, 1)
            dve.wait_ge(s_st, u.n * 2 + 1)
            nc.vector.memset(wait_cell[:, :], 0.0)
            for b in range(UB):
                ins = nc.vector.bn_aggr(stats[:, b, 6:8], stats[:, b, 0:6])
            ins.then_inc(s_st, 1)
            done(dve, s_st, u, 2)
            nc.vector.tensor_scalar(stats[:, :, 9:10], stats[:, :, 7:8], LN_EPS, None, ALU.add).then_inc(s_ag, 1)

        def ln_apply(dve, u, src, dst, stats, sems):
            s_st, s_ag, s_rs, s_out = sems
            done(dve, s_rs, u)
            for b in range(UB):
                ins = nc.vector.tensor_scalar(dst[:, b, :], src[:, b, :], stats[:, b, 6:7], stats[:, b, 8:9],
                                              ALU.subtract, ALU.mult)
            ins.then_inc(s_out, 1)

        def layer_norm(dve, u, src, dst, stats, sems):
            ln_stats(dve, u, src, stats, sems)
            ln_apply(dve, u, src, dst, stats, sems)

        def rstd(pool, u, stats, sems):
            s_st, s_ag, s_rs, s_out = sems
            done(pool, s_ag, u)
            nc.gpsimd.tensor_tensor(stats[:, :, 8:9], stats[:, :, 9:10], minus_half[:, :, :], ALU.pow).then_inc(s_rs, 1)

        def to_feature(dst, src):
            for c in range(NC_):
                for b in range(UB):
                    ins = nc.tensor.transpose(dst[:, c * T + b * S:c * T + (b + 1) * S],
                                              src[:, b, c * P:(c + 1) * P], ident)
            return ins

        def chunks(ap):
            return ap.rearrange("p (c t) -> p c t", c=NC_)

        def seqs(ap):
            return ap.rearrange("p (b d) -> p b d", b=UB)


        def low_part(dst, src, high):
            return nc.vector.tensor_tensor(dst, src, high.bitcast(F32), ALU.subtract)

        def matmul_split(dst, left, right, start, stop):
            for k, (a_, b_) in enumerate(((0, 0), (0, 1), (1, 0))):
                ins = nc.tensor.matmul(dst, left[a_], right[b_], start=start and k == 0, stop=stop and k == 2,
                                       skip_group_check=True)
            return ins

        def add(engine, part):
            phases[engine].append(part)

        pool_cell = sb("pool_cell", [1, 8])

        def carry(pool, k):
            nc.gpsimd.tensor_tensor(pool_cell[:, k:k + 1], pool_cell[:, 7:8], pool_cell[:, 7:8], ALU.add)

        A = {}
        for n in ("x", "cx"):
            A[n] = arena_x.take([P, 2, UB, D])
        for n in ("xF", "cF", "thx", "tha", "a", "ash", "m", "g", "pp", "w", "r1", "x1F", "qr", "kr", "x2F"):
            A[n] = arena_x.take([P, 2, NC_, T])
        A["rp"] = arena_x.take([P, NC_, T])
        A["t1"] = arena_x.take([P, NC_, T])
        A["t2"] = arena_x.take([P, NC_, T])
        for n in ("x1", "x2", "v"):
            A[n] = arena_x.take([P, 2, UB, D])
        A["r2"] = arena_x.take([P, UB, D])
        A["sc"] = arena_x.take([P, 2, UB, S])
        A_st1 = sb("A_st1", [P, UB, 10])
        A_st2 = sb("A_st2", [P, UB, 10])

        a_in = sem2("a_in")
        aT_x, aT_c, aT_r1, aT_x1, aT_x2 = (sem("aT_" + n) for n in ("x", "c", "r1", "x1", "x2"))
        a_gate, a_k, a_v, a_q, a_score, a_ret, a_logit = (
            sem("a_" + n) for n in ("gate", "k", "v", "q", "score", "ret", "logit"))
        a_xF, a_cF, a_thx, a_tha, a_dec, a_vs, a_x1F, a_x2F, a_lg = (
            sem("a_" + n) for n in ("xF", "cF", "thx", "tha", "dec", "vs", "x1F", "x2F", "lg"))
        a_sh, a_min, a_m1, a_m2, a_g1, a_g2, a_p, a_rp, a_w, a_s, a_h, a_r1 = (
            sem("a_" + n) for n in ("sh", "min", "m1", "m2", "g1", "g2", "p", "rp", "w", "s", "h", "r1"))
        a_qt, a_qr, a_kt, a_kr, a_sc, a_r2 = (sem("a_" + n) for n in ("qt", "qr", "kt", "kr", "sc", "r2"))
        ln1 = [sem("ln1_" + n) for n in ("st", "ag", "rs", "out")]
        ln2 = [sem("ln2_" + n) for n in ("st", "ag", "rs", "out")]
        a_x1, a_x2 = ln1[3], ln2[3]
        a_st = sem2("a_st")
        A_LAG = 3

        def a_sync(sp):
            def step(t):
                u = t.at(0, UNITS)
                if u:
                    done(sp, aT_x, u.back(2))
                    done(sp, aT_c, u.back(2))
                    sp.dma_start(A["x"][:, u.p, :, :], x_u[u.n]).then_inc(a_in[u.p], 16)
                    sp.dma_start(A["cx"][:, u.p, :, :], ctx_u[u.n]).then_inc(a_in[u.p], 16)
                u = t.at(3, UNITS)
                if u:
                    done(sp, a_x2, u)
                    sp.dma_start(x2_u[u.n], A["x2"][:, u.p, :, :]).then_inc(a_st[u.p], 16)
            pipelined(sp, UNITS, A_LAG, step)

        def a_tensor(pe):
            pe.wait_ge(s_vec, 1)

            def project(dst, name, src, par=None, odd=None):
                for m in range(NC_):
                    for c in range(NC_):
                        ws = w[name][:, c, m::2] if par else w[name][:, c, m * P:(m + 1) * P]
                        ins = nc.tensor.matmul(dst[:, m * T:(m + 1) * T], ws, src[:, c, :],
                                               start=(c == 0), stop=(c == NC_ - 1))
                return ins

            def step(t):
                u0, u1, u2, u3 = (t.at(k, UNITS) for k in range(4))
                if u0:
                    landed(pe, a_in, u0, 2)
                    done(pe, a_x1F, u0.back(2))
                    to_feature(bank(0), A["x"][:, u0.p]).then_inc(aT_x, 1)
                    done(pe, a_x2F, u0.back(4))
                    to_feature(bank(1), A["cx"][:, u0.p]).then_inc(aT_c, 1)
                if u3:
                    done(pe, a_x2, u3)
                    done(pe, a_cF, u0 or u3)
                    to_feature(bank(1), A["x2"][:, u3.p]).then_inc(aT_x2, 1)
                if u0:
                    done(pe, a_xF, u0)
                    done(pe, a_dec, u0.back(1))
                    done(pe, a_thx, u0.back(1))
                    done(pe, a_tha, u0.back(1))
                    for g in range(2):
                        for c in range(NC_):
                            ins = nc.tensor.matmul(bank(2 + g)[:, c * T:(c + 1) * T], gate_w[:, g, c, :],
                                                   A["xF"][:, u0.p, c, :], start=True, stop=True)
                    ins.then_inc(a_gate, 1)
                    done(pe, a_cF, u0)
                    done(pe, a_kt, u0.back(1))
                    project(bank(5), "L0_xattn_Wk", A["cF"][:, u0.p], par=True).then_inc(a_k, 1)
                if u1:
                    done(pe, a_r1, u1)
                    done(pe, a_qt, u1.back(1))
                    for b in range(UB):
                        for c in range(NC_):
                            ins = nc.tensor.transpose(bank(4)[:, b * D + c * P:b * D + (c + 1) * P],
                                                      A["r1"][:, u1.p, c, b * S:(b + 1) * S], ident)
                    ins.then_inc(aT_r1, 1)
                if u2:
                    done(pe, a_qr, u2)
                    done(pe, a_kr, u2)
                    done(pe, a_lg, u2.back(2))
                    for b in range(UB):
                        for c in range(NC_):
                            ins = nc.tensor.matmul(bank(7)[:, b * S:(b + 1) * S],
                                                   A["kr"][:, u2.p, c, b * S:(b + 1) * S],
                                                   A["qr"][:, u2.p, c, b * S:(b + 1) * S],
                                                   start=(c == 0), stop=(c == NC_ - 1))
                    ins.then_inc(a_score, 1)
                if u2:
                    done(pe, a_sc, u2)
                    done(pe, a_vs, u1 or u2)
                    for b in range(UB):
                        ins = nc.tensor.matmul(bank(6)[:, b * D:(b + 1) * D], A["sc"][:, u2.p, b, :],
                                               A["v"][:, u2.p, b, :], start=True, stop=True)
                    ins.then_inc(a_ret, 1)
                if u1:
                    done(pe, a_x1, u1)
                    done(pe, a_xF, u0 or u1)
                    to_feature(bank(0), A["x1"][:, u1.p]).then_inc(aT_x1, 1)
                if u0:
                    done(pe, a_r2, u0.back(2))
                    for b in range(UB):
                        for c in range(NC_):
                            ins = nc.tensor.matmul(bank(6)[:, b * D:(b + 1) * D],
                                                   A["cF"][:, u0.p, c, b * S:(b + 1) * S],
                                                   w["L0_xattn_Wv"][:, c, :], start=(c == 0), stop=(c == NC_ - 1))
                    ins.then_inc(a_v, 1)
                if u1:
                    done(pe, a_x1F, u1)
                    project(bank(4), "L0_xattn_Wq", A["x1F"][:, u1.p], par=True).then_inc(a_q, 1)
                if u3:
                    done(pe, a_x2F, u3)
                    done(pe, a_sc, u2 or u3)
                    for b in range(UB):
                        for c in range(NC_):
                            ins = nc.tensor.matmul(bank(7)[:, 256 + b * E0:256 + (b + 1) * E0],
                                                   A["x2F"][:, u3.p, c, b * S:(b + 1) * S], w_route[:, c, :],
                                                   start=(c == 0), stop=(c == NC_ - 1))
                    ins.then_inc(a_logit, 1)
            pipelined(pe, UNITS, A_LAG, step)

        def a_scalar(act):
            act.wait_ge(s_setup, 9)

            def step(t):
                u0, u1, u3 = t.at(0, UNITS), t.at(1, UNITS), t.at(3, UNITS)
                if u0:
                    done(act, aT_x, u0)
                    done(act, a_r1, u0.back(2))
                    nc.scalar.activation(A["xF"][:, u0.p], chunks(bank(0)), ACT.Copy).then_inc(a_xF, 1)
                    done(act, aT_c, u0)
                    done(act, a_v, u0.back(2))
                    nc.scalar.activation(A["cF"][:, u0.p], chunks(bank(1)), ACT.Copy).then_inc(a_cF, 1)
                if u3:
                    done(act, aT_x2, u3)
                    done(act, a_logit, u3.back(2))
                    nc.scalar.activation(A["x2F"][:, u3.p], chunks(bank(1)), ACT.Copy).then_inc(a_x2F, 1)
                if u0:
                    done(act, a_gate, u0)
                    done(act, a_g1, u0.back(2))
                    for c in range(NC_):
                        ins = nc.scalar.activation(A["tha"][:, u0.p, c, :], bank(3)[:, c * T:(c + 1) * T], ACT.Tanh,
                                                   bias=hgate_b[:, 2 + c:3 + c], scale=0.5)
                    ins.then_inc(a_tha, 1)
                    for c in range(NC_):
                        ins = nc.scalar.activation(A["thx"][:, u0.p, c, :], bank(2)[:, c * T:(c + 1) * T], ACT.Tanh,
                                                   bias=hgate_b[:, c:c + 1], scale=0.5)
                    ins.then_inc(a_thx, 1)
                    done(act, a_tha, u0)
                    done(act, a_m1, u0.back(2))
                    for c in range(NC_):
                        ins = nc.scalar.activation(A["a"][:, u0.p, c, :], A["tha"][:, u0.p, c, :], ACT.Exp,
                                                   bias=ndecay[:, c:c + 1], scale=ndecay[:, c:c + 1])
                    ins.then_inc(a_dec, 1)
                if u1:
                    done(act, aT_x1, u1)
                    done(act, a_q, u1.back(2))
                    nc.scalar.activation(A["x1F"][:, u1.p], chunks(bank(0)), ACT.Copy).then_inc(a_x1F, 1)
                if u0:
                    done(act, a_v, u0)
                    done(act, a_ret, u0.back(2))
                    nc.scalar.activation(A["v"][:, u0.p], seqs(bank(6)), ACT.Copy).then_inc(a_vs, 1)
                if u3:
                    done(act, a_logit, u3)
                    nc.scalar.activation(logits[:, bass.ds(u3.n * UB, UB), :],
                                         bank(7)[:, 256:256 + UB * E0].rearrange("p (b e) -> p b e", e=E0),
                                         ACT.Copy).then_inc(a_lg, 1)
                if u0:
                    done(act, a_m2, u0)
                    nc.scalar.activation(A["m"][:, u0.p], A["m"][:, u0.p], ACT.Sqrt).then_inc(a_rt, 1)
            pipelined(act, UNITS, A_LAG, step)

        def a_vector(dve):
            def bc(name, n):
                return table(name)[:, None, :].broadcast_to([P, n, S])

            def xpos(u, src, cos, sin, dst, s_t, s_r):
                t1, t2 = A["t1"], A["t2"]
                q = src.rearrange("p (c b s) -> p c b s", c=NC_, b=UB)
                nc.vector.tensor_tensor(t1[:, :, :].rearrange("p c (b s) -> p (c b) s", b=UB),
                                        src.rearrange("p (n s) -> p n s", s=S), bc(cos, NC_ * UB), ALU.mult)
                for c in range(NC_):
                    ins = nc.vector.tensor_tensor(t2[:, 1 - c, :].rearrange("p (b s) -> p b s", b=UB), q[:, c],
                                                  bc(sin, UB), ALU.mult)
                ins.then_inc(s_t, 1)
                done(dve, s_t, u)
                nc.vector.tensor_tensor(dst[:, 0, :], t1[:, 0, :], t2[:, 0, :], ALU.subtract)
                nc.vector.tensor_tensor(dst[:, 1, :], t1[:, 1, :], t2[:, 1, :], ALU.add).then_inc(s_r, 1)

            def step(t):
                u0, u1, u2 = t.at(0, UNITS), t.at(1, UNITS), t.at(2, UNITS)
                if u0:
                    p = u0.p
                    a4 = A["a"][:, p].rearrange("p c (b s) -> p (c b) s", b=UB)
                    sh4 = A["ash"][:, p].rearrange("p c (b s) -> p (c b) s", b=UB)
                    flat = {n: A[n][:, p].rearrange("p c t -> p (c t)") for n in ("ash", "pp", "w")}
                    done(dve, a_k, u0)
                    done(dve, a_score, u0.back(2))
                    xpos(u0, bank(5), "xpos_k_cos", "xpos_k_sin", A["kr"][:, p], a_kt, a_kr)
                if u1:
                    done(dve, aT_r1, u1)
                    ln_stats(dve, u1, seqs(bank(4)), A_st1, ln1)
                if u2:
                    done(dve, a_score, u2)
                    done(dve, a_ret, u2.back(2))
                    nc.vector.tensor_tensor(A["sc"][:, u2.p], bank(7)[:, 0:UB * S].rearrange("p (b s) -> p b s", b=UB),
                                            bc("decay_t", UB), ALU.mult).then_inc(a_sc, 1)
                if u1:
                    done(dve, aT_x1, u1.back(2))
                    done(dve, a_r2, u1.back(2))
                    ln_apply(dve, u1, seqs(bank(4)), A["x1"][:, u1.p], A_st1, ln1)
                if u2:
                    done(dve, a_ret, u2)
                    done(dve, a_x2, u2.back(1))
                    nc.vector.tensor_tensor(A["r2"][:, :, :], seqs(bank(6)), A["x1"][:, u2.p], ALU.add).then_inc(a_r2, 1)
                    done(dve, a_r2, u2)
                    ln_stats(dve, u2, A["r2"], A_st2, ln2)
                if u0:
                    done(dve, a_dec, u0)
                    done(dve, a_thx, u0)
                    nc.vector.tensor_scalar(sh4[:, :, 1:S], a4[:, :, 0:S - 1], 1.0 - A_EPS, None,
                                            ALU.min).then_inc(a_sh, 1)
                    done(dve, a_sh, u0)
                    nc.vector.tensor_scalar(A["a"][:, p], A["a"][:, p], 1.0 - A_EPS, None, ALU.min).then_inc(a_min, 1)
                    nc.vector.scalar_tensor_tensor(A["g"][:, p], A["thx"][:, p], 1.0, A["xF"][:, p], ALU.add,
                                                   ALU.mult).then_inc(a_g1, 1)
                    done(dve, a_sh, u0)
                    nc.vector.tensor_tensor_scan(flat["pp"], flat["ash"], table("floor"), 1.0, ALU.mult,
                                                 ALU.max).then_inc(a_p, 1)
                    done(dve, a_min, u0)
                    nc.vector.scalar_tensor_tensor(A["m"][:, p], A["a"][:, p], -0.25, A["a"][:, p], ALU.mult,
                                                   ALU.mult).then_inc(a_m1, 1)
                    done(dve, a_p, u0)
                    nc.vector.reciprocal(A["rp"][:, :, :], A["pp"][:, p]).then_inc(a_rp, 1)
                    done(dve, a_m1, u0)
                    nc.vector.tensor_scalar(A["m"][:, p], A["m"][:, p], 0.25, 0.25 * A_EPS, ALU.add,
                                            ALU.max).then_inc(a_m2, 1)
                if u2:
                    done(dve, aT_x2, u2.back(2))
                    landed(dve, a_st, u2.back(2))
                    ln_apply(dve, u2, A["r2"], A["x2"][:, u2.p], A_st2, ln2)
                if u1:
                    done(dve, a_q, u1)
                    done(dve, a_kr, u0 or u1)
                    xpos(u1, bank(4), "xpos_q_cos", "xpos_q_sin", A["qr"][:, u1.p], a_qt, a_qr)
                if u0:
                    done(dve, a_rt, u0)
                    done(dve, a_g1, u0)
                    nc.vector.tensor_tensor(A["g"][:, p], A["m"][:, p], A["g"][:, p], ALU.mult).then_inc(a_g2, 1)
                    done(dve, a_g2, u0)
                    done(dve, a_rp, u0)
                    nc.vector.scalar_tensor_tensor(A["w"][:, p], A["g"][:, p], SCAN_EPS, A["rp"][:, :, :], ALU.add,
                                                   ALU.mult).then_inc(a_w, 1)
                    done(dve, a_w, u0)
                    nc.vector.tensor_tensor_scan(flat["w"], table("keep"), flat["w"], 0.0, ALU.mult,
                                                 ALU.add).then_inc(a_s, 1)
                    done(dve, a_s, u0)
                    nc.vector.tensor_tensor(A["m"][:, p], A["pp"][:, p], A["w"][:, p], ALU.mult).then_inc(a_h, 1)
                    done(dve, a_h, u0)
                    nc.vector.tensor_tensor(A["r1"][:, p], A["m"][:, p], A["xF"][:, p], ALU.add).then_inc(a_r1, 1)
            nc.vector.memset(A["ash"][:, :, :, :], 0.0).then_inc(a_sh0, 1)
            dve.wait_ge(a_sh0, 1)
            pipelined(dve, UNITS, A_LAG, step)
        a_sh0, a_rt = sem("a_sh0"), sem("a_rt")

        def a_gpsimd(pool):
            def step(t):
                u = t.at(1, UNITS)
                if u:
                    rstd(pool, u, A_st1, ln1)
                u = t.at(2, UNITS)
                if u:
                    rstd(pool, u, A_st2, ln2)
            pipelined(pool, UNITS, A_LAG, step)

        phases["gpsimd"].append(a_gpsimd)

        phases["sync"].append(a_sync)
        phases["tensor"].append(a_tensor)
        phases["scalar"].append(a_scalar)
        phases["vector"].append(a_vector)
        KB = TOP0 * B
        R = {}
        arena_x.reset()
        for n in ("eq", "rk", "l2"):
            R[n] = arena_x.take([P, B, E0])
        R["oh"] = arena_x.take([P, TOP0, B, E0])
        R["tot"] = arena_x.take([P, E0, KB])
        R["inc"] = arena_x.take([P, E0, KB])
        R["pos"] = arena_x.take([P, KB, E0])
        R["sel"] = arena_x.take([P, KB, E0])
        for n in ("m1", "m2", "mr", "ex"):
            R[n] = arena_x.take([P, B])
        for n in ("posk", "basek", "valid", "slot", "slot2"):
            R[n] = arena_x.take([P, TOP0, B])
        R["x"] = arena_x.take([P, 2, UB, D])
        R["idx"] = arena_x.take([P, 2, TOP0, UB]).bitcast(I32)

        r_v = sem("r_v")
        r_ex, r_rank, r_slots = sem("r_ex"), sem("r_rank"), sem("r_slots")
        r_in, r_idx, r_sc = sem2("r_in"), sem("r_idx"), sem2("r_sc")
        r_go = sem("r_go")
        RV_GAP, RV_ONEHOT = 8, 9
        per_parity = UNITS // 2

        def r_vector(dve):
            k = [0]

            def then(ins):
                k[0] += 1
                ins.then_inc(r_v, 1)
                dve.wait_ge(r_v, k[0])

            def over_e(ap, n=B):
                return ap[:, :, None].broadcast_to([P, n, E0])

            def first_max(src, m, oh):
                then(nc.vector.tensor_reduce(m, src, AX, ALU.max))
                then(nc.vector.tensor_tensor(R["eq"], src, over_e(m), ALU.is_equal))
                then(nc.vector.tensor_tensor(R["rk"], R["eq"], table("rank")[:, None, :].broadcast_to([P, B, E0]),
                                             ALU.mult))
                then(nc.vector.tensor_reduce(R["mr"], R["rk"], AX, ALU.max))
                then(nc.vector.tensor_tensor(oh, R["rk"], over_e(R["mr"]), ALU.is_equal))

            dve.wait_ge(a_lg, UNITS)
            dve.wait_ge(aT_x2, UNITS)
            first_max(logits[:, :, :], R["m1"], R["oh"][:, 0])
            then(nc.vector.scalar_tensor_tensor(R["l2"], R["oh"][:, 0], -BIG, logits[:, :, :], ALU.mult, ALU.add))
            first_max(R["l2"], R["m2"], R["oh"][:, 1])
            then(nc.vector.tensor_tensor(R["m2"], R["m2"], R["m1"], ALU.subtract))
            k_gap = k[0]
            dve.wait_ge(r_ex, 1)
            then(nc.vector.tensor_scalar(R["m1"], R["ex"], 1.0, None, ALU.add))
            then(nc.vector.reciprocal(gates[:, 0, :], R["m1"]))
            then(nc.vector.tensor_tensor(gates[:, 1, :], gates[:, 0, :], R["ex"], ALU.mult))
            dve.wait_ge(r_rank, 1)
            then(nc.vector.tensor_copy(R["tot"], bank(1).rearrange("p (k e) -> p e k", e=E0)))
            tot, inc = (R[n].rearrange("p e k -> p (e k)") for n in ("tot", "inc"))
            then(nc.vector.tensor_tensor_scan(inc, table("keep_seg"), tot, 0.0, ALU.mult, ALU.add))
            then(nc.vector.tensor_tensor(tot, inc, tot, ALU.subtract))
            then(nc.vector.tensor_tensor(R["pos"], bank(0).rearrange("p (k e) -> p k e", e=E0),
                                         R["tot"].rearrange("p e k -> p k e"), ALU.add))
            oh = R["oh"].rearrange("p c b e -> p (c b) e")
            flat = {n: R[n].rearrange("p c b -> p (c b)") for n in ("posk", "basek", "valid", "slot", "slot2")}
            then(nc.vector.tensor_tensor(R["sel"], R["pos"], oh, ALU.mult))
            then(nc.vector.tensor_reduce(flat["posk"], R["sel"], AX, ALU.add))
            then(nc.vector.tensor_tensor(R["sel"], oh, table("base")[:, None, :].broadcast_to([P, KB, E0]), ALU.mult))
            then(nc.vector.tensor_reduce(flat["basek"], R["sel"], AX, ALU.add))
            then(nc.vector.tensor_scalar(flat["valid"], flat["posk"], float(CAP), None, ALU.is_lt))
            then(nc.vector.tensor_tensor(gates[:, :, :], gates[:, :, :], R["valid"], ALU.mult))
            then(nc.vector.tensor_tensor(flat["slot"], flat["posk"], flat["valid"], ALU.mult))
            then(nc.vector.tensor_tensor(flat["slot"], flat["slot"], flat["basek"], ALU.add))
            then(nc.vector.tensor_copy(slot_g[:, :, :], R["slot"]))
            then(nc.vector.tensor_scalar(flat["slot2"], flat["valid"], -4.0 * SLOTS, 4.0 * SLOTS, ALU.mult, ALU.add))
            then(nc.vector.tensor_tensor(flat["slot2"], flat["slot2"], flat["slot"], ALU.add))
            nc.vector.tensor_copy(slot_s[:, :, :], R["slot2"]).then_inc(r_slots, 1)
            return k_gap

        def r_scalar(act):
            act.wait_ge(r_v, 12)
            nc.scalar.activation(R["ex"], R["m2"], ACT.Exp).then_inc(r_ex, 1)

        def r_tensor(pe):
            pe.wait_ge(r_v, 11)
            pe.wait_ge(a_x1F, UNITS)
            pe.wait_ge(a_x2F, UNITS)
            oh = R["oh"].rearrange("p c b e -> p (c b e)")
            nc.tensor.matmul(bank(0), table("before"), oh, start=True, stop=True)
            nc.tensor.matmul(bank(1), table("ones"), oh, start=True, stop=True).then_inc(r_rank, 1)

        def r_sync(sp):
            sp.wait_ge(a_st[0], 16 * per_parity)
            sp.wait_ge(a_st[1], 16 * per_parity)
            sp.wait_ge(a_r1, UNITS)
            sp.wait_ge(a_score, UNITS)

            def step(t):
                if not (t.fixed and t.n < 2):
                    landed(sp, r_sc, t.back(2), 4)
                sp.dma_start(R["x"][:, t.p], x2_u[t.n]).then_inc(r_in[t.p], 16)
            pipelined(sp, UNITS, 0, step)

        def r_gpsimd(pool):
            pool.wait_ge(s_prefill, 16 * (SLOTS * D // (P * ZW)))
            pool.wait_ge(r_slots, 1)

            def step(t):
                landed(pool, r_in, t)
                landed(pool, r_sc, t.back(2), 4)
                carry(pool, 0)
                nc.gpsimd.tensor_copy(R["idx"][:, t.p], slot_s[:, :, bass.ds(t.n * UB, UB)]).then_inc(r_idx, 1)
                done(pool, r_idx, t)
                carry(pool, 1)
                for c in range(TOP0):
                    for b in range(UB):
                        nc.gpsimd.indirect_dma_start(
                            out=disp_d, out_offset=bass.IndirectOffsetOnAxis(ap=R["idx"][:, t.p, c, b:b + 1], axis=0),
                            in_=R["x"][:, t.p, b, :], in_offset=None, bounds_check=SLOTS - 1,
                            oob_is_err=False).then_inc(r_sc[t.p], 16)
            pipelined(pool, UNITS, 0, step)

        add("vector", r_vector)
        add("scalar", r_scalar)
        add("tensor", r_tensor)
        add("sync", r_sync)
        add("gpsimd", r_gpsimd)

        MT = 512
        MS = MT // P
        TILES = SLOTS // MT
        HC = HID0 // P
        M = {}
        arena_y.reset()
        arena_x.reset()
        M["x"] = arena_x.take([P, 2, MS, D])
        M["y"] = arena_x.take([P, 2, MS, D])
        M["hr"] = arena_x.take([P, 4, MT])
        M["xF"] = arena_x.take([P, 2, 2, NC_, MT], "m_xF_parts")
        M["h"] = arena_x.take([P, 2, HC, MT], "m_h_parts")
        WN = NC_ * HID0
        M["w"] = arena_y.take([P, 2, 2, WN])
        M["w_high"] = arena_y.view("m_w_high", 0, [P, 2, 2, WN])
        M["w1_low"] = arena_y.take([P, 2, WN], "m_w1_low")
        M["w2_low"] = arena_x.take([P, 2, WN], "m_w2_low")
        M["piece"] = arena_y.take([P, WN // 4], "m_piece")
        b1_e = sb("b1_e", [P, 2, HC])
        m_w, m_b1 = sem2("m_w"), sem("m_b1")
        m_in, m_T, m_xh, m_xF = sem2("m_in"), sem("m_T"), sem("m_xh"), sem("m_xF")
        m_hp, m_hs, m_hh, m_hl, m_yp, m_y = (sem("m_" + n) for n in ("hp", "hs", "hh", "hl", "yp", "y"))
        m_wa, m_wb, m_ws = sem("m_wa"), sem("m_wb"), sem("m_ws")
        m_st = sem2("m_st")
        disp_t = disp_d.rearrange("(n q p) d -> n p q d", p=P, q=MS)
        y_t = y_d.rearrange("(n q p) d -> n p q d", p=P, q=MS)
        w1_e = a["L0_ffn_w1"].rearrange("e (c p) h -> e p c h", p=P)
        w2_e = a["L0_ffn_w2"].rearrange("e (c p) d -> e p c d", p=P)
        PIECES, PW = 4, WN // 4

        def m_weights(sp, v):
            buf = (v.c // 2) % 2
            sp.dma_start(M["w"][:, buf, 0].rearrange("p (c h) -> p c h", c=NC_), w1_e[v.div(2)]).then_inc(m_w[buf], 16)
            sp.dma_start(M["w"][:, buf, 1].rearrange("p (c d) -> p c d", c=HC), w2_e[v.div(2)]).then_inc(m_w[buf], 16)

        def m_sync(sp):
            m_weights(sp, Unit(0, 0))
            m_weights(sp, Unit(0, 2))
            for k in range(2):
                sp.wait_ge(r_sc[k], 16 * 4 * per_parity)

            def step(t):
                u = t.at(0, TILES)
                if u and not (u.fixed and u.n >= TILES):
                    done(sp, m_T, u.back(2))
                    sp.dma_start(M["x"][:, u.p], disp_t[u.n]).then_inc(m_in[u.p], 16)
                v = t.back(-2)
                if t.c % 2 == 0 and not (t.fixed and not 2 <= t.n < TILES - 2):
                    done(sp, m_yp, t.back(1))
                    m_weights(sp, v)
                u = t.at(2, TILES)
                if u:
                    done(sp, m_y, u, 2)
                    sp.dma_start(y_t[u.n], M["y"][:, u.p]).then_inc(m_st[u.p], 16)
            pipelined(sp, TILES, 2, step, unroll=4, peel=4)

        def m_tensor(pe):
            pe.wait_ge(r_slots, 1)
            for s in (a_dec, a_thx, a_qr, a_kr, a_r2, a_sc, a_lg):
                pe.wait_ge(s, UNITS)

            def step(t):
                u = t.at(1, TILES)
                if u:
                    wb = (u.c // 2) % 2
                    w1 = [x.rearrange("p (c h) -> p c h", c=NC_) for x in (M["w_high"][:, wb, 0], M["w1_low"][:, wb])]
                    w2 = [x.rearrange("p (c d) -> p c d", c=HC) for x in (M["w_high"][:, wb, 1], M["w2_low"][:, wb])]
                    pe.wait_ge(m_ws, (u.div(2) + 1) * 2 * PIECES)
                    done(pe, m_xF, u, 2)
                    for m in range(HC):
                        if m >= 4:
                            pe.wait_ge(m_hh, u.n * HC + m - 3)
                        else:
                            done(pe, m_hh, u.back(1), HC)
                        for c in range(NC_):
                            ins = matmul_split(bank(2 + m % 4), [x[:, c, m * P:(m + 1) * P] for x in w1],
                                               [M["xF"][:, u.p, k, c, :] for k in range(2)], c == 0, c == NC_ - 1)
                        ins.then_inc(m_hp, 1)
                u0 = t.at(0, TILES)
                if u0:
                    landed(pe, m_in, u0)
                    done(pe, m_xF, u0.back(1), 2)
                    for c in range(NC_):
                        for q in range(MS):
                            ins = nc.tensor.transpose(bank(c)[:, q * P:(q + 1) * P],
                                                      M["x"][:, u0.p, q, c * P:(c + 1) * P], ident)
                    ins.then_inc(m_T, 1)
                if u:
                    done(pe, m_y, u.back(1), 2)
                    for m in range(HC):
                        pe.wait_ge(m_hl, u.n * HC + (m + 1))
                        for q in range(MS):
                            ins = matmul_split(bank(6 + q // 2)[:, (q % 2) * D:(q % 2 + 1) * D],
                                               [M["h"][:, k, m, q * P:(q + 1) * P] for k in range(2)],
                                               [x[:, m, :] for x in w2], m == 0 and q % 2 == 0, m == HC - 1)
                    ins.then_inc(m_yp, 1)
            pipelined(pe, TILES, 1, step, unroll=4, peel=4)

        def m_scalar(act):
            def step(t):
                u = t.at(1, TILES)
                if u:
                    if u.c % 2 == 0:
                        act.wait_ge(m_b1, u.div(2) + 1)
                    for m in range(HC):
                        if m >= 4:
                            act.wait_ge(m_hl, u.n * HC + m - 3)
                        else:
                            done(act, m_hl, u.back(1), HC)
                        act.wait_ge(m_hp, u.n * HC + (m + 1))
                        nc.scalar.activation(M["hr"][:, m % 4, :], bank(2 + m % 4), ACT.Relu,
                                             bias=b1_e[:, (u.c // 2) % 2, m:m + 1]).then_inc(m_hs, 1)
                        if m == 0:
                            done(act, m_yp, u.back(1))
                        nc.scalar.activation(M["h"][:, 0, m, :], bank(2 + m % 4), ACT.Relu,
                                             bias=b1_e[:, (u.c // 2) % 2, m:m + 1]).then_inc(m_hh, 1)
                u0 = t.at(0, TILES)
                if u0:
                    done(act, m_T, u0)
                    done(act, m_hp, u0.back(2), HC)
                    for c in range(NC_):
                        nc.scalar.activation(M["xF"][:, u0.p, 0, c, :], bank(c), ACT.Copy).then_inc(m_xh, 1)
            pipelined(act, TILES, 1, step, unroll=4, peel=4)

        def m_vector(dve):
            def split_piece(v, which, k):
                buf, n = (v.c // 2) % 2, v.div(2) * (2 * PIECES) + (which * PIECES + k)
                at = slice(k * PW, (k + 1) * PW)
                low = (M["w1_low"], M["w2_low"])[which][:, buf, at]
                if not (v.fixed and n == 0):
                    dve.wait_ge(m_ws, n)
                nc.vector.tensor_copy(M["piece"], M["w"][:, buf, which, at]).then_inc(m_wa, 1)
                dve.wait_ge(m_wa, n + 1)
                low_part(low, M["w"][:, buf, which, at], M["piece"]).then_inc(m_wb, 1)
                dve.wait_ge(m_wb, n + 1)
                nc.vector.tensor_copy(M["w_high"][:, buf, which, at], M["piece"].bitcast(F32)).then_inc(m_ws, 1)

            def step(t):
                u = t.at(1, TILES)
                if u:
                    v = u.back(-2)
                    more = not (v.fixed and v.n >= TILES)
                    if u.c % 2 == 0:
                        done(dve, m_hs, u.back(3), HC)
                        nc.vector.tensor_scalar(b1_e[:, (u.c // 2) % 2, :],
                                                vec[:, bass.ds(u.div(2) * HC + V_B1, HC)], 0.0, None,
                                                ALU.add).then_inc(m_b1, 1)
                    for m in range(HC):
                        if m == 0:
                            done(dve, m_yp, u.back(1))
                        dve.wait_ge(m_hh, u.n * HC + (m + 1))
                        low_part(M["h"][:, 1, m, :], M["hr"][:, m % 4, :], M["h"][:, 0, m, :]).then_inc(m_hl, 1)
                        if more and m % 2 == 1:
                            if m == 1:
                                dve.wait_ge(m_w[(v.c // 2) % 2], (v.div(4) + 1) * 32)
                            split_piece(v, u.c % 2, m // 2)
                u0 = t.at(0, TILES)
                if u0:
                    done(dve, m_hp, u0.back(2), HC)
                    for c in range(NC_):
                        dve.wait_ge(m_xh, u0.n * NC_ + (c + 1))
                        low_part(M["xF"][:, u0.p, 1, c, :], bank(c), M["xF"][:, u0.p, 0, c, :]).then_inc(m_xF, 1)
                if u:
                    done(dve, m_yp, u)
                    landed(dve, m_st, u.back(2))
                    for k in range(2):
                        nc.vector.tensor_tensor(M["y"][:, u.p, 2 * k:2 * k + 2, :], seqs(bank(6 + k)),
                                                b2_b[:, bass.ds(u.div(2), 1), :].broadcast_to([P, 2, D]),
                                                ALU.add).then_inc(m_y, 1)
            dve.wait_ge(m_w[0], 32)
            for which in range(2):
                for k in range(PIECES):
                    split_piece(Unit(0, 0), which, k)
            pipelined(dve, TILES, 1, step, unroll=4, peel=4)

        add("sync", m_sync)
        add("tensor", m_tensor)
        add("scalar", m_scalar)
        add("vector", m_vector)
        def m_end(sp):
            for k in range(2):
                sp.wait_ge(m_st[k], 16 * (TILES // 2))

        add("sync", m_end)
        run_layer()

        arena_y.reset()
        C = {}
        for n in ("x2", "v", "x4"):
            C[n] = arena_y.take([P, 2, UB, D])
        C["x3"] = arena_y.take([P, 4, UB, D])
        C["y"] = arena_y.take([P, 2, TOP0, UB, D])
        C["x3F"] = arena_y.take([P, NC_, T])
        for n in ("q", "k"):
            C[n] = arena_y.take([P, H1, T])
        C["t2q"] = arena_y.take([P, H1, T])
        C["t2k"] = C["t2q"]
        C["e"] = arena_y.take([P, 2, UB * H1, S])
        C["pT"] = arena_y.take([P, UB * H1, S])
        C["oF"] = arena_y.take([P, H1, T])
        C["r"] = arena_y.take([P, UB, D])
        C["r4"] = arena_y.take([P, UB, D])
        C["mx"] = arena_y.take([P, UB * H1])
        C["sum"] = arena_y.take([P, UB * H1])
        C["rec"] = arena_y.take([P, UB * H1])
        c_idx_t = sb("c_idx_t", [P, 2, TOP0, UB], I32)
        C_st3, C_st4 = sb("C_st3", [P, UB, 10]), sb("C_st4", [P, UB, 10])
        c_in, c_y, c_st = sem2("c_in"), sem2("c_y"), sem2("c_st")
        c_idx, c_mix, c_x3T, c_q, c_k, c_v, c_S, c_pT, c_o, c_wo = (
            sem("c_" + n) for n in ("idx", "mix", "x3T", "q", "k", "v", "S", "pT", "o", "wo"))
        c_x3F, c_q2, c_k2, c_vs, c_ex, c_pTs, c_os = (
            sem("c_" + n) for n in ("x3F", "q2", "k2", "vs", "ex", "pTs", "os"))
        c_qt, c_qr, c_kt, c_kr, c_mx, c_sub, c_sum, c_p, c_r4 = (
            sem("c_" + n) for n in ("qt", "qr", "kt", "kr", "mx", "sub", "sum", "p", "r4"))
        ln3 = [sem("ln3_" + n) for n in ("st", "ag", "rs", "out")]
        ln4 = [sem("ln4_" + n) for n in ("st", "ag", "rs", "out")]
        c_x3, c_x4 = ln3[3], ln4[3]
        C_LAG = 3

        def c_sync(sp):

            def step(t):
                u = t.at(0, UNITS)
                if u:
                    done(sp, c_mix, u.back(2), 2)
                    sp.dma_start(C["x2"][:, u.p], x2_u[u.n]).then_inc(c_in[u.p], 16)
                u = t.at(3, UNITS)
                if u:
                    done(sp, c_x4, u)
                    sp.dma_start(x4_u[u.n], C["x4"][:, u.p]).then_inc(c_st[u.p], 16)
            pipelined(sp, UNITS, C_LAG, step, unroll=4)

        def c_gpsimd(pool):

            def step(t):
                u = t.at(0, UNITS)
                if u:
                    landed(pool, c_y, u.back(2), 4)
                    nc.gpsimd.tensor_copy(c_idx_t[:, u.p], slot_g[:, :, bass.ds(u.n * UB, UB)]).then_inc(c_idx, 1)
                    done(pool, c_idx, u)
                    carry(pool, 2)
                    done(pool, c_mix, u.back(2), 2)
                    carry(pool, 3)
                    for k in range(TOP0):
                        for b in range(UB):
                            nc.gpsimd.indirect_dma_start(
                                out=C["y"][:, u.p, k, b, :], out_offset=None, in_=y_d,
                                in_offset=bass.IndirectOffsetOnAxis(ap=c_idx_t[:, u.p, k, b:b + 1], axis=0),
                                ).then_inc(c_y[u.p], 16)
                    rstd(pool, u, C_st3, ln3)
                u = t.at(3, UNITS)
                if u:
                    rstd(pool, u, C_st4, ln4)
            pipelined(pool, UNITS, C_LAG, step, unroll=4)

        def heads(ap):
            return ap.rearrange("p (n s) -> p n s", s=S)

        def c_tensor(pe):

            def step(t):
                u = t.at(2, UNITS)
                if u:
                    done(pe, c_p, u)
                    done(pe, c_pTs, u.back(1))
                    for n in range(UB * H1):
                        ins = nc.tensor.transpose(bank(5)[:, n * S:(n + 1) * S], C["e"][:, u.p, n, :], ident)
                    ins.then_inc(c_pT, 1)
                u = t.at(1, UNITS)
                if u:
                    done(pe, c_qr, u)
                    done(pe, c_kr, u)
                    done(pe, c_q2, u)
                    done(pe, c_k2, u)
                    done(pe, c_sub, u.back(1))
                    nc.tensor.matmul(bank(4), ident_bf[:, :],
                                     causal_bf[:, None, :].broadcast_to([P, UB * H1, S]), start=True, stop=False,
                                     skip_group_check=True)
                    for b in range(UB):
                        for h in range(H1):
                            n = b * H1 + h
                            ins = nc.tensor.matmul(bank(4)[:, n * S:(n + 1) * S], C["q"][:, h, b * S:(b + 1) * S],
                                                   C["k"][:, h, b * S:(b + 1) * S], start=False,
                                                   stop=(n == UB * H1 - 1), skip_group_check=True)
                    ins.then_inc(c_S, 1)
                u = t.at(2, UNITS)
                if u:
                    done(pe, c_pTs, u)
                    done(pe, c_os, u.back(1))
                    for b in range(UB):
                        for h in range(H1):
                            ins = nc.tensor.matmul(bank(6)[:, h * T + b * S:h * T + (b + 1) * S],
                                                   C["v"][:, u.p, b, h * P:(h + 1) * P],
                                                   C["pT"][:, b * H1 + h, :], start=True, stop=True)
                    ins.then_inc(c_o, 1)
                u = t.at(0, UNITS)
                if u:
                    done(pe, c_x3, u)
                    done(pe, c_x3F, u.back(1))
                    to_feature(bank(0), C["x3"][:, u.c % 4]).then_inc(c_x3T, 1)
                u = t.at(2, UNITS)
                if u:
                    done(pe, c_os, u)
                    done(pe, c_r4, u.back(1))
                    for b in range(UB):
                        for h in range(H1):
                            ins = nc.tensor.matmul(bank(7)[:, b * D:(b + 1) * D], C["oF"][:, h, b * S:(b + 1) * S],
                                                   w["L1_attn_wo"][:, h, :], start=(h == 0), stop=(h == H1 - 1))
                    ins.then_inc(c_wo, 1)
                u = t.at(0, UNITS)
                if u:
                    done(pe, c_x3F, u)
                    for name, k, s_out, read in (("L1_attn_wq", 1, c_q, (c_qt, c_q2)), ("L1_attn_wk", 2, c_k, (c_kt, c_k2))):
                        for r in read:
                            done(pe, r, u.back(1))
                        for h in range(H1):
                            for c in range(NC_):
                                ins = nc.tensor.matmul(bank(k)[:, h * T:(h + 1) * T], w[name][:, c, h * P:(h + 1) * P],
                                                       C["x3F"][:, c, :], start=(c == 0), stop=(c == NC_ - 1))
                        ins.then_inc(s_out, 1)
                    done(pe, c_vs, u.back(1))
                    for b in range(UB):
                        for c in range(NC_):
                            ins = nc.tensor.matmul(bank(3)[:, b * D:(b + 1) * D], C["x3F"][:, c, b * S:(b + 1) * S],
                                                   w["L1_attn_wv"][:, c, :], start=(c == 0), stop=(c == NC_ - 1))
                    ins.then_inc(c_v, 1)
            pipelined(pe, UNITS, C_LAG, step, unroll=4)

        def c_scalar(act):
            def step(t):
                u = t.at(1, UNITS)
                if u:
                    done(act, c_qt, u)
                    done(act, c_S, u.back(1))
                    nc.scalar.activation(C["q"][64:P], bank(1)[64:P, :].rearrange("p (h t) -> p h t", h=H1),
                                         ACT.Copy).then_inc(c_q2, 1)
                    done(act, c_kt, u)
                    nc.scalar.activation(C["k"][64:P], bank(2)[64:P, :].rearrange("p (h t) -> p h t", h=H1),
                                         ACT.Copy).then_inc(c_k2, 1)
                u = t.at(2, UNITS)
                if u:
                    done(act, c_pT, u)
                    done(act, c_o, u.back(1))
                    nc.scalar.activation(C["pT"], heads(bank(5)), ACT.Copy).then_inc(c_pTs, 1)
                    done(act, c_o, u)
                    done(act, c_wo, u.back(1))
                    nc.scalar.activation(C["oF"], chunks(bank(6)), ACT.Copy).then_inc(c_os, 1)
                u = t.at(0, UNITS)
                if u:
                    done(act, c_x3T, u)
                    done(act, c_v, u.back(1))
                    nc.scalar.activation(C["x3F"], chunks(bank(0)), ACT.Copy).then_inc(c_x3F, 1)
                u = t.at(1, UNITS)
                if u:
                    done(act, c_sub, u)
                    nc.scalar.activation(C["e"][:, u.p], C["e"][:, u.p], ACT.Exp, scale=1.0 / P).then_inc(c_ex, 1)
                u = t.at(0, UNITS)
                if u:
                    done(act, c_v, u)
                    done(act, c_o, u.back(2))
                    nc.scalar.activation(C["v"][:, u.p], seqs(bank(3)), ACT.Copy).then_inc(c_vs, 1)
            pipelined(act, UNITS, C_LAG, step, unroll=4)

        def c_vector(dve):
            def rope(u, src, dst, t2, s_t, s_r):
                s3 = heads(src)
                d3, t3 = heads(dst.rearrange("p h t -> p (h t)")), heads(t2.rearrange("p h t -> p (h t)"))

                def tb(name, lo, hi):
                    return table(name)[lo:hi, None, :].broadcast_to([hi - lo, UB * H1, S])
                nc.vector.tensor_tensor(d3[0:64], s3[0:64], tb("rope_cos", 0, 64), ALU.mult)
                nc.vector.tensor_tensor(t3[0:32], s3[32:64], tb("rope_sin", 32, 64), ALU.mult)
                nc.vector.tensor_tensor(t3[32:64], s3[0:32], tb("rope_sin", 0, 32), ALU.mult).then_inc(s_t, 1)
                done(dve, s_t, u)
                nc.vector.tensor_tensor(d3[0:64], d3[0:64], t3[0:64], ALU.add).then_inc(s_r, 1)

            def step(t):
                u = t.at(2, UNITS)
                if u:
                    e = C["e"][:, u.p]
                    done(dve, c_ex, u)
                    nc.vector.tensor_reduce(C["sum"], e, AX, ALU.add).then_inc(c_sum, 1)
                    dve.wait_ge(c_sum, u.n * 2 + 1)
                    nc.vector.reciprocal(C["rec"], C["sum"]).then_inc(c_sum, 1)
                    dve.wait_ge(c_sum, u.n * 2 + 2)
                    nc.vector.tensor_tensor(e, e, C["rec"][:, :, None].broadcast_to([P, UB * H1, S]),
                                            ALU.mult).then_inc(c_p, 1)
                u = t.at(1, UNITS)
                if u:
                    done(dve, c_q, u)
                    done(dve, c_S, u.back(1))
                    rope(u, bank(1), C["q"], C["t2q"], c_qt, c_qr)
                    done(dve, c_k, u)
                    done(dve, c_qr, u)
                    rope(u, bank(2), C["k"], C["t2k"], c_kt, c_kr)
                u = t.at(0, UNITS)
                if u:
                    landed(dve, c_in, u)
                    landed(dve, c_y, u, 4)
                    done(dve, c_x3, u.back(1))
                    for k in range(TOP0):
                        for b in range(UB):
                            ins = nc.vector.scalar_tensor_tensor(
                                C["r"][:, b, :], C["y"][:, u.p, k, b, :], gates[:, k, bass.ds(u.n * UB + b, 1)],
                                C["x2"][:, u.p, b, :] if k == 0 else C["r"][:, b, :], ALU.mult, ALU.add)
                        ins.then_inc(c_mix, 1)
                        dve.wait_ge(c_mix, u.n * 2 + (k + 1))
                    layer_norm(dve, u, C["r"], C["x3"][:, u.c % 4], C_st3, ln3)
                u = t.at(3, UNITS)
                if u:
                    done(dve, c_wo, u)
                    done(dve, c_x4, u.back(1))
                    nc.vector.tensor_tensor(C["r4"], seqs(bank(7)), C["x3"][:, u.c % 4], ALU.add).then_inc(c_r4, 1)
                    done(dve, c_r4, u)
                    landed(dve, c_st, u.back(2))
                    layer_norm(dve, u, C["r4"], C["x4"][:, u.p], C_st4, ln4)
                u = t.at(1, UNITS)
                if u:
                    done(dve, c_S, u)
                    done(dve, c_pT, u.back(2))
                    nc.vector.tensor_reduce(C["mx"], heads(bank(4)), AX, ALU.max).then_inc(c_mx, 1)
                    done(dve, c_mx, u)
                    nc.vector.tensor_tensor(C["e"][:, u.p], heads(bank(4)),
                                            C["mx"][:, :, None].broadcast_to([P, UB * H1, S]),
                                            ALU.subtract).then_inc(c_sub, 1)
            pipelined(dve, UNITS, C_LAG, step, unroll=4)

        add("sync", c_sync)
        add("gpsimd", c_gpsimd)
        add("tensor", c_tensor)
        add("scalar", c_scalar)
        add("vector", c_vector)
        arena_x.reset()
        VW = 2 * HD
        X = {}
        X["x4"] = arena_x.take([P, 2, UB, D])
        X["cx"] = arena_x.take([P, 2, UB, D])
        X["xb"] = arena_x.take([P, 4, UB, D])
        X["x4F"] = arena_x.take([P, NC_, T])
        X["cF"] = arena_x.take([P, NC_, T])
        X["q"] = arena_x.take([P, 2, NC_, T])
        X["k"] = arena_x.take([P, 2, 2, NC_ * T])
        X["v"] = arena_x.take([P, 2, UB, NH, VW])
        X["e"] = arena_x.take([P, UB, NH, S])
        X["eT"] = arena_x.take([P, 2, NH * S])
        X["aF"] = arena_x.take([P, NC_, T])
        X["x5"] = arena_x.take([P, 2, UB, D])
        X["r"] = arena_x.take([P, UB, D])
        X["mx"] = arena_x.take([P, 2, NH])
        X["rec"] = arena_x.take([P, NC_, S])
        X["half"] = arena_x.take([P, 2, VW])
        ARENA_X_E = arena_x.at
        X_st = sb("X_st", [P, UB, 10])
        x_in, x_st = sem2("x_in"), sem2("x_st")
        x_xT, x_cT, x_q, x_k, x_v, x_S, x_eT, x_pv, x_wo = (
            sem("x_" + n) for n in ("xT", "cT", "q", "k", "v", "S", "eT", "pv", "wo"))
        x_xF, x_cF, x_qs, x_ks, x_ex, x_eTs = (
            sem("x_" + n) for n in ("xF", "cF", "qs", "ks", "ex", "eTs"))
        x_mask = sem("x_mask")
        x_vs, x_mx, x_sub, x_rec, x_at, x_r, x_xb, x_one = (
            sem("x_" + n) for n in ("vs", "mx", "sub", "rec", "at", "r", "xb", "one"))
        ln5 = [sem("ln5_" + n) for n in ("st", "ag", "rs", "out")]
        x_x5 = ln5[3]
        E_LAG = 3

        def seq_done(eng, s, u, b, per=1, k=None):
            if u.fixed and u.n < 0:
                return
            if b < 0:
                u, b = u.back(1), b + 2
                if u.fixed and u.n < 0:
                    return
            eng.wait_ge(s, u.n * (2 * per) + (b * per + (per if k is None else k)))

        def e_sync(sp):
            sp.wait_ge(c_st[0], 16 * per_parity)
            sp.wait_ge(c_st[1], 16 * per_parity)
            d_weights(sp)

            def step(t):
                u = t.at(0, UNITS)
                if u:
                    done(sp, x_xb, u.back(2))
                    done(sp, x_xT, u.back(2))
                    sp.dma_start(X["x4"][:, u.p], x4_u[u.n]).then_inc(x_in[u.p], 16)
                    done(sp, x_cT, u.back(2))
                    sp.dma_start(X["cx"][:, u.p], ctx_u[u.n]).then_inc(x_in[u.p], 16)
                u = t.at(3, UNITS)
                if u:
                    done(sp, x_x5, u)
                    sp.dma_start(x5_u[u.n], X["x5"][:, u.p]).then_inc(x_st[u.p], 16)
            pipelined(sp, UNITS, E_LAG, step, unroll=4)

        def e_gpsimd(pool):

            def step(t):
                u = t.at(2, UNITS)
                if u:
                    rstd(pool, u, X_st, ln5)
                u = t.at(0, UNITS)
                if u:
                    landed(pool, x_in, u, 2)
                    done(pool, x_r, u.back(4))
                    for b in range(UB):
                        ins = nc.gpsimd.tensor_tensor(X["xb"][:, u.c % 4, b, :], X["x4"][:, u.p, b, :], bo_b[:, :],
                                                      ALU.add)
                    ins.then_inc(x_xb, 1)
            pipelined(pool, UNITS, E_LAG, step, unroll=4)

        def e_tensor(pe):
            pe.wait_ge(c_x3F, UNITS)
            pe.wait_ge(c_q2, UNITS)
            pe.wait_ge(c_k2, UNITS)
            pe.wait_ge(c_vs, UNITS)
            pe.wait_ge(c_sub, UNITS)
            pe.wait_ge(c_pTs, UNITS)
            pe.wait_ge(c_os, UNITS)
            pe.wait_ge(c_r4, UNITS)

            def scores(u, b):
                seq_done(pe, x_sub, u, b - 1)
                for quad in range(4):
                    ins = nc.tensor.matmul(bank(quad), ones_row[:, :],
                                           mask_row[:, None, bass.ds(u.n * T + b * S, S)].broadcast_to([1, 4, S]),
                                           start=True, stop=False, skip_group_check=True)
                ins.then_inc(x_mask, 1)
                seq_done(pe, x_mask, u, b)
                for c in range(NC_):
                    for par in range(2):
                        for quad in range(4):
                            rows = slice(32 * quad, 32 * quad + 32)
                            at = (2 * c + par) * S
                            ins = nc.tensor.matmul(bank(quad)[:, at:at + S],
                                                   X["q"][rows, u.p, c, b * S:(b + 1) * S],
                                                   X["k"][rows, u.p, par, c * T + b * S:c * T + (b + 1) * S],
                                                   start=False, stop=(c == 1 and par == 1), skip_group_check=True)
                ins.then_inc(x_S, 1)

            def attend(u, b):
                seq_done(pe, x_ex, u, b)
                for g in range(4):
                    seq_done(pe, x_eTs, u, b, 4, g - 1) if g >= 2 else seq_done(pe, x_eTs, u, b - 1, 4, g + 3)
                    for k in range(4):
                        ins = nc.tensor.transpose(bank(4 + g % 2)[:, k * S:(k + 1) * S], X["e"][:, b, 4 * g + k, :],
                                                  ident)
                    ins.then_inc(x_eT, 1)

            def values(u, b):
                seq_done(pe, x_eTs, u, b, 4)
                for c in range(NC_):
                    for par in range(2):
                        for kind in range(2):
                            for quad in range(4):
                                at = (4 * quad + 2 * c + par) * S
                                left = (X["v"][:, u.p, b, 8 * c + 2 * quad + par, :], X["half"][:, par, :])[kind]
                                ins = nc.tensor.matmul(
                                    bank(7)[32 * quad:32 * quad + 32, (kind * NC_ + c) * S:(kind * NC_ + c + 1) * S],
                                    left, X["eT"][:, b, at:at + S], start=(c == par == kind == 0), stop=(c == par == kind == 1),
                                    skip_group_check=True)
                ins.then_inc(x_pv, 1)

            def project(dst, name, src):
                for m in range(NC_):
                    for c in range(NC_):
                        ins = nc.tensor.matmul(dst[:, m * T:(m + 1) * T], w[name][:, c, m * P:(m + 1) * P],
                                               src[:, c, :], start=(c == 0), stop=(c == NC_ - 1))
                return ins

            def project_rows(dst, name, src):
                for b in range(UB):
                    for c in range(NC_):
                        ins = nc.tensor.matmul(dst[:, b * D:(b + 1) * D], src[:, c, b * S:(b + 1) * S],
                                               w[name][:, c, :], start=(c == 0), stop=(c == NC_ - 1))
                return ins

            def step(t):
                u0, u1, u2 = t.at(0, UNITS), t.at(1, UNITS), t.at(2, UNITS)
                if u1:
                    done(pe, x_qs, u1)
                    done(pe, x_ks, u1, 4)
                    scores(u1, 0)
                if u0:
                    landed(pe, x_in, u0, 2)
                    done(pe, x_vs, u0.back(1))
                    done(pe, x_r, u0.back(3))
                    to_feature(bank(6), X["x4"][:, u0.p]).then_inc(x_xT, 1)
                if u2:
                    attend(u2, 1)
                if u0:
                    done(pe, x_xF, u0)
                    project(bank(6), "L1_xattn_Wq", X["x4F"]).then_inc(x_q, 1)
                    if u2:
                        seq_done(pe, x_eTs, u2, 1, 4, 3)
                    to_feature(bank(4), X["cx"][:, u0.p]).then_inc(x_cT, 1)
                if u2:
                    seq_done(pe, x_at, u2, 0)
                    values(u2, 1)
                if u0:
                    done(pe, x_cF, u0)
                    project(bank(5), "L1_xattn_Wk", X["cF"]).then_inc(x_k, 1)
                    done(pe, x_qs, u0)
                    project_rows(bank(6), "L1_xattn_Wv", X["cF"]).then_inc(x_v, 1)
                if u1:
                    scores(u1, 1)
                    if u0:
                        done(pe, x_ks, u0, 4)
                    attend(u1, 0)
                if u2:
                    seq_done(pe, x_at, u2, 1)
                    if u0:
                        done(pe, x_vs, u0)
                    else:
                        done(pe, x_r, u2.back(1))
                    project_rows(bank(6), "L1_xattn_Wo", X["aF"]).then_inc(x_wo, 1)
                if u1:
                    done(pe, x_vs, u1)
                    if u2:
                        seq_done(pe, x_at, u2, 1)
                    values(u1, 0)
            pipelined(pe, UNITS, E_LAG, step, unroll=4)

        def e_scalar(act):

            def turned(u, b):
                for g in range(4):
                    seq_done(act, x_eT, u, b, 4, g + 1)
                    if g == 0:
                        seq_done(act, x_pv, u.back(1), b)
                    nc.scalar.activation(X["eT"][:, b, g * 512:(g + 1) * 512], bank(4 + g % 2), ACT.Copy)\
                        .then_inc(x_eTs, 1)

            def step(t):
                u0, u1, u2 = t.at(0, UNITS), t.at(1, UNITS), t.at(2, UNITS)
                if u0:
                    done(act, x_xT, u0)
                    done(act, x_q, u0.back(1))
                    nc.scalar.activation(X["x4F"], chunks(bank(6)), ACT.Copy).then_inc(x_xF, 1)
                if u2:
                    turned(u2, 1)
                if u0:
                    done(act, x_q, u0)
                    seq_done(act, x_S, u0.back(2), 1)
                    for c in range(NC_):
                        ins = nc.scalar.activation(X["q"][:, u0.p, c, :], bank(6)[:, c * T:(c + 1) * T], ACT.Identity,
                                                   bias=vec[:, V_BQ + c:V_BQ + c + 1])
                    ins.then_inc(x_qs, 1)
                    done(act, x_cT, u0)
                    done(act, x_v, u0.back(1))
                    nc.scalar.activation(X["cF"], chunks(bank(4)), ACT.Copy).then_inc(x_cF, 1)
                if u1:
                    seq_done(act, x_sub, u1, 0)
                    nc.scalar.activation(X["e"][:, 0], X["e"][:, 0], ACT.Exp, scale=HD ** -0.5).then_inc(x_ex, 1)
                if u0:
                    done(act, x_k, u0)
                    for par, name in enumerate(("even_heads", "odd_heads")):
                        for c in range(NC_):
                            nc.scalar.activation(X["k"][:, u0.p, par, c * T:(c + 1) * T], bank(5)[:, c * T:(c + 1) * T],
                                                 ACT.Identity, bias=kb_par[:, par, c:c + 1],
                                                 scale=table(name)).then_inc(x_ks, 1)
                if u1:
                    turned(u1, 0)
                    seq_done(act, x_sub, u1, 1)
                    nc.scalar.activation(X["e"][:, 1], X["e"][:, 1], ACT.Exp, scale=HD ** -0.5).then_inc(x_ex, 1)
            pipelined(act, UNITS, E_LAG, step, unroll=4)

        def e_vector(dve):
            nc.vector.memset(X["v"].rearrange("p a b h o -> p (a b h o)"), 0.0).then_inc(x_one, 1)
            nc.vector.memset(X["half"].rearrange("p a o -> p (a o)"), 0.0).then_inc(x_one, 1)
            dve.wait_ge(x_one, 2)
            for par in range(2):
                nc.vector.memset(X["half"][:, par, par * HD:(par + 1) * HD], 1.0).then_inc(x_one, 1)

            def less_max(u, b):
                s3 = psum[:, 0:4, :].rearrange("p q (k s) -> p (q k) s", s=S)
                seq_done(dve, x_S, u, b)
                seq_done(dve, x_eT, u.back(1), b, 4)
                nc.vector.tensor_reduce(X["mx"][:, b, :], s3, AX, ALU.max).then_inc(x_mx, 1)
                seq_done(dve, x_mx, u, b)
                nc.vector.tensor_tensor(X["e"][:, b], s3, X["mx"][:, b, :, None].broadcast_to([P, NH, S]),
                                        ALU.subtract).then_inc(x_sub, 1)

            def normalise(u, b):
                seq_done(dve, x_pv, u, b)
                seq_done(dve, x_at, u, b - 1)
                nc.vector.reciprocal(X["rec"], bank(7)[:, D:2 * D].rearrange("p (c s) -> p c s", c=NC_)).then_inc(x_rec, 1)
                seq_done(dve, x_rec, u, b)
                nc.vector.tensor_tensor(X["aF"][:, :, b * S:(b + 1) * S],
                                        bank(7)[:, 0:D].rearrange("p (c s) -> p c s", c=NC_), X["rec"],
                                        ALU.mult).then_inc(x_at, 1)

            def step(t):
                u0, u1, u2 = t.at(0, UNITS), t.at(1, UNITS), t.at(2, UNITS)
                if u1:
                    less_max(u1, 0)
                if u2:
                    normalise(u2, 1)
                if u0:
                    done(dve, x_v, u0)
                    seq_done(dve, x_pv, u0.back(2), 1)
                    for par in range(2):
                        ins = nc.vector.tensor_tensor(
                            X["v"][:, u0.p].rearrange("p b (i k) o -> p (b i) k o", k=2)[:, :, par,
                                                                                       par * HD:(par + 1) * HD],
                            bank(6).rearrange("p (i k d) -> p i k d", k=2, d=HD)[:, :, par, :],
                            bv2_b[:, :].rearrange("p (i k d) -> p i k d", k=2, d=HD)[:, :, par, :], ALU.add)
                    ins.then_inc(x_vs, 1)
                if u1:
                    less_max(u1, 1)
                if u2:
                    done(dve, x_wo, u2)
                    done(dve, x_xb, u2)
                    done(dve, x_x5, u2.back(1))
                    nc.vector.tensor_tensor(X["r"], seqs(bank(6)), X["xb"][:, u2.c % 4], ALU.add).then_inc(x_r, 1)
                    done(dve, x_r, u2)
                    ln_stats(dve, u2, X["r"], X_st, ln5)
                if u1:
                    normalise(u1, 0)
                if u2:
                    landed(dve, x_st, u2.back(2))
                    ln_apply(dve, u2, X["r"], X["x5"][:, u2.p], X_st, ln5)
            pipelined(dve, UNITS, E_LAG, step, unroll=4)

        add("sync", e_sync)
        add("gpsimd", e_gpsimd)
        add("tensor", e_tensor)
        add("scalar", e_scalar)
        add("vector", e_vector)

        HIDD = NE1 * PD
        HJ = HIDD // P
        N_TOP, TOP_LESS = 18, 2
        SL = HJ // 2
        arena_x.reset()
        arena_y.reset()
        K = {}
        K["vd"] = arena_y.take([P, NC_, HIDD])
        K["vu"] = arena_y.take([P, HJ, D])
        K["x5"] = arena_x.take([P, 4, UB, D])
        K["x5F"] = arena_x.take([P, 2, NC_, T])
        K["r"] = arena_x.take([P, UB, D])
        K["th"] = arena_x.take([P, 2, 2, T])
        K["t"] = arena_x.take([P, 2, 2, T])
        K["g"] = arena_x.take([P, 2, 2, T])
        K["hF"] = arena_x.take([P, T])[0:PD, :]
        for n in ("sim", "gt", "eq", "cum", "ex", "rem"):
            K[n] = arena_x.take([P, UB, NE1])
        K["mx8"] = arena_x.take([P, UB, 8])
        K["ngt"] = arena_x.take([P, UB])
        K["sum"] = arena_x.take([P, UB])
        expand = arena_x.take([P, HIDD // 2]).bitcast(BF16)
        parts = arena_x.take([P, UB, 4 * NE1 // 2]).bitcast(BF16)
        wT = arena_x.take([P, 2, T // 2]).bitcast(BF16)
        K_st = arena_x.take([P, UB, 10])
        keep_ex = arena_x.take([P, UB, NE1])
        d_w = sem("d_w")
        d_in, d_st = sem2("d_in"), sem2("d_st")
        d_xT, d_h, d_sim, d_z, d_wb, d_up, d_wTp = (sem("d_" + n) for n in ("xT", "h", "sim", "z", "wb", "up", "wTp"))
        d_xF, d_hF, d_sims, d_th, d_ex, d_wT = (sem("d_" + n) for n in ("xF", "hF", "sims", "th", "ex", "wT"))
        d_one, d_top, d_t, d_g, d_r = (sem("d_" + n) for n in ("one", "top", "t", "g", "r"))
        ln6 = [sem("ln6_" + n) for n in ("st", "ag", "rs", "out")]
        d_out = ln6[3]
        D_LAG = 2

        def slice_done(eng, s, u, k):
            seq_done(eng, s, u, k // 4, 4, k % 4 + 1)

        def d_weights(eng):
            eng.dma_start(K["vd"], a["down"].rearrange("(c p) h -> p c h", p=P)).then_inc(d_w, 16)
            eng.dma_start(K["vu"], a["up"].rearrange("(j p) d -> p j d", p=P)).then_inc(d_w, 16)

        def d_sync(sp):
            for k in range(2):
                sp.wait_ge(x_st[k], 16 * per_parity)

            def step(t):
                u = t.at(0, UNITS)
                if u:
                    landed(sp, d_st, u.back(4))
                    done(sp, d_xT, u.back(2))
                    sp.dma_start(K["x5"][:, u.c % 4], x5_u[u.n]).then_inc(d_in[u.p], 16)
                u = t.at(2, UNITS)
                if u:
                    done(sp, d_out, u)
                    sp.dma_start(out_u[u.n], K["x5"][:, u.c % 4]).then_inc(d_st[u.p], 16)
            pipelined(sp, UNITS, D_LAG, step, unroll=4)
            for k in range(2):
                sp.wait_ge(d_st[k], 16 * per_parity)

        def d_gpsimd(pool):
            def step(t):
                u = t.at(2, UNITS)
                if u:
                    rstd(pool, u, K_st, ln6)
            pipelined(pool, UNITS, D_LAG, step, unroll=4)

        def d_tensor(pe):
            pe.wait_ge(d_w, 32)
            pe.wait_ge(d_one, 5)
            pe.wait_ge(x_r, UNITS)
            seq_done(pe, x_eTs, Unit(0, UNITS - 1), 1, 4)

            def up(u, s):
                slice_done(pe, d_g, u, s)
                for k in range(2):
                    for b in range(UB):
                        ins = nc.tensor.matmul(bank(4 + u.p)[:, b * D:(b + 1) * D],
                                               K["g"][:, s % 2, k, b * S:(b + 1) * S], K["vu"][:, 2 * s + k, :],
                                               start=(s == 0 and k == 0 and b == 0), stop=(s == SL - 1 and k == 1),
                                               skip_group_check=True)
                ins.then_inc(d_up, 1)

            def step(t):
                u0, u1, u2 = t.at(0, UNITS), t.at(1, UNITS), t.at(2, UNITS)
                for s in range(SL):
                    if u1:
                        if s == 0:
                            done(pe, d_xF, u1)
                        slice_done(pe, d_t, u1, s - 2)
                        for k in range(2):
                            j = 2 * s + k
                            for c in range(NC_):
                                ins = nc.tensor.matmul(bank(s % 2)[:, k * T:(k + 1) * T],
                                                       K["vd"][:, c, j * P:(j + 1) * P], K["x5F"][:, u1.p, c, :],
                                                       start=(c == 0), stop=(c == NC_ - 1))
                        ins.then_inc(d_z, 1)
                        if s == 0:
                            done(pe, d_wT, u1, 2)
                        slice_done(pe, d_g, u1, s - 2)
                        for k in range(2):
                            j = 2 * s + k
                            for part in range(2):
                                ins = nc.tensor.matmul(bank(2 + s % 2)[:, k * T:(k + 1) * T],
                                                       expand[:, j * P:(j + 1) * P], wT[:, part, :],
                                                       start=(part == 0), stop=(part == 1))
                        ins.then_inc(d_wb, 1)
                    if s >= 2 and u1:
                        if s == 2:
                            done(pe, d_r, u1.back(2))
                        up(u1, s - 2)
                    if s < 2 and u2:
                        up(u2, SL + s - 2)
                    if not u0:
                        continue
                    if s == 0:
                        landed(pe, d_in, u0)
                        done(pe, d_wT, u0.back(1), 2)
                        to_feature(bank(6), K["x5"][:, u0.c % 4]).then_inc(d_xT, 1)
                    if s == 1:
                        done(pe, d_xF, u0)
                        done(pe, d_sims, u0.back(1))
                        for c in range(NC_):
                            ins = nc.tensor.matmul(bank(7)[0:PD, 0:T], w_hash[:, c, :], K["x5F"][:, u0.p, c, :],
                                                   start=(c == 0), stop=(c == NC_ - 1))
                        ins.then_inc(d_h, 1)
                    if s == 2:
                        done(pe, d_hF, u0)
                        for b in range(UB):
                            ins = nc.tensor.matmul(bank(7)[:, T + b * NE1:T + (b + 1) * NE1],
                                                   K["hF"][:, b * S:(b + 1) * S], w_keys[:, :], start=True, stop=True)
                        ins.then_inc(d_sim, 1)
                    if s == SL - 1:
                        done(pe, d_top, u0, N_TOP)
                        for part in range(2):
                            for b in range(UB):
                                ins = nc.tensor.transpose(
                                    bank(6)[:, part * P:(part + 1) * P].bitcast(BF16)[:, b * S:(b + 1) * S],
                                    parts[:, b, part * P:(part + 1) * P], ident_bf[:, :])
                        ins.then_inc(d_wTp, 1)
            pipelined(pe, UNITS, D_LAG, step, unroll=4)

        def d_scalar(act):
            def step(t):
                u0, u1 = t.at(0, UNITS), t.at(1, UNITS)
                for s in range(SL):
                    if u1:
                        slice_done(act, d_z, u1, s)
                        slice_done(act, d_t, u1, s - 2)
                        nc.scalar.activation(K["th"][:, s % 2], bank(s % 2).rearrange("p (k t) -> p k t", k=2), ACT.Tanh,
                                             scale=0.5).then_inc(d_th, 1)
                    if not u0:
                        continue
                    if s == 0:
                        done(act, d_xT, u0)
                        slice_done(act, d_z, u0.back(2), SL - 1)
                        nc.scalar.activation(K["x5F"][:, u0.p], chunks(bank(6)), ACT.Copy).then_inc(d_xF, 1)
                    if s == 1:
                        done(act, d_h, u0)
                        done(act, d_sim, u0.back(1))
                        nc.scalar.activation(K["hF"], bank(7)[0:PD, 0:T], ACT.Copy).then_inc(d_hF, 1)
                    if s == 2:
                        done(act, d_sim, u0)
                        done(act, d_top, u0.back(1), N_TOP)
                        nc.scalar.activation(K["sim"], bank(7)[:, T:T + UB * NE1].rearrange("p (b e) -> p b e", b=UB),
                                             ACT.Copy).then_inc(d_sims, 1)
                    if s == 4:
                        act.wait_ge(d_top, u0.n * N_TOP + TOP_LESS)
                        nc.scalar.activation(K["ex"], K["ex"], ACT.Exp).then_inc(d_ex, 1)
                    if s == SL - 1:
                        done(act, d_wTp, u0)
                        slice_done(act, d_wb, u1, SL - 1) if u1 else None
                        for part in range(2):
                            nc.scalar.activation(wT[:, part, :], bank(6)[:, part * P:(part + 1) * P].bitcast(BF16),
                                                 ACT.Copy).then_inc(d_wT, 1)
            pipelined(act, UNITS, D_LAG, step, unroll=4)

        def d_vector(dve):
            dve.wait_ge(x_st[0], 16 * per_parity)
            dve.wait_ge(x_st[1], 16 * per_parity)
            for lo in (0, NE1):
                rows = slice(lo, lo + NE1)
                nc.vector.tensor_scalar(expand[rows, :].rearrange("p (e r) -> p e r", r=PD),
                                        ident[rows, lo:lo + NE1, None].broadcast_to([NE1, NE1, PD]), 1.0, None,
                                        ALU.mult).then_inc(d_one, 1)
            nc.vector.memset(parts[:, :, 3 * NE1:], 0.0).then_inc(d_one, 1)
            nc.vector.memset(keep_ex[:, :, 1:], 1.0).then_inc(d_one, 1)
            nc.vector.memset(keep_ex[:, :, 0:1], 0.0).then_inc(d_one, 1)
            dve.wait_ge(d_one, 5)

            def choose(u):
                steps = [0]

                def after(ins):
                    ins.then_inc(d_top, 1)
                    steps[0] += 1

                def ready():
                    dve.wait_ge(d_top, u.n * N_TOP + steps[0])

                def per_b(ap, k=0):
                    return ap[:, :, k:k + 1].broadcast_to([P, UB, NE1])

                done(dve, d_sims, u)
                nc.vector.memset(wait_cell[:, :], 0.0)
                for b in range(UB):
                    ins = nc.vector.max(K["mx8"][:, b, :], K["sim"][:, b, :])
                after(ins)
                ready()
                after(nc.vector.tensor_tensor(K["ex"], K["sim"], per_b(K["mx8"]), ALU.subtract))
                after(nc.vector.tensor_tensor(K["gt"], K["sim"], per_b(K["mx8"], TOP1 - 1), ALU.is_gt))
                after(nc.vector.tensor_tensor(K["eq"], K["sim"], per_b(K["mx8"], TOP1 - 1), ALU.is_equal))
                ready()
                after(nc.vector.tensor_reduce(K["ngt"], K["gt"], AX, ALU.add))
                after(nc.vector.tensor_tensor_scan(K["cum"].rearrange("p b e -> p (b e)"), keep_ex.rearrange("p b e -> p (b e)"),
                                                   K["eq"].rearrange("p b e -> p (b e)"), 0.0, ALU.mult, ALU.add))
                ready()
                after(nc.vector.tensor_tensor(K["cum"], K["cum"], K["ngt"][:, :, None].broadcast_to([P, UB, NE1]),
                                              ALU.add))
                ready()
                after(nc.vector.scalar_tensor_tensor(K["eq"], K["cum"], float(TOP1), K["eq"], ALU.is_le, ALU.mult))
                ready()
                after(nc.vector.tensor_tensor(K["gt"], K["gt"], K["eq"], ALU.add))
                ready()
                done(dve, d_ex, u)
                after(nc.vector.tensor_tensor(K["ex"], K["ex"], K["gt"], ALU.mult))
                ready()
                after(nc.vector.tensor_reduce(K["sum"], K["ex"], AX, ALU.add))
                ready()
                after(nc.vector.reciprocal(K["sum"], K["sum"]))
                ready()
                after(nc.vector.tensor_scalar(K["sum"], K["sum"], scale_b[:, 0:1], 0.5, ALU.mult, ALU.mult))
                ready()
                after(nc.vector.tensor_tensor(K["ex"], K["ex"], K["sum"][:, :, None].broadcast_to([P, UB, NE1]),
                                              ALU.mult))
                ready()
                done(dve, d_wTp, u.back(1))
                after(nc.vector.tensor_scalar(parts[:, :, 0:NE1], K["ex"], 1.0, None, ALU.mult))
                ready()
                after(nc.vector.tensor_tensor(K["rem"], K["ex"], parts[:, :, 0:NE1], ALU.subtract))
                ready()
                after(nc.vector.tensor_scalar(parts[:, :, NE1:2 * NE1], K["rem"], 1.0, None, ALU.mult))
                ready()
                after(nc.vector.tensor_tensor(parts[:, :, 2 * NE1:3 * NE1], K["rem"], parts[:, :, NE1:2 * NE1],
                                              ALU.subtract))
                assert steps[0] == N_TOP, steps

            def step(t):
                u0, u1, u2 = t.at(0, UNITS), t.at(1, UNITS), t.at(2, UNITS)
                for s in range(SL):
                    if u1:
                        slice_done(dve, d_th, u1, s)
                        slice_done(dve, d_g, u1, s - 2)
                        z = bank(s % 2).rearrange("p (k t) -> p k t", k=2)
                        nc.vector.scalar_tensor_tensor(K["t"][:, s % 2], K["th"][:, s % 2], 1.0, z, ALU.add,
                                                       ALU.mult).then_inc(d_t, 1)
                        slice_done(dve, d_t, u1, s)
                        slice_done(dve, d_wb, u1, s)
                        slice_done(dve, d_up, u1, s - 2)
                        nc.vector.tensor_tensor(K["g"][:, s % 2], K["t"][:, s % 2],
                                                bank(2 + s % 2).rearrange("p (k t) -> p k t", k=2),
                                                ALU.mult).then_inc(d_g, 1)
                    if s == 3 and u0:
                        choose(u0)
                    if s == 2 and u2:
                        slice_done(dve, d_up, u2, SL - 1)
                        done(dve, d_out, u2.back(1))
                        nc.vector.scalar_tensor_tensor(K["r"], K["x5"][:, u2.c % 4], 2.0, seqs(bank(4 + u2.p)),
                                                       ALU.mult, ALU.add).then_inc(d_r, 1)
                        done(dve, d_r, u2)
                        layer_norm(dve, u2, K["r"], K["x5"][:, u2.c % 4], K_st, ln6)
            pipelined(dve, UNITS, D_LAG, step, unroll=4)

        add("sync", d_sync)
        add("gpsimd", d_gpsimd)
        add("tensor", d_tensor)
        add("scalar", d_scalar)
        add("vector", d_vector)
        run_layer()


def kernel(**inputs):
    import concourse.bacc as _bacc
    from concourse.bass_utils import run_bass_kernel_spmd as _run

    nc = _bacc.Bacc("TRN2", target_bir_lowering=False, num_devices=1)
    table, where = constants()
    given = {k: np.asarray(v) for k, v in inputs.items()}
    given["mask"] = given.pop("mask_BxS2_bk0")
    given["hash_t"] = given.pop("L1_ffn_hasher_w").T
    given["keys_t"] = given.pop("L1_ffn_keys").T
    given["down"] = given.pop("L1_ffn_values_down").transpose(1, 0, 2).reshape(D, NE1 * PD)
    given["up"] = given.pop("L1_ffn_values_up").reshape(NE1 * PD, D)
    given["constants"] = table
    arrays, args = {}, {}
    for name, v in given.items():
        v = np.ascontiguousarray(v)
        arrays[f"in_{name}"] = v
        args[name] = nc.dram_tensor(f"in_{name}", v.shape, mybir.dt.from_np(v.dtype), kind="ExternalInput").ap()
    out = nc.dram_tensor("out_0", (B, S, D), F32, kind="ExternalOutput").ap()
    decoder(nc, args, where, out)
    return _run(nc, [arrays], core_ids=[0]).results[0]["out_0"]
```

```python
from contextlib import ExitStack

import numpy as np
import concourse.bass as bass
from concourse import mybir

F32 = mybir.dt.float32
BF16 = mybir.dt.bfloat16
F32R = mybir.dt.float32r
I32 = mybir.dt.int32
U8 = mybir.dt.uint8
ALU = mybir.AluOpType
ACT = mybir.ActivationFunctionType
AX = mybir.AxisListType.X

P = 128
B, S, D = 32, 128, 256
NC_ = D // P
UB = 2
T = UB * S
UNITS = B // UB
LN_EPS = 1e-5
BIG = 1e30

E0, HID0, TOP0 = 8, 1024, 2
CAP = TOP0 * B * S // E0
SLOTS = E0 * CAP
BW = 32
MIN_DECAY, A_EPS, SCAN_EPS = 0.001, 1e-5, 1e-7
GAMMA, THETA, SCALE_BASE = 0.96875, 10000.0, 512.0
H1 = 2
NH, HD = 16, 16
NE1, PD, TOP1 = 64, 32, 4


def constants():
    f = np.float32
    pos = np.arange(S, dtype=f)
    half = D // 2
    scale_vec = (np.arange(0, D, 2, dtype=f) + f(0.4 * D)) / f(1.4 * D)
    scale = (scale_vec[None, :] ** (pos / f(SCALE_BASE))[:, None]).astype(f)
    freqs = (f(1.0) / f(THETA) ** (np.arange(half, dtype=f) / f(half))).astype(f)
    ang = pos[:, None] * freqs[None, :]
    sin, cos = np.sin(ang).astype(f), np.cos(ang).astype(f)
    inv = (f(1.0) / scale).astype(f)
    diff = pos[:, None] - pos[None, :]
    decay = np.where(diff >= 0, f(GAMMA) ** diff, 0).astype(f)
    rot = 32
    rang = pos[:, None] * np.power(f(10000.0), -np.arange(rot, dtype=f) / f(rot)).astype(f)[None, :]
    rsin, rcos = np.sin(rang).astype(f), np.cos(rang).astype(f)
    rope_c = np.zeros((P, S), f)
    rope_c[0:32], rope_c[32:64] = rcos.T, rcos.T
    rope_s = np.zeros((P, S), f)
    rope_s[0:32], rope_s[32:64] = rsin.T, -rsin.T
    first = (np.arange(NC_ * T) % S) == 0
    odd = ((np.arange(P) // HD) % 2).astype(f)
    seg = np.arange(E0 * TOP0 * B) % (TOP0 * B) != 0

    def row(a):
        return np.broadcast_to(np.asarray(a, f), (P, len(a)))

    tables = {
        "ident": np.eye(P, dtype=f),
        "xpos_q_cos": (cos * scale).T, "xpos_q_sin": (sin * scale).T,
        "xpos_k_cos": (cos * inv).T, "xpos_k_sin": (sin * inv).T,
        "decay_t": decay.T,
        "rope_cos": rope_c, "rope_sin": rope_s,
        "causal": np.where(diff >= 0, 0, -BIG).astype(f),
        "before": (diff.T > 0).astype(f),
        "ones": np.ones((P, P), f),
        "floor": row(np.where(first, 1.0, SCAN_EPS)),
        "keep": row(np.where(first, 0.0, 1.0)),
        "keep_seg": row(seg.astype(f)),
        "rank": row(E0 - np.arange(E0)),
        "base": row(np.arange(E0) * CAP),
        "even_heads": (1 - odd)[:, None], "odd_heads": odd[:, None],
    }
    at, parts, where = 0, [], {}
    for name, a in tables.items():
        where[name] = (at, a.shape[1])
        at += a.shape[1]
        parts.append(np.asarray(a, f))
    return np.ascontiguousarray(np.concatenate(parts, axis=1)), where


class Arena:

    def __init__(self, nc, start, tile, size):
        self.nc, self.start, self.tile, self.size, self.at = nc, start, tile, size, 0

    def reset(self, at=0):
        self.at = at

    def take(self, shape, rounded=None):
        n = int(np.prod(shape[1:]))
        if rounded:
            self.at = -(-self.at // 8) * 8
        assert self.at + n <= self.size, (self.at + n, self.size)
        self.at += n
        if rounded:
            return self.view(rounded, self.at - n, shape)
        return self.shaped(self.tile[:, self.at - n:self.at], shape)

    def view(self, name, at, shape):
        n = int(np.prod(shape[1:]))
        tile = self.nc.alloc_sbuf_tensor_at(name, [P, n], F32R, offset=self.start + 4 * at)
        return self.shaped(tile[:, :], shape)

    @staticmethod
    def shaped(ap, shape):
        if len(shape) > 2:
            names = "abcdef"[:len(shape) - 1]
            ap = ap.rearrange("p (" + " ".join(names) + ") -> p " + " ".join(names),
                              **dict(zip(names, shape[1:])))
        return ap


class Unit:

    def __init__(self, i, c, m=2):
        self.i, self.c, self.m = i, c, m
        self.fixed = isinstance(i, int)

    @property
    def n(self):
        return self.c if self.fixed else self.i * self.m + self.c

    def div(self, k):
        return self.c // k if self.fixed else self.i * (self.m // k) + self.c // k

    @property
    def p(self):
        return self.c % 2

    def back(self, k):
        return Unit(self.i, self.c - k, self.m)

    def at(self, k, count):
        u = self.back(k)
        return u if not u.fixed or 0 <= u.n < count else None


def pipelined(eng, count, lag, step, unroll=2, peel=0):
    head = lag + 2
    head += (count - head) % unroll
    for t in range(head):
        step(Unit(0, t, unroll))
    with eng.Fori(0, (count - head - peel) // unroll) as i:
        for j in range(unroll):
            step(Unit(i, head + j, unroll))
    for t in range(count - peel, count + lag):
        step(Unit(0, t, unroll))


def done(eng, sem, u, per=1):
    if u.fixed and u.n < 0:
        return
    eng.wait_ge(sem, (u.n + 1) * per)


def landed(eng, sems, u, per=1):
    if u.fixed and u.n < 0:
        return
    eng.wait_ge(sems[u.p], (u.div(2) + 1) * (16 * per))


def decoder(nc, a, where, out):
    ctx = ExitStack()
    with ctx:
        def sb(name, shape, dt=F32):
            return ctx.enter_context(nc.sbuf_tensor(name, shape, dt))

        in_use = []

        def sem(name):
            in_use.append(nc.alloc_semaphore(name))
            return in_use[-1]

        def sem2(name):
            return [sem(name + "_0"), sem(name + "_1")]

        psum = ctx.enter_context(nc.psum_tensor("psum", [P, 8, 512], F32))

        def bank(k):
            return psum[:, k, :]

        def units(ap):
            return ap.rearrange("(u b) s d -> u s b d", b=UB)

        ZW = 512
        x2_d = nc.dram_tensor("x2_d", [B, S, D], F32, kind="Internal").ap()
        x4_d = nc.dram_tensor("x4_d", [B, S, D], F32, kind="Internal").ap()
        x5_d = nc.dram_tensor("x5_d", [B, S, D], F32, kind="Internal").ap()
        disp_d = nc.dram_tensor("disp_d", [SLOTS, D], F32, kind="Internal").ap()
        y_d = nc.dram_tensor("y_d", [SLOTS, D], F32, kind="Internal").ap()
        x_u, ctx_u, out_u = units(a["x"]), units(a["ctx_1024"]), units(out)
        x2_u, x4_u, x5_u = units(x2_d), units(x4_d), units(x5_d)

        n_const = a["constants"].shape[1]
        const = sb("const", [P, n_const])

        def table(name):
            at, n = where[name]
            return const[:, at:at + n]

        ident = table("ident")
        gate_w = sb("gate_w", [P, 2, NC_, P])
        w = {n: sb(n, [P, NC_, D]) for n in
             ("L0_xattn_Wq", "L0_xattn_Wk", "L0_xattn_Wv", "L1_attn_wq", "L1_attn_wk", "L1_attn_wv",
              "L1_attn_wo", "L1_xattn_Wq", "L1_xattn_Wk", "L1_xattn_Wv", "L1_xattn_Wo")}
        w_route = sb("w_route", [P, NC_, E0])
        w_hash = sb("w_hash", [P, NC_, PD])
        w_keys = sb("w_keys", [PD, NE1])
        VEC_ROWS = 10 + E0 * HID0 // P
        vec_rows = sb("vec_rows", [VEC_ROWS, P])
        vec = sb("vec", [P, VEC_ROWS])
        V_A, V_BIN, V_BA, V_BQ, V_BK, V_B1 = 0, 2, 4, 6, 8, 10
        hgate_b = sb("hgate_b", [P, 4])
        sp_tmp = sb("sp_tmp", [P, 3, NC_])
        ndecay = sb("ndecay", [P, NC_])
        kb_par = sb("kb_par", [P, 2, NC_])
        bv2_b = sb("bv2_b", [P, UB * D])
        bo_b = sb("bo_b", [P, D])
        b2_b = sb("b2_b", [P, E0, D])
        scale_b = sb("scale_b", [P, 1])
        ARENA_X, ARENA_Y = 23040, 14464
        arena_x = Arena(nc, -(-nc.sbuf_base // 32) * 32, sb("arena_x", [P, ARENA_X]), ARENA_X)
        arena_y = Arena(nc, -(-nc.sbuf_base // 32) * 32, sb("arena_y", [P, ARENA_Y]), ARENA_Y)
        mask_u8 = arena_y.take([P, B * S // 4])[0:1, :].bitcast(U8)
        mask_row = sb("mask_row", [1, B * S], BF16)
        ones_row = sb("ones_row", [1, P], BF16)
        ident_bf = sb("ident_bf", [P, P], BF16)
        causal_bf = sb("causal_bf", [P, P], BF16)
        zeros = sb("zeros", [P, ZW])
        wait_cell = sb("wait_cell", [1, 2])
        minus_half = sb("minus_half", [P, UB, 1])
        logits = sb("logits", [P, B, E0])
        gates = sb("gates", [P, TOP0, B])
        slot_g = sb("slot_g", [P, TOP0, B], I32)
        slot_s = sb("slot_s", [P, TOP0, B], I32)

        s_const, s_zero, s_prefill = sem("s_const"), sem("s_zero"), sem("s_prefill")
        s_vecT, s_vec, s_setup = sem("s_vecT"), sem("s_vec"), sem("s_setup")
        s_act_setup = sem("s_act_setup")

        s_pow = sem("s_pow")
        loads = [(const[:, :], a["constants"])]
        vec_src = [("L0_attn_a_param", 2), ("L0_attn_b_in", 2), ("L0_attn_b_a", 2),
                   ("L1_xattn_bq", 2), ("L1_xattn_bk", 2), ("L0_ffn_b1", E0 * HID0 // P)]
        at = 0
        for name, n in vec_src:
            v = a[name]
            if len(v.shape) == 2:
                v = v.rearrange("a b -> (a b)")
            loads.append((vec_rows[at:at + n, :], v.rearrange("(r p) -> r p", p=P)))
            at += n
        diag = []
        for g, name in enumerate(("L0_attn_w_in", "L0_attn_w_a")):
            for h in range(D // BW):
                c, r = divmod(h, P // BW)
                diag.append((gate_w[r * BW:(r + 1) * BW, g, c, r * BW:(r + 1) * BW], a[name][h]))
        for name in ("L0_xattn_Wq", "L0_xattn_Wk", "L0_xattn_Wv"):
            loads.append((w[name][:, :, :], a[name].rearrange("(c p) n -> p c n", p=P)))
        loads.append((w_route[:, :, :], a["L0_ffn_wg"].rearrange("(c p) n -> p c n", p=P)))
        N_EARLY = len(loads) + len(diag)
        late = []
        for name in ("L1_attn_wq", "L1_attn_wk", "L1_attn_wv"):
            late.append((w[name][:, :, :], a[name].rearrange("(c p) h n -> p c (h n)", p=P)))
        late.append((w["L1_attn_wo"][:, :, :], a["L1_attn_wo"].rearrange("h p n -> p h n")))
        for name in ("L1_xattn_Wq", "L1_xattn_Wk", "L1_xattn_Wv", "L1_xattn_Wo"):
            late.append((w[name][:, :, :], a[name].rearrange("(c p) n -> p c n", p=P)))
        late.append((w_hash[:, :, :], a["hash_t"].rearrange("(c p) n -> p c n", p=P)))
        late.append((w_keys[:, :], a["keys_t"]))
        for b in range(UB):
            late.append((bv2_b[:, b * D:(b + 1) * D],
                         a["L1_xattn_bv"].rearrange("(a n) -> a n", a=1).broadcast_to([P, D])))
        late.append((bo_b[:, :], a["L1_xattn_bo"].rearrange("(a n) -> a n", a=1).broadcast_to([P, D])))
        late.append((b2_b[:, :, :], a["L0_ffn_b2"].rearrange("(a e) n -> a e n", a=1).broadcast_to([P, E0, D])))
        late.append((scale_b[:, :], a["L1_ffn_scale"].rearrange("(a n) -> a n", a=1).broadcast_to([P, 1])))
        late.append((mask_u8[:, :], a["mask"].rearrange("(a b) s -> a (b s)", a=1)))
        s_late = sem("s_late")
        N_LATE = len(late)

        phases = {"sync": [], "tensor": [], "scalar": [], "vector": [], "gpsimd": []}

        def run_layer():
            with nc.Block() as block:
                @block.sync
                def _(eng):
                    for part in phases["sync"]:
                        part(eng)

                @block.tensor
                def _(eng):
                    for part in phases["tensor"]:
                        part(eng)

                @block.scalar
                def _(eng):
                    for part in phases["scalar"]:
                        part(eng)

                @block.vector
                def _(eng):
                    for part in phases["vector"]:
                        part(eng)

                @block.gpsimd
                def _(eng):
                    for part in phases["gpsimd"]:
                        part(eng)
            nc.clear_and_free_semaphores(list(in_use))
            nc.all_engine_barrier()
            in_use.clear()
            for parts in phases.values():
                parts.clear()

        def setup_sync(sp):
            for dst, src in loads:
                sp.dma_start(dst, src).then_inc(s_const, 16)
            sp.wait_ge(s_zero, 1)
            for dst, src in diag:
                sp.dma_start(dst, src).then_inc(s_const, 16)

        def setup_pool(pool):
            nc.gpsimd.memset(gate_w[:, :, :, :], 0.0).then_inc(s_zero, 1)
            nc.gpsimd.memset(zeros[:, :], 0.0).then_inc(s_zero, 1)
            nc.gpsimd.memset(pool_cell[:, :], 0.0).then_inc(s_pow, 1)
            nc.gpsimd.memset(minus_half[:, :, :], -0.5).then_inc(s_pow, 1)
            pool.wait_ge(s_pow, 2)

        def setup_scalar(act):
            act.wait_ge(s_vec, 1)
            nc.scalar.activation(sp_tmp[:, 0, :], vec[:, V_A:V_A + 2], ACT.Abs).then_inc(s_act_setup, 1)
            act.wait_ge(s_act_setup, 1)
            nc.scalar.activation(sp_tmp[:, 1, :], sp_tmp[:, 0, :], ACT.Exp, scale=-1.0).then_inc(s_act_setup, 1)
            act.wait_ge(s_act_setup, 2)
            nc.scalar.activation(sp_tmp[:, 2, :], sp_tmp[:, 1, :], ACT.Ln, bias=1.0).then_inc(s_act_setup, 1)

        def setup_tensor(pe):
            pe.wait_ge(s_const, 16 * N_EARLY)
            nc.tensor.transpose(bank(7)[:, 0:VEC_ROWS], vec_rows[:, :], ident[0:VEC_ROWS, 0:VEC_ROWS]).then_inc(s_vecT, 1)

        def setup_vector(dve):
            dve.wait_ge(s_vecT, 1)
            nc.vector.tensor_copy(vec[:, :], bank(7)[:, 0:VEC_ROWS]).then_inc(s_vec, 1)
            dve.wait_ge(s_vec, 1)
            nc.vector.tensor_scalar(hgate_b[:, :], vec[:, V_BIN:V_BIN + 4], 0.5, None, ALU.mult).then_inc(s_setup, 1)
            nc.vector.tensor_scalar(kb_par[:, 0, :], vec[:, V_BK:V_BK + 2], table("even_heads"), None,
                                    ALU.mult).then_inc(s_setup, 1)
            nc.vector.tensor_scalar(kb_par[:, 1, :], vec[:, V_BK:V_BK + 2], table("odd_heads"), None,
                                    ALU.mult).then_inc(s_setup, 1)
            nc.vector.tensor_scalar(ndecay[:, :], vec[:, V_A:V_A + 2], 0.0, MIN_DECAY, ALU.max,
                                    ALU.add).then_inc(s_setup, 1)
            nc.vector.tensor_copy(ident_bf[:, :], ident).then_inc(s_setup, 1)
            nc.vector.tensor_copy(causal_bf[:, :], table("causal")).then_inc(s_setup, 1)
            nc.vector.memset(ones_row[:, :], 1.0).then_inc(s_setup, 1)
            dve.wait_ge(s_act_setup, 3)
            dve.wait_ge(s_setup, 4)
            nc.vector.tensor_tensor(ndecay[:, :], ndecay[:, :], sp_tmp[:, 2, :], ALU.add).then_inc(s_setup, 1)
            dve.wait_ge(s_setup, 8)
            nc.vector.tensor_scalar(ndecay[:, :], ndecay[:, :], -0.5, None, ALU.mult).then_inc(s_setup, 1)
        N_SETUP = 10

        phases["sync"].append(setup_sync)
        phases["gpsimd"].append(setup_pool)
        phases["scalar"].append(setup_scalar)
        phases["tensor"].append(setup_tensor)
        phases["vector"].append(setup_vector)

        def ln_bn(dve, u, src, stats, sems):
            for b in range(UB):
                ins = nc.vector.bn_stats(stats[:, b, 0:6], src[:, b, :])
            ins.then_inc(sems[0], 1)

        def ln_moments(dve, u, stats, sems, cell=0):
            s_st, s_ag, s_rs, s_out = sems
            dve.wait_ge(s_st, u.n * 2 + 1)
            nc.vector.memset(wait_cell[:, cell:cell + 1], 0.0)
            for b in range(UB):
                ins = nc.vector.bn_aggr(stats[:, b, 6:8], stats[:, b, 0:6])
            ins.then_inc(s_st, 1)

        def ln_eps(dve, u, stats, sems):
            done(dve, sems[0], u, 2)
            nc.vector.tensor_scalar(stats[:, :, 9:10], stats[:, :, 7:8], LN_EPS, None, ALU.add).then_inc(sems[1], 1)

        def ln_stats(dve, u, src, stats, sems):
            ln_bn(dve, u, src, stats, sems)
            ln_moments(dve, u, stats, sems)
            ln_eps(dve, u, stats, sems)

        def ln_apply(dve, u, src, dst, stats, sems):
            s_st, s_ag, s_rs, s_out = sems
            done(dve, s_rs, u)
            for b in range(UB):
                ins = nc.vector.tensor_scalar(dst[:, b, :], src[:, b, :], stats[:, b, 6:7], stats[:, b, 8:9],
                                              ALU.subtract, ALU.mult)
            ins.then_inc(s_out, 1)

        def layer_norm(dve, u, src, dst, stats, sems):
            ln_stats(dve, u, src, stats, sems)
            ln_apply(dve, u, src, dst, stats, sems)

        def rstd(pool, u, stats, sems):
            s_st, s_ag, s_rs, s_out = sems
            done(pool, s_ag, u)
            nc.gpsimd.tensor_tensor(stats[:, :, 8:9], stats[:, :, 9:10], minus_half[:, :, :], ALU.pow).then_inc(s_rs, 1)

        def to_feature(dst, src):
            for c in range(NC_):
                for b in range(UB):
                    ins = nc.tensor.transpose(dst[:, c * T + b * S:c * T + (b + 1) * S],
                                              src[:, b, c * P:(c + 1) * P], ident)
            return ins

        def chunks(ap):
            return ap.rearrange("p (c t) -> p c t", c=NC_)

        def seqs(ap):
            return ap.rearrange("p (b d) -> p b d", b=UB)


        def low_part(dst, src, high):
            return nc.vector.tensor_tensor(dst, src, high.bitcast(F32), ALU.subtract)

        def matmul_split(dst, left, right, start, stop):
            for k, (a_, b_) in enumerate(((0, 0), (0, 1), (1, 0))):
                ins = nc.tensor.matmul(dst, left[a_], right[b_], start=start and k == 0, stop=stop and k == 2,
                                       skip_group_check=True)
            return ins

        def add(engine, part):
            phases[engine].append(part)

        pool_cell = sb("pool_cell", [1, 8])

        def carry(pool, k):
            nc.gpsimd.tensor_tensor(pool_cell[:, k:k + 1], pool_cell[:, 7:8], pool_cell[:, 7:8], ALU.add)

        A = {}
        for n in ("x", "cx"):
            A[n] = arena_x.take([P, 2, UB, D])
        for n in ("xF", "cF", "thx", "tha", "a", "ash", "m", "g", "pp", "w", "r1", "x1F", "qr", "kr", "x2F"):
            A[n] = arena_x.take([P, 2, NC_, T])
        A["rp"] = arena_x.take([P, NC_, T])
        A["t1"] = arena_x.take([P, NC_, T])
        A["t2"] = arena_x.take([P, NC_, T])
        for n in ("x1", "x2", "v"):
            A[n] = arena_x.take([P, 2, UB, D])
        A["r2"] = arena_x.take([P, UB, D])
        A["sc"] = arena_x.take([P, 2, UB, S])
        A_st1 = sb("A_st1", [P, UB, 10])
        A_st2 = sb("A_st2", [P, UB, 10])

        a_in = sem2("a_in")
        aT_x, aT_c, aT_r1, aT_x1, aT_x2 = (sem("aT_" + n) for n in ("x", "c", "r1", "x1", "x2"))
        a_gate, a_k, a_v, a_q, a_score, a_ret, a_logit = (
            sem("a_" + n) for n in ("gate", "k", "v", "q", "score", "ret", "logit"))
        a_xF, a_cF, a_thx, a_tha, a_dec, a_vs, a_x1F, a_x2F, a_lg = (
            sem("a_" + n) for n in ("xF", "cF", "thx", "tha", "dec", "vs", "x1F", "x2F", "lg"))
        a_sh, a_min, a_m1, a_m2, a_g1, a_g2, a_p, a_rp, a_w, a_s, a_h, a_r1 = (
            sem("a_" + n) for n in ("sh", "min", "m1", "m2", "g1", "g2", "p", "rp", "w", "s", "h", "r1"))
        a_qt, a_qr, a_kt, a_kr, a_sc, a_r2 = (sem("a_" + n) for n in ("qt", "qr", "kt", "kr", "sc", "r2"))
        ln1 = [sem("ln1_" + n) for n in ("st", "ag", "rs", "out")]
        ln2 = [sem("ln2_" + n) for n in ("st", "ag", "rs", "out")]
        a_x1, a_x2 = ln1[3], ln2[3]
        a_st = sem2("a_st")
        A_LAG = 3

        def a_sync(sp):
            def step(t):
                u = t.at(0, UNITS)
                if u:
                    done(sp, aT_x, u.back(2))
                    done(sp, aT_c, u.back(2))
                    sp.dma_start(A["x"][:, u.p, :, :], x_u[u.n]).then_inc(a_in[u.p], 16)
                    sp.dma_start(A["cx"][:, u.p, :, :], ctx_u[u.n]).then_inc(a_in[u.p], 16)
                u = t.at(3, UNITS)
                if u:
                    done(sp, a_x2, u)
                    sp.dma_start(x2_u[u.n], A["x2"][:, u.p, :, :]).then_inc(a_st[u.p], 16)
                if t.fixed and t.n == 2:
                    for dst, src in late:
                        sp.dma_start(dst, src).then_inc(s_late, 16)
            pipelined(sp, UNITS, A_LAG, step)

        def a_tensor(pe):
            pe.wait_ge(s_vec, 1)

            def project(dst, name, src, par=None, odd=None):
                for m in range(NC_):
                    for c in range(NC_):
                        ws = w[name][:, c, m::2] if par else w[name][:, c, m * P:(m + 1) * P]
                        ins = nc.tensor.matmul(dst[:, m * T:(m + 1) * T], ws, src[:, c, :],
                                               start=(c == 0), stop=(c == NC_ - 1))
                return ins

            def step(t):
                u0, u1, u2, u3 = (t.at(k, UNITS) for k in range(4))
                if u0:
                    landed(pe, a_in, u0, 2)
                    done(pe, a_x2F, u0.back(4))
                    to_feature(bank(1), A["cx"][:, u0.p]).then_inc(aT_c, 1)
                    done(pe, a_x1F, u0.back(2))
                    to_feature(bank(0), A["x"][:, u0.p]).then_inc(aT_x, 1)
                    done(pe, a_cF, u0)
                    done(pe, a_kt, u0.back(1))
                    project(bank(5), "L0_xattn_Wk", A["cF"][:, u0.p], par=True).then_inc(a_k, 1)
                if u3:
                    done(pe, a_x2, u3)
                    done(pe, a_cF, u0 or u3)
                    to_feature(bank(1), A["x2"][:, u3.p]).then_inc(aT_x2, 1)
                if u0:
                    done(pe, a_xF, u0)
                    done(pe, a_dec, u0.back(1))
                    done(pe, a_thx, u0.back(1))
                    done(pe, a_tha, u0.back(1))
                    for g in range(2):
                        for c in range(NC_):
                            ins = nc.tensor.matmul(bank(2 + g)[:, c * T:(c + 1) * T], gate_w[:, g, c, :],
                                                   A["xF"][:, u0.p, c, :], start=True, stop=True)
                    ins.then_inc(a_gate, 1)
                if u2:
                    done(pe, a_qr, u2)
                    done(pe, a_kr, u2)
                    done(pe, a_lg, u2.back(2))
                    for b in range(UB):
                        for c in range(NC_):
                            ins = nc.tensor.matmul(bank(7)[:, b * S:(b + 1) * S],
                                                   A["kr"][:, u2.p, c, b * S:(b + 1) * S],
                                                   A["qr"][:, u2.p, c, b * S:(b + 1) * S],
                                                   start=(c == 0), stop=(c == NC_ - 1))
                    ins.then_inc(a_score, 1)
                if u1:
                    done(pe, a_r1, u1)
                    done(pe, a_qt, u1.back(1))
                    for b in range(UB):
                        for c in range(NC_):
                            ins = nc.tensor.transpose(bank(4)[:, b * D + c * P:b * D + (c + 1) * P],
                                                      A["r1"][:, u1.p, c, b * S:(b + 1) * S], ident)
                    ins.then_inc(aT_r1, 1)
                if u2:
                    done(pe, a_sc, u2)
                    done(pe, a_vs, u1 or u2)
                    for b in range(UB):
                        ins = nc.tensor.matmul(bank(6)[:, b * D:(b + 1) * D], A["sc"][:, u2.p, b, :],
                                               A["v"][:, u2.p, b, :], start=True, stop=True)
                    ins.then_inc(a_ret, 1)
                if u1:
                    done(pe, a_x1, u1)
                    done(pe, a_xF, u0 or u1)
                    to_feature(bank(0), A["x1"][:, u1.p]).then_inc(aT_x1, 1)
                if u0:
                    done(pe, a_r2, u0.back(2))
                    for b in range(UB):
                        for c in range(NC_):
                            ins = nc.tensor.matmul(bank(6)[:, b * D:(b + 1) * D],
                                                   A["cF"][:, u0.p, c, b * S:(b + 1) * S],
                                                   w["L0_xattn_Wv"][:, c, :], start=(c == 0), stop=(c == NC_ - 1))
                    ins.then_inc(a_v, 1)
                if u1:
                    done(pe, a_x1F, u1)
                    project(bank(4), "L0_xattn_Wq", A["x1F"][:, u1.p], par=True).then_inc(a_q, 1)
                if u3:
                    done(pe, a_x2F, u3)
                    done(pe, a_sc, u2 or u3)
                    for b in range(UB):
                        for c in range(NC_):
                            ins = nc.tensor.matmul(bank(7)[:, 256 + b * E0:256 + (b + 1) * E0],
                                                   A["x2F"][:, u3.p, c, b * S:(b + 1) * S], w_route[:, c, :],
                                                   start=(c == 0), stop=(c == NC_ - 1))
                    ins.then_inc(a_logit, 1)
            pipelined(pe, UNITS, A_LAG, step)

        def a_scalar(act):
            act.wait_ge(s_setup, 9)

            def step(t):
                u0, u1, u3 = t.at(0, UNITS), t.at(1, UNITS), t.at(3, UNITS)
                if u0:
                    done(act, aT_c, u0)
                    done(act, a_v, u0.back(2))
                    nc.scalar.activation(A["cF"][:, u0.p], chunks(bank(1)), ACT.Copy).then_inc(a_cF, 1)
                    done(act, aT_x, u0)
                    done(act, a_r1, u0.back(2))
                    nc.scalar.activation(A["xF"][:, u0.p], chunks(bank(0)), ACT.Copy).then_inc(a_xF, 1)
                if u3:
                    done(act, aT_x2, u3)
                    done(act, a_logit, u3.back(2))
                    nc.scalar.activation(A["x2F"][:, u3.p], chunks(bank(1)), ACT.Copy).then_inc(a_x2F, 1)
                if u0:
                    done(act, a_gate, u0)
                    done(act, a_g1, u0.back(2))
                    for c in range(NC_):
                        ins = nc.scalar.activation(A["tha"][:, u0.p, c, :], bank(3)[:, c * T:(c + 1) * T], ACT.Tanh,
                                                   bias=hgate_b[:, 2 + c:3 + c], scale=0.5)
                    ins.then_inc(a_tha, 1)
                    for c in range(NC_):
                        ins = nc.scalar.activation(A["thx"][:, u0.p, c, :], bank(2)[:, c * T:(c + 1) * T], ACT.Tanh,
                                                   bias=hgate_b[:, c:c + 1], scale=0.5)
                    ins.then_inc(a_thx, 1)
                    done(act, a_tha, u0)
                    done(act, a_m1, u0.back(2))
                    for c in range(NC_):
                        ins = nc.scalar.activation(A["a"][:, u0.p, c, :], A["tha"][:, u0.p, c, :], ACT.Exp,
                                                   bias=ndecay[:, c:c + 1], scale=ndecay[:, c:c + 1])
                    ins.then_inc(a_dec, 1)
                if u1:
                    done(act, aT_x1, u1)
                    done(act, a_q, u1.back(2))
                    nc.scalar.activation(A["x1F"][:, u1.p], chunks(bank(0)), ACT.Copy).then_inc(a_x1F, 1)
                if u0:
                    done(act, a_v, u0)
                    done(act, a_ret, u0.back(2))
                    nc.scalar.activation(A["v"][:, u0.p], seqs(bank(6)), ACT.Copy).then_inc(a_vs, 1)
                if u3:
                    done(act, a_logit, u3)
                    nc.scalar.activation(logits[:, bass.ds(u3.n * UB, UB), :],
                                         bank(7)[:, 256:256 + UB * E0].rearrange("p (b e) -> p b e", e=E0),
                                         ACT.Copy).then_inc(a_lg, 1)
                if t.fixed and 2 <= t.n < 6:
                    if t.n == 2:
                        act.wait_ge(s_zero, 2)
                    n = P * ZW // D
                    part = SLOTS // n // 4
                    for k in range((t.n - 2) * part, (t.n - 1) * part):
                        act.dma_start(disp_d[k * n:(k + 1) * n, :].rearrange("(p r) d -> p (r d)", p=P),
                                      zeros[:, :]).then_inc(s_prefill, 16)
                if u0:
                    done(act, a_m2, u0)
                    nc.scalar.activation(A["m"][:, u0.p], A["m"][:, u0.p], ACT.Sqrt).then_inc(a_rt, 1)
            pipelined(act, UNITS, A_LAG, step)

        def a_vector(dve):
            def bc(name, n):
                return table(name)[:, None, :].broadcast_to([P, n, S])

            def xpos(src, cos, sin, s_t):
                t1, t2 = A["t1"], A["t2"]
                q = src.rearrange("p (c b s) -> p c b s", c=NC_, b=UB)
                nc.vector.tensor_tensor(t1[:, :, :].rearrange("p c (b s) -> p (c b) s", b=UB),
                                        src.rearrange("p (n s) -> p n s", s=S), bc(cos, NC_ * UB), ALU.mult)
                for c in range(NC_):
                    ins = nc.vector.tensor_tensor(t2[:, 1 - c, :].rearrange("p (b s) -> p b s", b=UB), q[:, c],
                                                  bc(sin, UB), ALU.mult)
                ins.then_inc(s_t, 1)

            def xpos_sums(u, dst, s_t, s_r):
                done(dve, s_t, u)
                nc.vector.tensor_tensor(dst[:, 0, :], A["t1"][:, 0, :], A["t2"][:, 0, :], ALU.subtract)
                nc.vector.tensor_tensor(dst[:, 1, :], A["t1"][:, 1, :], A["t2"][:, 1, :], ALU.add).then_inc(s_r, 1)

            def step(t):
                u0, u1, u2 = t.at(0, UNITS), t.at(1, UNITS), t.at(2, UNITS)
                if u0:
                    p = u0.p
                    a4 = A["a"][:, p].rearrange("p c (b s) -> p (c b) s", b=UB)
                    sh4 = A["ash"][:, p].rearrange("p c (b s) -> p (c b) s", b=UB)
                    flat = {n: A[n][:, p].rearrange("p c t -> p (c t)") for n in ("ash", "pp", "w")}
                    done(dve, a_k, u0)
                    done(dve, a_kr, u0.back(1))
                    done(dve, a_qr, u0.back(2))
                    xpos(bank(5), "xpos_k_cos", "xpos_k_sin", a_kt)
                if u2:
                    done(dve, a_score, u2)
                    done(dve, a_ret, u2.back(2))
                    nc.vector.tensor_tensor(A["sc"][:, u2.p], bank(7)[:, 0:UB * S].rearrange("p (b s) -> p b s", b=UB),
                                            bc("decay_t", UB), ALU.mult).then_inc(a_sc, 1)
                if u1:
                    done(dve, aT_r1, u1)
                    ln_stats(dve, u1, seqs(bank(4)), A_st1, ln1)
                if u0:
                    done(dve, a_dec, u0)
                    done(dve, a_thx, u0)
                    nc.vector.tensor_scalar(sh4[:, :, 1:S], a4[:, :, 0:S - 1], 1.0 - A_EPS, None,
                                            ALU.min).then_inc(a_sh, 1)
                    done(dve, a_sh, u0)
                    nc.vector.tensor_scalar(A["a"][:, p], A["a"][:, p], 1.0 - A_EPS, None, ALU.min).then_inc(a_min, 1)
                if u1:
                    done(dve, aT_x1, u1.back(2))
                    done(dve, a_r2, u1.back(2))
                    ln_apply(dve, u1, seqs(bank(4)), A["x1"][:, u1.p], A_st1, ln1)
                if u2:
                    done(dve, a_ret, u2)
                    done(dve, a_x2, u2.back(1))
                    nc.vector.tensor_tensor(A["r2"][:, :, :], seqs(bank(6)), A["x1"][:, u2.p], ALU.add).then_inc(a_r2, 1)
                    done(dve, a_r2, u2)
                    ln_stats(dve, u2, A["r2"], A_st2, ln2)
                if u0:
                    nc.vector.scalar_tensor_tensor(A["g"][:, p], A["thx"][:, p], 1.0, A["xF"][:, p], ALU.add,
                                                   ALU.mult).then_inc(a_g1, 1)
                    done(dve, a_min, u0)
                    done(dve, a_r1, u0.back(2))
                    nc.vector.scalar_tensor_tensor(A["m"][:, p], A["a"][:, p], -0.25, A["a"][:, p], ALU.mult,
                                                   ALU.mult).then_inc(a_m1, 1)
                    done(dve, a_m1, u0)
                    nc.vector.tensor_scalar(A["m"][:, p], A["m"][:, p], 0.25, 0.25 * A_EPS, ALU.add,
                                            ALU.max).then_inc(a_m2, 1)
                    done(dve, a_sh, u0)
                    nc.vector.tensor_tensor_scan(flat["pp"], flat["ash"], table("floor"), 1.0, ALU.mult,
                                                 ALU.max).then_inc(a_p, 1)
                    done(dve, a_p, u0)
                    nc.vector.reciprocal(A["rp"][:, :, :], A["pp"][:, p]).then_inc(a_rp, 1)
                if u2:
                    done(dve, aT_x2, u2.back(2))
                    landed(dve, a_st, u2.back(2))
                    ln_apply(dve, u2, A["r2"], A["x2"][:, u2.p], A_st2, ln2)
                if u1:
                    done(dve, a_q, u1)
                    done(dve, a_kr, u0 or u1)
                    xpos(bank(4), "xpos_q_cos", "xpos_q_sin", a_qt)
                    xpos_sums(u1, A["qr"][:, u1.p], a_qt, a_qr)
                if t.fixed and t.n == 4:
                    dve.wait_ge(s_late, 16 * N_LATE)
                    nc.vector.tensor_scalar(mask_row[:, :], mask_u8[:, :], -BIG, None, ALU.mult).then_inc(s_setup, 1)
                if u0:
                    done(dve, a_rt, u0)
                    done(dve, a_g1, u0)
                    nc.vector.tensor_tensor(A["g"][:, p], A["m"][:, p], A["g"][:, p], ALU.mult).then_inc(a_g2, 1)
                    done(dve, a_g2, u0)
                    done(dve, a_rp, u0)
                    nc.vector.scalar_tensor_tensor(A["w"][:, p], A["g"][:, p], SCAN_EPS, A["rp"][:, :, :], ALU.add,
                                                   ALU.mult).then_inc(a_w, 1)
                    done(dve, a_w, u0)
                    nc.vector.tensor_tensor_scan(flat["w"], table("keep"), flat["w"], 0.0, ALU.mult,
                                                 ALU.add).then_inc(a_s, 1)
            nc.vector.memset(A["ash"][:, :, :, :], 0.0).then_inc(a_sh0, 1)
            dve.wait_ge(a_sh0, 1)
            pipelined(dve, UNITS, A_LAG, step)
        a_sh0, a_rt = sem("a_sh0"), sem("a_rt")

        def a_gpsimd(pool):
            def step(t):
                u0, u1, u2 = t.at(0, UNITS), t.at(1, UNITS), t.at(2, UNITS)
                if u0:
                    kr = A["kr"][:, u0.p]
                    done(pool, a_kt, u0)
                    done(pool, a_score, u0.back(2))
                    nc.gpsimd.tensor_tensor(kr[:, 0, :], A["t1"][:, 0, :], A["t2"][:, 0, :], ALU.subtract)
                    nc.gpsimd.tensor_tensor(kr[:, 1, :], A["t1"][:, 1, :], A["t2"][:, 1, :], ALU.add).then_inc(a_kr, 1)
                if u1:
                    rstd(pool, u1, A_st1, ln1)
                if u2:
                    rstd(pool, u2, A_st2, ln2)
                if u0:
                    done(pool, a_s, u0)
                    nc.gpsimd.tensor_tensor(A["m"][:, u0.p], A["pp"][:, u0.p], A["w"][:, u0.p], ALU.mult).then_inc(a_h, 1)
                    done(pool, a_h, u0)
                    done(pool, aT_r1, u0.back(2))
                    nc.gpsimd.tensor_tensor(A["r1"][:, u0.p], A["m"][:, u0.p], A["xF"][:, u0.p],
                                            ALU.add).then_inc(a_r1, 1)
            pipelined(pool, UNITS, A_LAG, step)

        phases["gpsimd"].append(a_gpsimd)

        phases["sync"].append(a_sync)
        phases["tensor"].append(a_tensor)
        phases["scalar"].append(a_scalar)
        phases["vector"].append(a_vector)
        KB = TOP0 * B
        R = {}
        arena_x.reset()
        for n in ("eq", "rk", "l2"):
            R[n] = arena_x.take([P, B, E0])
        R["oh"] = arena_x.take([P, TOP0, B, E0])
        R["tot"] = arena_x.take([P, E0, KB])
        R["inc"] = arena_x.take([P, E0, KB])
        R["pos"] = arena_x.take([P, KB, E0])
        R["sel"] = arena_x.take([P, KB, E0])
        for n in ("m1", "m2", "mr", "ex"):
            R[n] = arena_x.take([P, B])
        for n in ("posk", "basek", "valid", "slot", "slot2"):
            R[n] = arena_x.take([P, TOP0, B])
        R["x"] = arena_x.take([P, 2, UB, D])
        R["idx"] = arena_x.take([P, 2, TOP0, UB]).bitcast(I32)

        r_v = sem("r_v")
        r_ex, r_rank, r_slots = sem("r_ex"), sem("r_rank"), sem("r_slots")
        r_in, r_idx, r_sc = sem2("r_in"), sem("r_idx"), sem2("r_sc")
        r_go = sem("r_go")
        RV_GAP, RV_ONEHOT = 8, 9
        per_parity = UNITS // 2

        def r_vector(dve):
            k = [0]

            def then(ins):
                k[0] += 1
                ins.then_inc(r_v, 1)
                dve.wait_ge(r_v, k[0])

            def over_e(ap, n=B):
                return ap[:, :, None].broadcast_to([P, n, E0])

            def first_max(src, m, oh):
                then(nc.vector.tensor_reduce(m, src, AX, ALU.max))
                then(nc.vector.tensor_tensor(R["eq"], src, over_e(m), ALU.is_equal))
                then(nc.vector.tensor_tensor(R["rk"], R["eq"], table("rank")[:, None, :].broadcast_to([P, B, E0]),
                                             ALU.mult))
                then(nc.vector.tensor_reduce(R["mr"], R["rk"], AX, ALU.max))
                then(nc.vector.tensor_tensor(oh, R["rk"], over_e(R["mr"]), ALU.is_equal))

            dve.wait_ge(a_lg, UNITS)
            dve.wait_ge(aT_x2, UNITS)
            first_max(logits[:, :, :], R["m1"], R["oh"][:, 0])
            then(nc.vector.scalar_tensor_tensor(R["l2"], R["oh"][:, 0], -BIG, logits[:, :, :], ALU.mult, ALU.add))
            first_max(R["l2"], R["m2"], R["oh"][:, 1])
            then(nc.vector.tensor_tensor(R["m2"], R["m2"], R["m1"], ALU.subtract))
            k_gap = k[0]
            dve.wait_ge(r_ex, 1)
            then(nc.vector.tensor_scalar(R["m1"], R["ex"], 1.0, None, ALU.add))
            then(nc.vector.reciprocal(gates[:, 0, :], R["m1"]))
            then(nc.vector.tensor_tensor(gates[:, 1, :], gates[:, 0, :], R["ex"], ALU.mult))
            dve.wait_ge(r_rank, 1)
            then(nc.vector.tensor_copy(R["tot"], bank(1).rearrange("p (k e) -> p e k", e=E0)))
            tot, inc = (R[n].rearrange("p e k -> p (e k)") for n in ("tot", "inc"))
            then(nc.vector.tensor_tensor_scan(inc, table("keep_seg"), tot, 0.0, ALU.mult, ALU.add))
            then(nc.vector.tensor_tensor(tot, inc, tot, ALU.subtract))
            then(nc.vector.tensor_tensor(R["pos"], bank(0).rearrange("p (k e) -> p k e", e=E0),
                                         R["tot"].rearrange("p e k -> p k e"), ALU.add))
            oh = R["oh"].rearrange("p c b e -> p (c b) e")
            flat = {n: R[n].rearrange("p c b -> p (c b)") for n in ("posk", "basek", "valid", "slot", "slot2")}
            then(nc.vector.tensor_tensor(R["sel"], R["pos"], oh, ALU.mult))
            then(nc.vector.tensor_reduce(flat["posk"], R["sel"], AX, ALU.add))
            then(nc.vector.tensor_tensor(R["sel"], oh, table("base")[:, None, :].broadcast_to([P, KB, E0]), ALU.mult))
            then(nc.vector.tensor_reduce(flat["basek"], R["sel"], AX, ALU.add))
            then(nc.vector.tensor_scalar(flat["valid"], flat["posk"], float(CAP), None, ALU.is_lt))
            then(nc.vector.tensor_tensor(gates[:, :, :], gates[:, :, :], R["valid"], ALU.mult))
            then(nc.vector.tensor_tensor(flat["slot"], flat["posk"], flat["valid"], ALU.mult))
            then(nc.vector.tensor_tensor(flat["slot"], flat["slot"], flat["basek"], ALU.add))
            then(nc.vector.tensor_copy(slot_g[:, :, :], R["slot"]))
            then(nc.vector.tensor_scalar(flat["slot2"], flat["valid"], -4.0 * SLOTS, 4.0 * SLOTS, ALU.mult, ALU.add))
            then(nc.vector.tensor_tensor(flat["slot2"], flat["slot2"], flat["slot"], ALU.add))
            nc.vector.tensor_copy(slot_s[:, :, :], R["slot2"]).then_inc(r_slots, 1)
            return k_gap

        def r_scalar(act):
            act.wait_ge(r_v, 12)
            nc.scalar.activation(R["ex"], R["m2"], ACT.Exp).then_inc(r_ex, 1)

        def r_tensor(pe):
            pe.wait_ge(r_v, 11)
            pe.wait_ge(a_x1F, UNITS)
            pe.wait_ge(a_x2F, UNITS)
            oh = R["oh"].rearrange("p c b e -> p (c b e)")
            nc.tensor.matmul(bank(0), table("before"), oh, start=True, stop=True)
            nc.tensor.matmul(bank(1), table("ones"), oh, start=True, stop=True).then_inc(r_rank, 1)

        def r_sync(sp):
            sp.wait_ge(a_st[0], 16 * per_parity)
            sp.wait_ge(a_st[1], 16 * per_parity)
            sp.wait_ge(a_r1, UNITS)
            sp.wait_ge(a_score, UNITS)

            def step(t):
                if not (t.fixed and t.n < 2):
                    landed(sp, r_sc, t.back(2), 4)
                sp.dma_start(R["x"][:, t.p], x2_u[t.n]).then_inc(r_in[t.p], 16)
            pipelined(sp, UNITS, 0, step)

        def r_gpsimd(pool):
            pool.wait_ge(s_prefill, 16 * (SLOTS * D // (P * ZW)))
            pool.wait_ge(r_slots, 1)

            def step(t):
                landed(pool, r_in, t)
                landed(pool, r_sc, t.back(2), 4)
                carry(pool, 0)
                nc.gpsimd.tensor_copy(R["idx"][:, t.p], slot_s[:, :, bass.ds(t.n * UB, UB)]).then_inc(r_idx, 1)
                done(pool, r_idx, t)
                carry(pool, 1)
                for c in range(TOP0):
                    for b in range(UB):
                        nc.gpsimd.indirect_dma_start(
                            out=disp_d, out_offset=bass.IndirectOffsetOnAxis(ap=R["idx"][:, t.p, c, b:b + 1], axis=0),
                            in_=R["x"][:, t.p, b, :], in_offset=None, bounds_check=SLOTS - 1,
                            oob_is_err=False).then_inc(r_sc[t.p], 16)
            pipelined(pool, UNITS, 0, step)

        add("vector", r_vector)
        add("scalar", r_scalar)
        add("tensor", r_tensor)
        add("sync", r_sync)
        add("gpsimd", r_gpsimd)

        MT = 512
        MS = MT // P
        TILES = SLOTS // MT
        HC = HID0 // P
        M = {}
        arena_y.reset()
        arena_x.reset()
        M["x"] = arena_x.take([P, 2, MS, D])
        M["y"] = arena_x.take([P, 2, MS, D])
        M["hr"] = arena_x.take([P, 4, MT])
        M["xF"] = arena_x.take([P, 2, 2, NC_, MT], "m_xF_parts")
        M["h"] = arena_x.take([P, 2, HC, MT], "m_h_parts")
        WN = NC_ * HID0
        M["w"] = arena_y.take([P, 2, 2, WN])
        M["w_high"] = arena_y.view("m_w_high", 0, [P, 2, 2, WN])
        M["w1_low"] = arena_y.take([P, 2, WN], "m_w1_low")
        M["w2_low"] = arena_x.take([P, 2, WN], "m_w2_low")
        M["piece"] = arena_y.take([P, WN // 4], "m_piece")
        b1_e = sb("b1_e", [P, 2, HC])
        m_w, m_b1 = sem2("m_w"), sem("m_b1")
        m_in, m_T, m_xh, m_xF = sem2("m_in"), sem("m_T"), sem("m_xh"), sem("m_xF")
        m_hp, m_hs, m_hh, m_hl, m_yp, m_y = (sem("m_" + n) for n in ("hp", "hs", "hh", "hl", "yp", "y"))
        m_wa, m_wb, m_ws = sem("m_wa"), sem("m_wb"), sem("m_ws")
        m_st = sem2("m_st")
        disp_t = disp_d.rearrange("(n q p) d -> n p q d", p=P, q=MS)
        y_t = y_d.rearrange("(n q p) d -> n p q d", p=P, q=MS)
        w1_e = a["L0_ffn_w1"].rearrange("e (c p) h -> e p c h", p=P)
        w2_e = a["L0_ffn_w2"].rearrange("e (c p) d -> e p c d", p=P)
        PIECES, PW = 4, WN // 4

        def m_weights(sp, v):
            buf = (v.c // 2) % 2
            sp.dma_start(M["w"][:, buf, 0].rearrange("p (c h) -> p c h", c=NC_), w1_e[v.div(2)]).then_inc(m_w[buf], 16)
            sp.dma_start(M["w"][:, buf, 1].rearrange("p (c d) -> p c d", c=HC), w2_e[v.div(2)]).then_inc(m_w[buf], 16)

        def m_sync(sp):
            sp.wait_ge(s_setup, N_SETUP)
            m_weights(sp, Unit(0, 0))
            m_weights(sp, Unit(0, 2))
            for k in range(2):
                sp.wait_ge(r_sc[k], 16 * 4 * per_parity)

            def step(t):
                u = t.at(0, TILES)
                if u and not (u.fixed and u.n >= TILES):
                    done(sp, m_T, u.back(2))
                    sp.dma_start(M["x"][:, u.p], disp_t[u.n]).then_inc(m_in[u.p], 16)
                v = t.back(-2)
                if t.c % 2 == 0 and not (t.fixed and not 2 <= t.n < TILES - 2):
                    done(sp, m_yp, t.back(1))
                    m_weights(sp, v)
                u = t.at(2, TILES)
                if u:
                    done(sp, m_y, u, 2)
                    sp.dma_start(y_t[u.n], M["y"][:, u.p]).then_inc(m_st[u.p], 16)
            pipelined(sp, TILES, 2, step, unroll=4, peel=4)

        def m_tensor(pe):
            pe.wait_ge(r_slots, 1)
            for s in (a_dec, a_thx, a_qr, a_kr, a_r2, a_sc, a_lg):
                pe.wait_ge(s, UNITS)

            def step(t):
                u = t.at(1, TILES)
                if u:
                    wb = (u.c // 2) % 2
                    w1 = [x.rearrange("p (c h) -> p c h", c=NC_) for x in (M["w_high"][:, wb, 0], M["w1_low"][:, wb])]
                    w2 = [x.rearrange("p (c d) -> p c d", c=HC) for x in (M["w_high"][:, wb, 1], M["w2_low"][:, wb])]
                    pe.wait_ge(m_ws, (u.div(2) + 1) * 2 * PIECES)
                    done(pe, m_xF, u, 2)
                    for m in range(HC):
                        if m >= 4:
                            pe.wait_ge(m_hh, u.n * HC + m - 3)
                        else:
                            done(pe, m_hh, u.back(1), HC)
                        for c in range(NC_):
                            ins = matmul_split(bank(2 + m % 4), [x[:, c, m * P:(m + 1) * P] for x in w1],
                                               [M["xF"][:, u.p, k, c, :] for k in range(2)], c == 0, c == NC_ - 1)
                        ins.then_inc(m_hp, 1)
                u0 = t.at(0, TILES)
                if u0:
                    landed(pe, m_in, u0)
                    done(pe, m_xF, u0.back(1), 2)
                    for c in range(NC_):
                        for q in range(MS):
                            ins = nc.tensor.transpose(bank(c)[:, q * P:(q + 1) * P],
                                                      M["x"][:, u0.p, q, c * P:(c + 1) * P], ident)
                    ins.then_inc(m_T, 1)
                if u:
                    done(pe, m_y, u.back(1), 2)
                    for m in range(HC):
                        pe.wait_ge(m_hl, u.n * HC + (m + 1))
                        for q in range(MS):
                            ins = matmul_split(bank(6 + q // 2)[:, (q % 2) * D:(q % 2 + 1) * D],
                                               [M["h"][:, k, m, q * P:(q + 1) * P] for k in range(2)],
                                               [x[:, m, :] for x in w2], m == 0 and q % 2 == 0, m == HC - 1)
                    ins.then_inc(m_yp, 1)
            pipelined(pe, TILES, 1, step, unroll=4, peel=4)

        def m_scalar(act):
            def step(t):
                u = t.at(1, TILES)
                if u:
                    if u.c % 2 == 0:
                        act.wait_ge(m_b1, u.div(2) + 1)
                    for m in range(HC):
                        if m >= 4:
                            act.wait_ge(m_hl, u.n * HC + m - 3)
                        else:
                            done(act, m_hl, u.back(1), HC)
                        act.wait_ge(m_hp, u.n * HC + (m + 1))
                        nc.scalar.activation(M["hr"][:, m % 4, :], bank(2 + m % 4), ACT.Relu,
                                             bias=b1_e[:, (u.c // 2) % 2, m:m + 1]).then_inc(m_hs, 1)
                        if m == 0:
                            done(act, m_yp, u.back(1))
                        nc.scalar.activation(M["h"][:, 0, m, :], bank(2 + m % 4), ACT.Relu,
                                             bias=b1_e[:, (u.c // 2) % 2, m:m + 1]).then_inc(m_hh, 1)
                u0 = t.at(0, TILES)
                if u0:
                    done(act, m_T, u0)
                    done(act, m_hp, u0.back(2), HC)
                    for c in range(NC_):
                        nc.scalar.activation(M["xF"][:, u0.p, 0, c, :], bank(c), ACT.Copy).then_inc(m_xh, 1)
            pipelined(act, TILES, 1, step, unroll=4, peel=4)

        def m_vector(dve):
            def split_piece(v, which, k):
                buf, n = (v.c // 2) % 2, v.div(2) * (2 * PIECES) + (which * PIECES + k)
                at = slice(k * PW, (k + 1) * PW)
                low = (M["w1_low"], M["w2_low"])[which][:, buf, at]
                if not (v.fixed and n == 0):
                    dve.wait_ge(m_ws, n)
                nc.vector.tensor_copy(M["piece"], M["w"][:, buf, which, at]).then_inc(m_wa, 1)
                dve.wait_ge(m_wa, n + 1)
                low_part(low, M["w"][:, buf, which, at], M["piece"]).then_inc(m_wb, 1)
                dve.wait_ge(m_wb, n + 1)
                nc.vector.tensor_copy(M["w_high"][:, buf, which, at], M["piece"].bitcast(F32)).then_inc(m_ws, 1)

            def step(t):
                u = t.at(1, TILES)
                if u:
                    v = u.back(-2)
                    more = not (v.fixed and v.n >= TILES)
                    if u.c % 2 == 0:
                        done(dve, m_hs, u.back(3), HC)
                        nc.vector.tensor_scalar(b1_e[:, (u.c // 2) % 2, :],
                                                vec[:, bass.ds(u.div(2) * HC + V_B1, HC)], 0.0, None,
                                                ALU.add).then_inc(m_b1, 1)
                    for m in range(HC):
                        if m == 0:
                            done(dve, m_yp, u.back(1))
                        dve.wait_ge(m_hh, u.n * HC + (m + 1))
                        low_part(M["h"][:, 1, m, :], M["hr"][:, m % 4, :], M["h"][:, 0, m, :]).then_inc(m_hl, 1)
                        if more and m % 2 == 1:
                            if m == 1:
                                dve.wait_ge(m_w[(v.c // 2) % 2], (v.div(4) + 1) * 32)
                            split_piece(v, u.c % 2, m // 2)
                u0 = t.at(0, TILES)
                if u0:
                    done(dve, m_hp, u0.back(2), HC)
                    for c in range(NC_):
                        dve.wait_ge(m_xh, u0.n * NC_ + (c + 1))
                        low_part(M["xF"][:, u0.p, 1, c, :], bank(c), M["xF"][:, u0.p, 0, c, :]).then_inc(m_xF, 1)
                if u:
                    done(dve, m_yp, u)
                    landed(dve, m_st, u.back(2))
                    for k in range(2):
                        nc.vector.tensor_tensor(M["y"][:, u.p, 2 * k:2 * k + 2, :], seqs(bank(6 + k)),
                                                b2_b[:, bass.ds(u.div(2), 1), :].broadcast_to([P, 2, D]),
                                                ALU.add).then_inc(m_y, 1)
            dve.wait_ge(m_w[0], 32)
            for which in range(2):
                for k in range(PIECES):
                    split_piece(Unit(0, 0), which, k)
            pipelined(dve, TILES, 1, step, unroll=4, peel=4)

        add("sync", m_sync)
        add("tensor", m_tensor)
        add("scalar", m_scalar)
        add("vector", m_vector)
        def m_end(sp):
            for k in range(2):
                sp.wait_ge(m_st[k], 16 * (TILES // 2))

        add("sync", m_end)
        run_layer()

        arena_y.reset()
        C = {}
        for n in ("x2", "v", "x4"):
            C[n] = arena_y.take([P, 2, UB, D])
        C["x3"] = arena_y.take([P, 4, UB, D])
        C["y"] = arena_y.take([P, 2, TOP0, UB, D])
        C["x3F"] = arena_y.take([P, NC_, T])
        for n in ("q", "k"):
            C[n] = arena_y.take([P, H1, T])
        C["t2q"] = arena_y.take([P, H1, T])
        C["t2k"] = C["t2q"]
        C["e"] = arena_y.take([P, 2, UB * H1, S])
        C["pT"] = arena_y.take([P, UB * H1, S])
        C["oF"] = arena_y.take([P, H1, T])
        C["r"] = arena_y.take([P, UB, D])
        C["r4"] = arena_y.take([P, UB, D])
        C["mx"] = arena_y.take([P, UB * H1])
        C["sum"] = arena_y.take([P, UB * H1])
        C["rec"] = arena_y.take([P, UB * H1])
        c_idx_t = sb("c_idx_t", [P, 2, TOP0, UB], I32)
        C_st3, C_st4 = sb("C_st3", [P, UB, 10]), sb("C_st4", [P, UB, 10])
        c_in, c_y, c_st = sem2("c_in"), sem2("c_y"), sem2("c_st")
        c_idx, c_mix, c_x3T, c_q, c_k, c_v, c_S, c_pT, c_o, c_wo = (
            sem("c_" + n) for n in ("idx", "mix", "x3T", "q", "k", "v", "S", "pT", "o", "wo"))
        c_x3F, c_q2, c_k2, c_vs, c_ex, c_pTs, c_os = (
            sem("c_" + n) for n in ("x3F", "q2", "k2", "vs", "ex", "pTs", "os"))
        c_qt, c_qr, c_kt, c_kr, c_mx, c_sub, c_sum, c_p, c_r4 = (
            sem("c_" + n) for n in ("qt", "qr", "kt", "kr", "mx", "sub", "sum", "p", "r4"))
        ln3 = [sem("ln3_" + n) for n in ("st", "ag", "rs", "out")]
        ln4 = [sem("ln4_" + n) for n in ("st", "ag", "rs", "out")]
        c_x3, c_x4 = ln3[3], ln4[3]
        C_LAG = 4

        def c_sync(sp):

            def step(t):
                u = t.at(0, UNITS)
                if u:
                    done(sp, c_mix, u.back(2), 2)
                    sp.dma_start(C["x2"][:, u.p], x2_u[u.n]).then_inc(c_in[u.p], 16)
                u = t.at(4, UNITS)
                if u:
                    done(sp, c_x4, u)
                    sp.dma_start(x4_u[u.n], C["x4"][:, u.p]).then_inc(c_st[u.p], 16)
            pipelined(sp, UNITS, C_LAG, step, unroll=4)

        def c_gpsimd(pool):

            def step(t):
                u = t.at(0, UNITS)
                if u:
                    landed(pool, c_y, u.back(2), 4)
                    nc.gpsimd.tensor_copy(c_idx_t[:, u.p], slot_g[:, :, bass.ds(u.n * UB, UB)]).then_inc(c_idx, 1)
                    done(pool, c_idx, u)
                    carry(pool, 2)
                    done(pool, c_mix, u.back(2), 2)
                    carry(pool, 3)
                    for k in range(TOP0):
                        for b in range(UB):
                            nc.gpsimd.indirect_dma_start(
                                out=C["y"][:, u.p, k, b, :], out_offset=None, in_=y_d,
                                in_offset=bass.IndirectOffsetOnAxis(ap=c_idx_t[:, u.p, k, b:b + 1], axis=0),
                                ).then_inc(c_y[u.p], 16)
                u0, u3 = t.at(1, UNITS), t.at(4, UNITS)
                if u0:
                    rstd(pool, u0, C_st3, ln3)
                if u3:
                    rstd(pool, u3, C_st4, ln4)
            pipelined(pool, UNITS, C_LAG, step, unroll=4)

        def heads(ap):
            return ap.rearrange("p (n s) -> p n s", s=S)

        def c_tensor(pe):

            def project(u, k, name, s_out, read):
                for r in read:
                    done(pe, r, u.back(1))
                for h in range(H1):
                    for c in range(NC_):
                        ins = nc.tensor.matmul(bank(k)[:, h * T:(h + 1) * T], w[name][:, c, h * P:(h + 1) * P],
                                               C["x3F"][:, c, :], start=(c == 0), stop=(c == NC_ - 1))
                ins.then_inc(s_out, 1)

            def step(t):
                t = t.back(1)
                u0, u1, u2 = (t.at(k, UNITS) for k in range(3))
                if u0:
                    done(pe, c_x3, u0)
                    done(pe, c_x3F, u0.back(1))
                    to_feature(bank(0), C["x3"][:, u0.c % 4]).then_inc(c_x3T, 1)
                    done(pe, c_x3F, u0)
                    project(u0, 1, "L1_attn_wq", c_q, (c_qt, c_q2))
                if u1:
                    done(pe, c_qr, u1)
                    done(pe, c_kr, u1)
                    done(pe, c_q2, u1)
                    done(pe, c_k2, u1)
                    done(pe, c_sub, u1.back(1))
                    nc.tensor.matmul(bank(4), ident_bf[:, :],
                                     causal_bf[:, None, :].broadcast_to([P, UB * H1, S]), start=True, stop=False,
                                     skip_group_check=True)
                    for b in range(UB):
                        for h in range(H1):
                            n = b * H1 + h
                            ins = nc.tensor.matmul(bank(4)[:, n * S:(n + 1) * S], C["q"][:, h, b * S:(b + 1) * S],
                                                   C["k"][:, h, b * S:(b + 1) * S], start=False,
                                                   stop=(n == UB * H1 - 1), skip_group_check=True)
                    ins.then_inc(c_S, 1)
                if u0:
                    project(u0, 2, "L1_attn_wk", c_k, (c_kt, c_k2))
                if u2:
                    done(pe, c_p, u2)
                    done(pe, c_pTs, u2.back(1))
                    for n in range(UB * H1):
                        ins = nc.tensor.transpose(bank(5)[:, n * S:(n + 1) * S], C["e"][:, u2.p, n, :], ident)
                    ins.then_inc(c_pT, 1)
                if u0:
                    done(pe, c_vs, u0.back(1))
                    for b in range(UB):
                        for c in range(NC_):
                            ins = nc.tensor.matmul(bank(3)[:, b * D:(b + 1) * D], C["x3F"][:, c, b * S:(b + 1) * S],
                                                   w["L1_attn_wv"][:, c, :], start=(c == 0), stop=(c == NC_ - 1))
                    ins.then_inc(c_v, 1)
                if u2:
                    done(pe, c_pTs, u2)
                    done(pe, c_os, u2.back(1))
                    for b in range(UB):
                        for h in range(H1):
                            ins = nc.tensor.matmul(bank(6)[:, h * T + b * S:h * T + (b + 1) * S],
                                                   C["v"][:, u2.p, b, h * P:(h + 1) * P],
                                                   C["pT"][:, b * H1 + h, :], start=True, stop=True)
                    ins.then_inc(c_o, 1)
                    done(pe, c_os, u2)
                    done(pe, c_r4, u2.back(1))
                    for b in range(UB):
                        for h in range(H1):
                            ins = nc.tensor.matmul(bank(7)[:, b * D:(b + 1) * D], C["oF"][:, h, b * S:(b + 1) * S],
                                                   w["L1_attn_wo"][:, h, :], start=(h == 0), stop=(h == H1 - 1))
                    ins.then_inc(c_wo, 1)
            pipelined(pe, UNITS, C_LAG, step, unroll=4)

        def c_scalar(act):
            def step(t):
                t = t.back(1)
                u0, u1, u2 = (t.at(k, UNITS) for k in range(3))
                if u0:
                    done(act, c_x3T, u0)
                    done(act, c_v, u0.back(1))
                    nc.scalar.activation(C["x3F"], chunks(bank(0)), ACT.Copy).then_inc(c_x3F, 1)
                if u1:
                    done(act, c_qt, u1)
                    done(act, c_S, u1.back(1))
                    nc.scalar.activation(C["q"][64:P], bank(1)[64:P, :].rearrange("p (h t) -> p h t", h=H1),
                                         ACT.Copy).then_inc(c_q2, 1)
                    done(act, c_kt, u1)
                    nc.scalar.activation(C["k"][64:P], bank(2)[64:P, :].rearrange("p (h t) -> p h t", h=H1),
                                         ACT.Copy).then_inc(c_k2, 1)
                if u2:
                    done(act, c_pT, u2)
                    done(act, c_o, u2.back(1))
                    nc.scalar.activation(C["pT"], heads(bank(5)), ACT.Copy).then_inc(c_pTs, 1)
                if u0:
                    done(act, c_v, u0)
                    done(act, c_o, u0.back(2))
                    nc.scalar.activation(C["v"][:, u0.p], seqs(bank(3)), ACT.Copy).then_inc(c_vs, 1)
                if u2:
                    done(act, c_o, u2)
                    done(act, c_wo, u2.back(1))
                    nc.scalar.activation(C["oF"], chunks(bank(6)), ACT.Copy).then_inc(c_os, 1)
                if u1:
                    done(act, c_sub, u1)
                    nc.scalar.activation(C["e"][:, u1.p], C["e"][:, u1.p], ACT.Exp, scale=1.0 / P).then_inc(c_ex, 1)
            pipelined(act, UNITS, C_LAG, step, unroll=4)

        def c_vector(dve):
            def rope_products(src, dst, t2, s_t):
                s3 = heads(src)
                d3, t3 = heads(dst.rearrange("p h t -> p (h t)")), heads(t2.rearrange("p h t -> p (h t)"))

                def tb(name, lo, hi):
                    return table(name)[lo:hi, None, :].broadcast_to([hi - lo, UB * H1, S])
                nc.vector.tensor_tensor(d3[0:64], s3[0:64], tb("rope_cos", 0, 64), ALU.mult)
                nc.vector.tensor_tensor(t3[0:32], s3[32:64], tb("rope_sin", 32, 64), ALU.mult)
                nc.vector.tensor_tensor(t3[32:64], s3[0:32], tb("rope_sin", 0, 32), ALU.mult).then_inc(s_t, 1)

            def rope_sum(dst, t2, s_r):
                nc.vector.tensor_tensor(dst[0:64], dst[0:64], t2[0:64], ALU.add).then_inc(s_r, 1)

            def mix(u, k):
                for b in range(UB):
                    ins = nc.vector.scalar_tensor_tensor(
                        C["r"][:, b, :], C["y"][:, u.p, k, b, :], gates[:, k, bass.ds(u.n * UB + b, 1)],
                        C["x2"][:, u.p, b, :] if k == 0 else C["r"][:, b, :], ALU.mult, ALU.add)
                ins.then_inc(c_mix, 1)

            def step(t):
                t = t.back(1)
                u0, u1, u2, u3 = (t.at(k, UNITS) for k in range(4))
                e = C["e"][:, u2.p] if u2 else None
                if u0:
                    landed(dve, c_in, u0)
                    landed(dve, c_y, u0, 4)
                    done(dve, c_x3, u0.back(1))
                    mix(u0, 0)
                if u0:
                    dve.wait_ge(c_mix, u0.n * 2 + 1)
                    mix(u0, 1)
                    dve.wait_ge(c_mix, u0.n * 2 + 2)
                    ln_bn(dve, u0, C["r"], C_st3, ln3)
                if u0:
                    ln_moments(dve, u0, C_st3, ln3, cell=1)
                if u0:
                    ln_eps(dve, u0, C_st3, ln3)
                if u1:
                    done(dve, c_q, u1)
                    done(dve, c_S, u1.back(1))
                    done(dve, c_kr, u1.back(1))
                    rope_products(bank(1), C["q"], C["t2q"], c_qt)
                if u0:
                    ln_apply(dve, u0, C["r"], C["x3"][:, u0.c % 4], C_st3, ln3)
                if u2:
                    done(dve, c_ex, u2)
                    nc.vector.tensor_reduce(C["sum"], e, AX, ALU.add).then_inc(c_sum, 1)
                if u2:
                    dve.wait_ge(c_sum, u2.n * 2 + 1)
                    nc.vector.reciprocal(C["rec"], C["sum"]).then_inc(c_sum, 1)
                if u1:
                    done(dve, c_qt, u1)
                    rope_sum(C["q"], C["t2q"], c_qr)
                if u2:
                    dve.wait_ge(c_sum, u2.n * 2 + 2)
                    nc.vector.tensor_tensor(e, e, C["rec"][:, :, None].broadcast_to([P, UB * H1, S]),
                                            ALU.mult).then_inc(c_p, 1)
                if u1:
                    done(dve, c_k, u1)
                    done(dve, c_qr, u1)
                    rope_products(bank(2), C["k"], C["t2k"], c_kt)
                if u3:
                    done(dve, c_wo, u3)
                    done(dve, c_x4, u3.back(1))
                    nc.vector.tensor_tensor(C["r4"], seqs(bank(7)), C["x3"][:, u3.c % 4], ALU.add).then_inc(c_r4, 1)
                if u1:
                    done(dve, c_kt, u1)
                    rope_sum(C["k"], C["t2k"], c_kr)
                if u3:
                    done(dve, c_r4, u3)
                    ln_bn(dve, u3, C["r4"], C_st4, ln4)
                if u3:
                    ln_moments(dve, u3, C_st4, ln4)
                if u3:
                    ln_eps(dve, u3, C_st4, ln4)
                if u1:
                    done(dve, c_S, u1)
                    done(dve, c_pT, u1.back(2))
                    nc.vector.tensor_reduce(C["mx"], heads(bank(4)), AX, ALU.max).then_inc(c_mx, 1)
                if u3:
                    landed(dve, c_st, u3.back(2))
                    ln_apply(dve, u3, C["r4"], C["x4"][:, u3.p], C_st4, ln4)
                if u1:
                    done(dve, c_mx, u1)
                    nc.vector.tensor_tensor(C["e"][:, u1.p], heads(bank(4)),
                                            C["mx"][:, :, None].broadcast_to([P, UB * H1, S]),
                                            ALU.subtract).then_inc(c_sub, 1)
            pipelined(dve, UNITS, C_LAG, step, unroll=4)

        add("sync", c_sync)
        add("gpsimd", c_gpsimd)
        add("tensor", c_tensor)
        add("scalar", c_scalar)
        add("vector", c_vector)
        arena_x.reset()
        VW = 2 * HD
        X = {}
        X["x4"] = arena_x.take([P, 2, UB, D])
        X["cx"] = arena_x.take([P, 2, UB, D])
        X["xb"] = arena_x.take([P, 4, UB, D])
        X["x4F"] = arena_x.take([P, NC_, T])
        X["cF"] = arena_x.take([P, NC_, T])
        X["q"] = arena_x.take([P, 2, NC_, T])
        X["k"] = arena_x.take([P, 2, 2, NC_ * T])
        X["v"] = arena_x.take([P, 2, UB, NH, VW])
        X["e"] = arena_x.take([P, UB, NH, S])
        X["eT"] = arena_x.take([P, 2, NH * S])
        X["aF"] = arena_x.take([P, NC_, T])
        X["x5"] = arena_x.take([P, 2, UB, D])
        X["r"] = arena_x.take([P, UB, D])
        X["mx"] = arena_x.take([P, 2, NH])
        X["rec"] = arena_x.take([P, NC_, S])
        X["half"] = arena_x.take([P, 2, VW])
        ARENA_X_E = arena_x.at
        X_st = sb("X_st", [P, UB, 10])
        x_in, x_st = sem2("x_in"), sem2("x_st")
        x_xT, x_cT, x_q, x_k, x_v, x_S, x_eT, x_pv, x_wo = (
            sem("x_" + n) for n in ("xT", "cT", "q", "k", "v", "S", "eT", "pv", "wo"))
        x_xF, x_cF, x_qs, x_ks, x_ex, x_eTs = (
            sem("x_" + n) for n in ("xF", "cF", "qs", "ks", "ex", "eTs"))
        x_mask = sem("x_mask")
        x_vs, x_mx, x_sub, x_rec, x_at, x_r, x_xb, x_one = (
            sem("x_" + n) for n in ("vs", "mx", "sub", "rec", "at", "r", "xb", "one"))
        ln5 = [sem("ln5_" + n) for n in ("st", "ag", "rs", "out")]
        x_x5 = ln5[3]
        E_LAG = 3

        def seq_done(eng, s, u, b, per=1, k=None):
            if u.fixed and u.n < 0:
                return
            if b < 0:
                u, b = u.back(1), b + 2
                if u.fixed and u.n < 0:
                    return
            eng.wait_ge(s, u.n * (2 * per) + (b * per + (per if k is None else k)))

        def e_sync(sp):
            def step(t):
                u = t.at(0, UNITS)
                if u:
                    done(sp, x_xb, u.back(2))
                    done(sp, x_xT, u.back(2))
                    landed(sp, c_st, u)
                    sp.dma_start(X["x4"][:, u.p], x4_u[u.n]).then_inc(x_in[u.p], 16)
                    done(sp, x_cT, u.back(2))
                    sp.dma_start(X["cx"][:, u.p], ctx_u[u.n]).then_inc(x_in[u.p], 16)
                if t.fixed and t.n == 1:
                    for k in range(2):
                        sp.wait_ge(c_st[k], 16 * per_parity)
                    d_weights(sp)
                u = t.at(3, UNITS)
                if u:
                    done(sp, x_x5, u)
                    sp.dma_start(x5_u[u.n], X["x5"][:, u.p]).then_inc(x_st[u.p], 16)
            pipelined(sp, UNITS, E_LAG, step, unroll=4)

        def e_gpsimd(pool):

            def step(t):
                u = t.at(2, UNITS)
                if u:
                    rstd(pool, u, X_st, ln5)
                u = t.at(0, UNITS)
                if u:
                    landed(pool, x_in, u, 2)
                    done(pool, x_r, u.back(4))
                    for b in range(UB):
                        ins = nc.gpsimd.tensor_tensor(X["xb"][:, u.c % 4, b, :], X["x4"][:, u.p, b, :], bo_b[:, :],
                                                      ALU.add)
                    ins.then_inc(x_xb, 1)
            pipelined(pool, UNITS, E_LAG, step, unroll=4)

        def e_tensor(pe):
            for part in (c_os, c_sub, c_pTs):
                pe.wait_ge(part, UNITS)

            def scores(u, b):
                seq_done(pe, x_sub, u, b - 1)
                for quad in range(4):
                    ins = nc.tensor.matmul(bank(quad), ones_row[:, :],
                                           mask_row[:, None, bass.ds(u.n * T + b * S, S)].broadcast_to([1, 4, S]),
                                           start=True, stop=False, skip_group_check=True)
                ins.then_inc(x_mask, 1)
                seq_done(pe, x_mask, u, b)
                for c in range(NC_):
                    for par in range(2):
                        for quad in range(4):
                            rows = slice(32 * quad, 32 * quad + 32)
                            at = (2 * c + par) * S
                            ins = nc.tensor.matmul(bank(quad)[:, at:at + S],
                                                   X["q"][rows, u.p, c, b * S:(b + 1) * S],
                                                   X["k"][rows, u.p, par, c * T + b * S:c * T + (b + 1) * S],
                                                   start=False, stop=(c == 1 and par == 1), skip_group_check=True)
                ins.then_inc(x_S, 1)

            def attend(u, b):
                seq_done(pe, x_ex, u, b)
                for g in range(4):
                    seq_done(pe, x_eTs, u, b, 4, g - 1) if g >= 2 else seq_done(pe, x_eTs, u, b - 1, 4, g + 3)
                    for k in range(4):
                        ins = nc.tensor.transpose(bank(4 + g % 2)[:, k * S:(k + 1) * S], X["e"][:, b, 4 * g + k, :],
                                                  ident)
                    ins.then_inc(x_eT, 1)

            def values(u, b):
                seq_done(pe, x_eTs, u, b, 4)
                for c in range(NC_):
                    for par in range(2):
                        for kind in range(2):
                            for quad in range(4):
                                at = (4 * quad + 2 * c + par) * S
                                left = (X["v"][:, u.p, b, 8 * c + 2 * quad + par, :], X["half"][:, par, :])[kind]
                                ins = nc.tensor.matmul(
                                    bank(7)[32 * quad:32 * quad + 32, (kind * NC_ + c) * S:(kind * NC_ + c + 1) * S],
                                    left, X["eT"][:, b, at:at + S], start=(c == par == kind == 0), stop=(c == par == kind == 1),
                                    skip_group_check=True)
                ins.then_inc(x_pv, 1)

            def project(dst, name, src):
                for m in range(NC_):
                    for c in range(NC_):
                        ins = nc.tensor.matmul(dst[:, m * T:(m + 1) * T], w[name][:, c, m * P:(m + 1) * P],
                                               src[:, c, :], start=(c == 0), stop=(c == NC_ - 1))
                return ins

            def project_rows(dst, name, src):
                for b in range(UB):
                    for c in range(NC_):
                        ins = nc.tensor.matmul(dst[:, b * D:(b + 1) * D], src[:, c, b * S:(b + 1) * S],
                                               w[name][:, c, :], start=(c == 0), stop=(c == NC_ - 1))
                return ins

            def step(t):
                u0, u1, u2 = t.at(0, UNITS), t.at(1, UNITS), t.at(2, UNITS)
                if t.fixed and t.n == 1:
                    for part in (c_x3F, c_qr, c_kr, c_q2, c_k2, c_vs, c_r4):
                        pe.wait_ge(part, UNITS)
                if u1:
                    done(pe, x_qs, u1)
                    done(pe, x_ks, u1, 4)
                    scores(u1, 0)
                if u0:
                    landed(pe, x_in, u0, 2)
                    done(pe, x_vs, u0.back(1))
                    done(pe, x_r, u0.back(3))
                    to_feature(bank(6), X["x4"][:, u0.p]).then_inc(x_xT, 1)
                if u2:
                    attend(u2, 1)
                if u0:
                    done(pe, x_xF, u0)
                    project(bank(6), "L1_xattn_Wq", X["x4F"]).then_inc(x_q, 1)
                    if u2:
                        seq_done(pe, x_eTs, u2, 1, 4, 3)
                    to_feature(bank(4), X["cx"][:, u0.p]).then_inc(x_cT, 1)
                if u2:
                    seq_done(pe, x_at, u2, 0)
                    values(u2, 1)
                if u0:
                    done(pe, x_cF, u0)
                    project(bank(5), "L1_xattn_Wk", X["cF"]).then_inc(x_k, 1)
                    done(pe, x_qs, u0)
                    project_rows(bank(6), "L1_xattn_Wv", X["cF"]).then_inc(x_v, 1)
                if u1:
                    scores(u1, 1)
                    if u0:
                        done(pe, x_ks, u0, 4)
                    attend(u1, 0)
                if u2:
                    seq_done(pe, x_at, u2, 1)
                    if u0:
                        done(pe, x_vs, u0)
                    else:
                        done(pe, x_r, u2.back(1))
                    project_rows(bank(6), "L1_xattn_Wo", X["aF"]).then_inc(x_wo, 1)
                if u1:
                    done(pe, x_vs, u1)
                    if u2:
                        seq_done(pe, x_at, u2, 1)
                    values(u1, 0)
            pipelined(pe, UNITS, E_LAG, step, unroll=4)

        def e_scalar(act):

            def turned(u, b):
                for g in range(4):
                    seq_done(act, x_eT, u, b, 4, g + 1)
                    if g == 0:
                        seq_done(act, x_pv, u.back(1), b)
                    nc.scalar.activation(X["eT"][:, b, g * 512:(g + 1) * 512], bank(4 + g % 2), ACT.Copy)\
                        .then_inc(x_eTs, 1)

            def step(t):
                u0, u1, u2 = t.at(0, UNITS), t.at(1, UNITS), t.at(2, UNITS)
                if u0:
                    done(act, x_xT, u0)
                    done(act, x_q, u0.back(1))
                    nc.scalar.activation(X["x4F"], chunks(bank(6)), ACT.Copy).then_inc(x_xF, 1)
                if u2:
                    turned(u2, 1)
                if u0:
                    done(act, x_q, u0)
                    seq_done(act, x_S, u0.back(2), 1)
                    for c in range(NC_):
                        ins = nc.scalar.activation(X["q"][:, u0.p, c, :], bank(6)[:, c * T:(c + 1) * T], ACT.Identity,
                                                   bias=vec[:, V_BQ + c:V_BQ + c + 1])
                    ins.then_inc(x_qs, 1)
                    done(act, x_cT, u0)
                    done(act, x_v, u0.back(1))
                    nc.scalar.activation(X["cF"], chunks(bank(4)), ACT.Copy).then_inc(x_cF, 1)
                if u1:
                    seq_done(act, x_sub, u1, 0)
                    nc.scalar.activation(X["e"][:, 0], X["e"][:, 0], ACT.Exp, scale=HD ** -0.5).then_inc(x_ex, 1)
                if u0:
                    done(act, x_k, u0)
                    for par, name in enumerate(("even_heads", "odd_heads")):
                        for c in range(NC_):
                            nc.scalar.activation(X["k"][:, u0.p, par, c * T:(c + 1) * T], bank(5)[:, c * T:(c + 1) * T],
                                                 ACT.Identity, bias=kb_par[:, par, c:c + 1],
                                                 scale=table(name)).then_inc(x_ks, 1)
                if u1:
                    turned(u1, 0)
                    seq_done(act, x_sub, u1, 1)
                    nc.scalar.activation(X["e"][:, 1], X["e"][:, 1], ACT.Exp, scale=HD ** -0.5).then_inc(x_ex, 1)
            pipelined(act, UNITS, E_LAG, step, unroll=4)

        def e_vector(dve):
            nc.vector.memset(X["v"].rearrange("p a b h o -> p (a b h o)"), 0.0).then_inc(x_one, 1)
            nc.vector.memset(X["half"].rearrange("p a o -> p (a o)"), 0.0).then_inc(x_one, 1)
            dve.wait_ge(x_one, 2)
            for par in range(2):
                nc.vector.memset(X["half"][:, par, par * HD:(par + 1) * HD], 1.0).then_inc(x_one, 1)

            def less_max(u, b):
                s3 = psum[:, 0:4, :].rearrange("p q (k s) -> p (q k) s", s=S)
                seq_done(dve, x_S, u, b)
                seq_done(dve, x_eT, u.back(1), b, 4)
                nc.vector.tensor_reduce(X["mx"][:, b, :], s3, AX, ALU.max).then_inc(x_mx, 1)
                seq_done(dve, x_mx, u, b)
                nc.vector.tensor_tensor(X["e"][:, b], s3, X["mx"][:, b, :, None].broadcast_to([P, NH, S]),
                                        ALU.subtract).then_inc(x_sub, 1)

            def normalise(u, b):
                seq_done(dve, x_pv, u, b)
                seq_done(dve, x_at, u, b - 1)
                nc.vector.reciprocal(X["rec"], bank(7)[:, D:2 * D].rearrange("p (c s) -> p c s", c=NC_)).then_inc(x_rec, 1)
                seq_done(dve, x_rec, u, b)
                nc.vector.tensor_tensor(X["aF"][:, :, b * S:(b + 1) * S],
                                        bank(7)[:, 0:D].rearrange("p (c s) -> p c s", c=NC_), X["rec"],
                                        ALU.mult).then_inc(x_at, 1)

            def step(t):
                u0, u1, u2 = t.at(0, UNITS), t.at(1, UNITS), t.at(2, UNITS)
                if u1:
                    less_max(u1, 0)
                if u2:
                    normalise(u2, 1)
                if u0:
                    done(dve, x_v, u0)
                    seq_done(dve, x_pv, u0.back(2), 1)
                    for par in range(2):
                        ins = nc.vector.tensor_tensor(
                            X["v"][:, u0.p].rearrange("p b (i k) o -> p (b i) k o", k=2)[:, :, par,
                                                                                       par * HD:(par + 1) * HD],
                            bank(6).rearrange("p (i k d) -> p i k d", k=2, d=HD)[:, :, par, :],
                            bv2_b[:, :].rearrange("p (i k d) -> p i k d", k=2, d=HD)[:, :, par, :], ALU.add)
                    ins.then_inc(x_vs, 1)
                if u1:
                    less_max(u1, 1)
                if u2:
                    done(dve, x_wo, u2)
                    done(dve, x_xb, u2)
                    done(dve, x_x5, u2.back(1))
                    nc.vector.tensor_tensor(X["r"], seqs(bank(6)), X["xb"][:, u2.c % 4], ALU.add).then_inc(x_r, 1)
                    done(dve, x_r, u2)
                    ln_stats(dve, u2, X["r"], X_st, ln5)
                if u1:
                    normalise(u1, 0)
                if t.fixed and 4 <= t.n < 8:
                    if t.n == 4:
                        dve.wait_ge(d_w, 32)
                    for k in range(2):
                        d_split(dve, 0, (t.n - 4) * 2 + k)
                if u2:
                    landed(dve, x_st, u2.back(2))
                    ln_apply(dve, u2, X["r"], X["x5"][:, u2.p], X_st, ln5)
            pipelined(dve, UNITS, E_LAG, step, unroll=4)

        add("sync", e_sync)
        add("gpsimd", e_gpsimd)
        add("tensor", e_tensor)
        add("scalar", e_scalar)
        add("vector", e_vector)

        HIDD = NE1 * PD
        HJ = HIDD // P
        N_TOP, TOP_LESS = 16, 2
        SL = HJ // 2
        arena_x.reset()
        arena_y.reset()
        K = {}
        VN = NC_ * HIDD
        K["v"] = arena_y.take([P, 2, VN])
        K["v_high"] = arena_y.view("d_v_high", 0, [P, 2, VN])
        K["vd_low"] = arena_y.take([P, VN], "d_vd_low")
        K["piece"] = arena_y.take([P, VN // SL], "d_piece")
        K["vu_low"] = arena_x.take([P, VN], "d_vu_low")
        K["x5"] = arena_x.take([P, 4, UB, D])
        K["x5F"] = arena_x.take([P, NC_, T])
        K["x5P"] = arena_x.take([P, 2, 2, NC_, T], "d_x5_parts")
        K["r"] = arena_x.take([P, UB, D])
        K["th"] = arena_x.take([P, 2, 2, T])
        K["t"] = arena_x.take([P, 2, 2, T])
        K["g"] = arena_x.take([P, 2, 2 * T])
        K["gP"] = arena_x.take([P, 2, 2, 2 * T], "d_g_parts")
        K["hF"] = arena_x.take([P, T])[0:PD, :]
        for n in ("sim", "gt", "eq", "cum", "ex"):
            K[n] = arena_x.take([P, UB, NE1])
        K["mx8"] = arena_x.take([P, UB, 8])
        K["ngt"] = arena_x.take([P, UB])
        K["sum"] = arena_x.take([P, UB])
        expand = arena_x.take([P, HIDD], "d_expand")
        parts = arena_x.take([P, UB, 2, NE1], "d_weight_parts")
        wT = arena_x.take([P, T], "d_weights_T")
        K_st = arena_x.take([P, UB, 10])
        keep_ex = arena_x.take([P, UB, NE1])
        d_w = sem("d_w")
        d_in, d_st = sem2("d_in"), sem2("d_st")
        d_xT, d_h, d_sim, d_z, d_wb, d_up, d_wTp = (sem("d_" + n) for n in ("xT", "h", "sim", "z", "wb", "up", "wTp"))
        d_xF, d_hF, d_sims, d_th, d_ex, d_wT = (sem("d_" + n) for n in ("xF", "hF", "sims", "th", "ex", "wT"))
        d_one, d_top, d_t, d_g, d_r = (sem("d_" + n) for n in ("one", "top", "t", "g", "r"))
        d_xh, d_xl, d_gh, d_gl = (sem("d_" + n) for n in ("xh", "xl", "gh", "gl"))
        d_va, d_vb, d_vs = (sem("d_" + n) for n in ("va", "vb", "vs"))
        ln6 = [sem("ln6_" + n) for n in ("st", "ag", "rs", "out")]
        d_out = ln6[3]
        D_LAG = 2

        def slice_done(eng, s, u, k):
            seq_done(eng, s, u, k // 4, 4, k % 4 + 1)

        def d_weights(eng):
            eng.dma_start(K["v"][:, 0].rearrange("p (c h) -> p c h", c=NC_),
                          a["down"].rearrange("(c p) h -> p c h", p=P)).then_inc(d_w, 16)
            eng.dma_start(K["v"][:, 1].rearrange("p (j d) -> p j d", j=HJ),
                          a["up"].rearrange("(j p) d -> p j d", p=P)).then_inc(d_w, 16)

        def d_split(dve, which, k):
            n = which * SL + k
            at = slice(k * VN // SL, (k + 1) * VN // SL)
            if n:
                dve.wait_ge(d_vs, n)
            nc.vector.tensor_copy(K["piece"], K["v"][:, which, at]).then_inc(d_va, 1)
            dve.wait_ge(d_va, n + 1)
            low_part((K["vd_low"], K["vu_low"])[which][:, at], K["v"][:, which, at], K["piece"]).then_inc(d_vb, 1)
            dve.wait_ge(d_vb, n + 1)
            nc.vector.tensor_copy(K["v_high"][:, which, at], K["piece"].bitcast(F32)).then_inc(d_vs, 1)

        def d_sync(sp):
            def step(t):
                u = t.at(0, UNITS)
                if u:
                    landed(sp, d_st, u.back(4))
                    done(sp, d_xT, u.back(2))
                    landed(sp, x_st, u)
                    sp.dma_start(K["x5"][:, u.c % 4], x5_u[u.n]).then_inc(d_in[u.p], 16)
                u = t.at(2, UNITS)
                if u:
                    done(sp, d_out, u)
                    sp.dma_start(out_u[u.n], K["x5"][:, u.c % 4]).then_inc(d_st[u.p], 16)
            pipelined(sp, UNITS, D_LAG, step, unroll=4)
            for k in range(2):
                sp.wait_ge(d_st[k], 16 * per_parity)

        def d_gpsimd(pool):
            def step(t):
                u1, u2 = t.at(1, UNITS), t.at(2, UNITS)
                for s in range(SL):
                    if u1:
                        slice_done(pool, d_gh, u1, s)
                        slice_done(pool, d_up, u1, s - 2)
                        nc.gpsimd.tensor_tensor(K["gP"][:, s % 2, 1], K["g"][:, s % 2],
                                                K["gP"][:, s % 2, 0].bitcast(F32), ALU.subtract).then_inc(d_gl, 1)
                    if s == 1 and u2:
                        rstd(pool, u2, K_st, ln6)
            pipelined(pool, UNITS, D_LAG, step, unroll=4)

        def d_tensor(pe):
            pe.wait_ge(d_vs, SL)
            pe.wait_ge(d_one, 4)
            down = [x.rearrange("p (c h) -> p c h", c=NC_) for x in (K["v_high"][:, 0], K["vd_low"])]
            up_w = [x.rearrange("p (j d) -> p j d", j=HJ) for x in (K["v_high"][:, 1], K["vu_low"])]
            pe.wait_ge(x_r, UNITS)
            seq_done(pe, x_eTs, Unit(0, UNITS - 1), 1, 4)

            def up(u, s):
                slice_done(pe, d_gl, u, s)
                if u.fixed and u.n == 0:
                    pe.wait_ge(d_vs, SL + s + 1)
                for k in range(2):
                    for b in range(UB):
                        at = k * T + b * S
                        ins = matmul_split(bank(4 + u.p)[:, b * D:(b + 1) * D],
                                           [K["gP"][:, s % 2, part, at:at + S] for part in range(2)],
                                           [x[:, 2 * s + k, :] for x in up_w],
                                           s == 0 and k == 0 and b == 0, s == SL - 1 and k == 1)
                ins.then_inc(d_up, 1)

            def step(t):
                u0, u1, u2 = t.at(0, UNITS), t.at(1, UNITS), t.at(2, UNITS)
                for s in range(SL):
                    if u1:
                        if s == 0:
                            done(pe, d_xl, u1)
                        slice_done(pe, d_t, u1, s - 2)
                        for k in range(2):
                            j = 2 * s + k
                            for c in range(NC_):
                                ins = matmul_split(bank(s % 2)[:, k * T:(k + 1) * T],
                                                   [x[:, c, j * P:(j + 1) * P] for x in down],
                                                   [K["x5P"][:, u1.p, part, c, :] for part in range(2)],
                                                   c == 0, c == NC_ - 1)
                        ins.then_inc(d_z, 1)
                        if s == 0:
                            done(pe, d_wT, u1)
                        slice_done(pe, d_g, u1, s - 2)
                        for k in range(2):
                            j = 2 * s + k
                            ins = nc.tensor.matmul(bank(2 + s % 2)[:, k * T:(k + 1) * T],
                                                   expand[:, j * P:(j + 1) * P], wT, start=True, stop=True)
                        ins.then_inc(d_wb, 1)
                    if s >= 2 and u1:
                        if s == 2:
                            done(pe, d_r, u1.back(2))
                        up(u1, s - 2)
                    if s < 2 and u2:
                        up(u2, SL + s - 2)
                    if not u0:
                        continue
                    if s == 0:
                        landed(pe, d_in, u0)
                        done(pe, d_wT, u0.back(1))
                        to_feature(bank(6), K["x5"][:, u0.c % 4]).then_inc(d_xT, 1)
                    if s == 1:
                        done(pe, d_xF, u0)
                        done(pe, d_sims, u0.back(1))
                        for c in range(NC_):
                            ins = nc.tensor.matmul(bank(7)[0:PD, 0:T], w_hash[:, c, :], K["x5F"][:, c, :],
                                                   start=(c == 0), stop=(c == NC_ - 1))
                        ins.then_inc(d_h, 1)
                    if s == 2:
                        done(pe, d_hF, u0)
                        for b in range(UB):
                            ins = nc.tensor.matmul(bank(7)[:, T + b * NE1:T + (b + 1) * NE1],
                                                   K["hF"][:, b * S:(b + 1) * S], w_keys[:, :], start=True, stop=True)
                        ins.then_inc(d_sim, 1)
                    if s == SL - 1:
                        done(pe, d_top, u0, N_TOP)
                        done(pe, d_xl, u0)
                        for b in range(UB):
                            ins = nc.tensor.transpose(bank(6)[:, b * S:(b + 1) * S],
                                                      parts[:, b].rearrange("p a e -> p (a e)").bitcast(F32), ident)
                        ins.then_inc(d_wTp, 1)
            pipelined(pe, UNITS, D_LAG, step, unroll=4)

        def d_scalar(act):
            def high(u, s):
                slice_done(act, d_g, u, s)
                slice_done(act, d_up, u, s - 2)
                nc.scalar.activation(K["gP"][:, s % 2, 0], K["g"][:, s % 2], ACT.Copy).then_inc(d_gh, 1)

            def step(t):
                u0, u1 = t.at(0, UNITS), t.at(1, UNITS)
                for s in range(SL):
                    if u1:
                        slice_done(act, d_z, u1, s)
                        slice_done(act, d_t, u1, s - 2)
                        nc.scalar.activation(K["th"][:, s % 2], bank(s % 2).rearrange("p (k t) -> p k t", k=2), ACT.Tanh,
                                             scale=0.5).then_inc(d_th, 1)
                        if s >= 1:
                            high(u1, s - 1)
                        if s == SL - 1:
                            high(u1, s)
                    if not u0:
                        continue
                    if s == 0:
                        done(act, d_xT, u0)
                        done(act, d_h, u0.back(1))
                        nc.scalar.activation(K["x5F"], chunks(bank(6)), ACT.Copy).then_inc(d_xF, 1)
                        slice_done(act, d_z, u0.back(2), SL - 1)
                        nc.scalar.activation(K["x5P"][:, u0.p, 0], chunks(bank(6)), ACT.Copy).then_inc(d_xh, 1)
                    if s == 1:
                        done(act, d_h, u0)
                        done(act, d_sim, u0.back(1))
                        nc.scalar.activation(K["hF"], bank(7)[0:PD, 0:T], ACT.Copy).then_inc(d_hF, 1)
                    if s == 2:
                        done(act, d_sim, u0)
                        done(act, d_top, u0.back(1), N_TOP)
                        nc.scalar.activation(K["sim"], bank(7)[:, T:T + UB * NE1].rearrange("p (b e) -> p b e", b=UB),
                                             ACT.Copy).then_inc(d_sims, 1)
                    if s == 4:
                        act.wait_ge(d_top, u0.n * N_TOP + TOP_LESS)
                        nc.scalar.activation(K["ex"], K["ex"], ACT.Exp).then_inc(d_ex, 1)
                    if s == SL - 1:
                        done(act, d_wTp, u0)
                        slice_done(act, d_wb, u1, SL - 1) if u1 else None
                        nc.scalar.activation(wT, bank(6)[:, 0:T], ACT.Copy).then_inc(d_wT, 1)
            pipelined(act, UNITS, D_LAG, step, unroll=4)

        def d_vector(dve):
            dve.wait_ge(x_st[0], 16 * per_parity)
            dve.wait_ge(x_st[1], 16 * per_parity)
            for lo in (0, NE1):
                rows = slice(lo, lo + NE1)
                nc.vector.tensor_scalar(expand[rows, :].rearrange("p (e r) -> p e r", r=PD),
                                        ident[rows, lo:lo + NE1, None].broadcast_to([NE1, NE1, PD]), 1.0, None,
                                        ALU.mult).then_inc(d_one, 1)
            nc.vector.memset(keep_ex[:, :, 1:], 1.0).then_inc(d_one, 1)
            nc.vector.memset(keep_ex[:, :, 0:1], 0.0).then_inc(d_one, 1)
            dve.wait_ge(d_one, 4)

            def choose(u):
                steps = [0]

                def after(ins):
                    ins.then_inc(d_top, 1)
                    steps[0] += 1

                def ready():
                    dve.wait_ge(d_top, u.n * N_TOP + steps[0])

                def per_b(ap, k=0):
                    return ap[:, :, k:k + 1].broadcast_to([P, UB, NE1])

                done(dve, d_sims, u)
                nc.vector.memset(wait_cell[:, 0:1], 0.0)
                for b in range(UB):
                    ins = nc.vector.max(K["mx8"][:, b, :], K["sim"][:, b, :])
                after(ins)
                ready()
                after(nc.vector.tensor_tensor(K["ex"], K["sim"], per_b(K["mx8"]), ALU.subtract))
                after(nc.vector.tensor_tensor(K["gt"], K["sim"], per_b(K["mx8"], TOP1 - 1), ALU.is_gt))
                after(nc.vector.tensor_tensor(K["eq"], K["sim"], per_b(K["mx8"], TOP1 - 1), ALU.is_equal))
                ready()
                after(nc.vector.tensor_reduce(K["ngt"], K["gt"], AX, ALU.add))
                after(nc.vector.tensor_tensor_scan(K["cum"].rearrange("p b e -> p (b e)"), keep_ex.rearrange("p b e -> p (b e)"),
                                                   K["eq"].rearrange("p b e -> p (b e)"), 0.0, ALU.mult, ALU.add))
                ready()
                after(nc.vector.tensor_tensor(K["cum"], K["cum"], K["ngt"][:, :, None].broadcast_to([P, UB, NE1]),
                                              ALU.add))
                ready()
                after(nc.vector.scalar_tensor_tensor(K["eq"], K["cum"], float(TOP1), K["eq"], ALU.is_le, ALU.mult))
                ready()
                after(nc.vector.tensor_tensor(K["gt"], K["gt"], K["eq"], ALU.add))
                ready()
                done(dve, d_ex, u)
                after(nc.vector.tensor_tensor(K["ex"], K["ex"], K["gt"], ALU.mult))
                ready()
                after(nc.vector.tensor_reduce(K["sum"], K["ex"], AX, ALU.add))
                ready()
                after(nc.vector.reciprocal(K["sum"], K["sum"]))
                ready()
                after(nc.vector.tensor_scalar(K["sum"], K["sum"], scale_b[:, 0:1], 0.5, ALU.mult, ALU.mult))
                ready()
                after(nc.vector.tensor_tensor(K["ex"], K["ex"], K["sum"][:, :, None].broadcast_to([P, UB, NE1]),
                                              ALU.mult))
                ready()
                done(dve, d_wTp, u.back(1))
                after(nc.vector.tensor_copy(parts[:, :, 0], K["ex"]))
                ready()
                after(low_part(parts[:, :, 1], K["ex"], parts[:, :, 0]))
                assert steps[0] == N_TOP, steps

            def step(t):
                u0, u1, u2 = t.at(0, UNITS), t.at(1, UNITS), t.at(2, UNITS)
                for s in range(SL):
                    if u1:
                        slice_done(dve, d_th, u1, s)
                        slice_done(dve, d_g, u1, s - 2)
                        z = bank(s % 2).rearrange("p (k t) -> p k t", k=2)
                        nc.vector.scalar_tensor_tensor(K["t"][:, s % 2], K["th"][:, s % 2], 1.0, z, ALU.add,
                                                       ALU.mult).then_inc(d_t, 1)
                        slice_done(dve, d_t, u1, s)
                        slice_done(dve, d_wb, u1, s)
                        slice_done(dve, d_gl, u1, s - 2)
                        nc.vector.tensor_tensor(K["g"][:, s % 2], K["t"][:, s % 2].rearrange("p k t -> p (k t)"),
                                                bank(2 + s % 2), ALU.mult).then_inc(d_g, 1)
                    if s == 0 and u0:
                        done(dve, d_xh, u0)
                        slice_done(dve, d_z, u0.back(2), SL - 1)
                        low_part(K["x5P"][:, u0.p, 1], chunks(bank(6)), K["x5P"][:, u0.p, 0]).then_inc(d_xl, 1)
                    if s == 3 and u0:
                        choose(u0)
                        if t.fixed and t.n == 0:
                            for k in range(SL):
                                d_split(dve, 1, k)
                    if s == 2 and u2:
                        slice_done(dve, d_up, u2, SL - 1)
                        done(dve, d_out, u2.back(1))
                        nc.vector.scalar_tensor_tensor(K["r"], K["x5"][:, u2.c % 4], 2.0, seqs(bank(4 + u2.p)),
                                                       ALU.mult, ALU.add).then_inc(d_r, 1)
                        done(dve, d_r, u2)
                        ln_stats(dve, u2, K["r"], K_st, ln6)
                    if s == 3 and u2:
                        ln_apply(dve, u2, K["r"], K["x5"][:, u2.c % 4], K_st, ln6)
            pipelined(dve, UNITS, D_LAG, step, unroll=4)

        add("sync", d_sync)
        add("gpsimd", d_gpsimd)
        add("tensor", d_tensor)
        add("scalar", d_scalar)
        add("vector", d_vector)
        run_layer()


def kernel(**inputs):
    import concourse.bacc as _bacc
    from concourse.bass_utils import run_bass_kernel_spmd as _run

    nc = _bacc.Bacc("TRN2", target_bir_lowering=False, num_devices=1)
    table, where = constants()
    given = {k: np.asarray(v) for k, v in inputs.items()}
    given["mask"] = given.pop("mask_BxS2_bk0")
    given["hash_t"] = given.pop("L1_ffn_hasher_w").T
    given["keys_t"] = given.pop("L1_ffn_keys").T
    given["down"] = given.pop("L1_ffn_values_down").transpose(1, 0, 2).reshape(D, NE1 * PD)
    given["up"] = given.pop("L1_ffn_values_up").reshape(NE1 * PD, D)
    given["constants"] = table
    arrays, args = {}, {}
    for name, v in given.items():
        v = np.ascontiguousarray(v)
        arrays[f"in_{name}"] = v
        args[name] = nc.dram_tensor(f"in_{name}", v.shape, mybir.dt.from_np(v.dtype), kind="ExternalInput").ap()
    out = nc.dram_tensor("out_0", (B, S, D), F32, kind="ExternalOutput").ap()
    decoder(nc, args, where, out)
    return _run(nc, [arrays], core_ids=[0]).results[0]["out_0"]
```
